# Optimizing a Trainium2 kernel written in Bass

```python
import numpy as np
import jax
import jax.numpy as jnp

def _softmax(x, axis=-1):
    return jax.nn.softmax(x, axis=axis)

def _gelu(x):
    return jax.nn.gelu(x, approximate=True)

def _silu(x):
    return jax.nn.silu(x)

def _sigmoid(x):
    return jax.nn.sigmoid(x)

def _layernorm(x, axis=-1, eps=1e-05):
    m = jnp.mean(x, axis=axis, keepdims=True)
    v = jnp.var(x, axis=axis, keepdims=True)
    return (x - m) / jnp.sqrt(v + eps)

def _scatter_add(tgt, idx, src, axis=0):
    return tgt.at[idx].add(src)

def _segment_sum(src, seg, n):
    return jax.ops.segment_sum(src, seg, n)
kernel_name = 'mk_sandwich_d2_jaxref_r8_494bf6'

def setup_inputs(seed: int=0):
    np.random.seed(seed)
    _w = jnp.asarray

    def _L0_attn_setup():
        import jax, jax.numpy as jnp
        import numpy as np
        B, N, D_MODEL, HEADS, DFF, M = (4, 512, 128, 16, 512, 32)
        DH = D_MODEL // HEADS
        EPS_K = 0.0001
        LN_EPS = 1e-05

        def softmax_kernel(x, proj, is_query):
            norm = x.shape[-1] ** (-0.25)
            ratio = proj.shape[0] ** (-0.5)
            xp = jnp.einsum('bhnd,md->bhnm', x * norm, proj)
            diag = jnp.sum(jnp.square(x), axis=-1, keepdims=True) * 0.5 * (norm * norm)
            if is_query:
                stab = jnp.max(xp, axis=-1, keepdims=True)
            else:
                stab = jnp.max(xp, axis=(-1, -2), keepdims=True)
            return ratio * (jnp.exp(xp - diag - stab) + EPS_K)

        def layer_norm(x, g, b):
            mu = jnp.mean(x, axis=-1, keepdims=True)
            var = jnp.mean(jnp.square(x - mu), axis=-1, keepdims=True)
            return (x - mu) * jax.lax.rsqrt(var + LN_EPS) * g + b
        key = jax.random.key(seed)
        ks = jax.random.split(key, 12)
        s = 0.02
        return {'video': jax.random.normal(ks[0], (B, N, D_MODEL), jnp.float32), 'Wq': jax.random.normal(ks[1], (D_MODEL, D_MODEL), jnp.float32) * s, 'bq': jnp.zeros((D_MODEL,), jnp.float32), 'Wk': jax.random.normal(ks[2], (D_MODEL, D_MODEL), jnp.float32) * s, 'bk': jnp.zeros((D_MODEL,), jnp.float32), 'Wv': jax.random.normal(ks[3], (D_MODEL, D_MODEL), jnp.float32) * s, 'bv': jnp.zeros((D_MODEL,), jnp.float32), 'Wo': jax.random.normal(ks[4], (D_MODEL, D_MODEL), jnp.float32) * s, 'bo': jnp.zeros((D_MODEL,), jnp.float32), 'proj': jax.random.normal(ks[5], (M, DH), jnp.float32), 'W1': jax.random.normal(ks[6], (DFF, D_MODEL), jnp.float32) * s, 'b1': jnp.zeros((DFF,), jnp.float32), 'W2': jax.random.normal(ks[7], (D_MODEL, DFF), jnp.float32) * s, 'b2': jnp.zeros((D_MODEL,), jnp.float32), 'g2': jnp.ones((D_MODEL,), jnp.float32), 'be2': jnp.zeros((D_MODEL,), jnp.float32), 'g3': jnp.ones((D_MODEL,), jnp.float32), 'be3': jnp.zeros((D_MODEL,), jnp.float32)}
    _L0_attn_in = _L0_attn_setup()

    def _L0_ffn_setup():
        import jax, jax.numpy as jnp
        import numpy as np
        NUM_HEADS = 16
        TOP_K = 2
        ROPE_BASE = 10000.0
        LN_EPS = 1e-05

        def _rope_sin_cos(S, D, dtype):
            inv_freq = 1.0 / ROPE_BASE ** (jnp.arange(0, D, 2, dtype=jnp.float32) / D)
            freqs = jnp.arange(S, dtype=jnp.float32)[:, None] * inv_freq[None, :]
            sin = jnp.sin(freqs).astype(dtype)[None, :, None, :]
            cos = jnp.cos(freqs).astype(dtype)[None, :, None, :]
            return (sin, cos)

        def _apply_rope(x, sin, cos):
            x1, x2 = (x[..., 0::2], x[..., 1::2])
            r1 = x1 * cos - x2 * sin
            r2 = x1 * sin + x2 * cos
            return jnp.stack([r1, r2], axis=-1).reshape(x.shape)

        def _layer_norm(x, w, b):
            mu = jnp.mean(x, axis=-1, keepdims=True)
            var = jnp.mean(jnp.square(x - mu), axis=-1, keepdims=True)
            return (x - mu) * jax.lax.rsqrt(var + LN_EPS) * w + b
        key = jax.random.key(seed)
        ks = jax.random.split(key, 8)
        B, S, E, NE = (2, 256, 128, 8)
        s = 0.02
        return {'x': jax.random.normal(ks[0], (B, S, E), dtype=jnp.float32), 'in_proj_w': jax.random.normal(ks[1], (3 * E, E), dtype=jnp.float32) * s, 'in_proj_b': jnp.zeros((3 * E,), dtype=jnp.float32), 'out_proj_w': jax.random.normal(ks[2], (E, E), dtype=jnp.float32) * s, 'out_proj_b': jnp.zeros((E,), dtype=jnp.float32), 'gate_w': jax.random.normal(ks[3], (NE, E), dtype=jnp.float32) * s, 'gate_b': jnp.zeros((NE,), dtype=jnp.float32), 'expert_w': jax.random.normal(ks[4], (NE, E, E), dtype=jnp.float32) * s, 'expert_b': jnp.zeros((NE, E), dtype=jnp.float32), 'ln1_w': jnp.ones((E,), dtype=jnp.float32), 'ln1_b': jnp.zeros((E,), dtype=jnp.float32), 'ln2_w': jnp.ones((E,), dtype=jnp.float32), 'ln2_b': jnp.zeros((E,), dtype=jnp.float32)}
    _L0_ffn_in = _L0_ffn_setup()

    def _L1_attn_setup():
        import jax, jax.numpy as jnp
        import numpy as np
        B, S, D, H = (2, 128, 128, 16)
        DK = D // H
        DE = D // 8
        SCALE = 1.0 / float(np.sqrt(DK))

        def _reference_tuple_inner(X, Wq, Wk, Wv, Wo, We):
            b, s, d = X.shape
            h, dk = (H, d // H)
            ctx = X @ We.T
            influence = jnp.einsum('bqe,bke->bqk', ctx, ctx)

            def heads(W):
                return (X @ W.T).reshape(b, s, h, dk).transpose(0, 2, 1, 3)
            Q, K, V = (heads(Wq), heads(Wk), heads(Wv))
            scores = jnp.einsum('bhqd,bhkd->bhqk', Q, K) * SCALE + 0.1 * influence[:, None]
            attn = jax.nn.softmax(scores, axis=-1)
            out = jnp.einsum('bhqk,bhkd->bhqd', attn, V)
            out = out.transpose(0, 2, 1, 3).reshape(b, s, d) @ Wo.T
            return (out, attn)
        key = jax.random.key(seed)
        ks = jax.random.split(key, 6)
        p = lambda k, shape: jax.random.normal(k, shape, dtype=jnp.float32) * 0.02
        return {'X': jax.random.normal(ks[0], (B, S, D), dtype=jnp.float32), 'Wq': p(ks[1], (D, D)), 'Wk': p(ks[2], (D, D)), 'Wv': p(ks[3], (D, D)), 'Wo': p(ks[4], (D, D)), 'We': p(ks[5], (DE, D))}
    _L1_attn_in = _L1_attn_setup()

    def _L1_ffn_setup():
        import jax, jax.numpy as jnp
        import numpy as np
        B, S, D, F, E, NS, K = (2, 128, 128, 512, 8, 8, 2)
        FS = F // NS
        key = jax.random.key(seed)
        ks = jax.random.split(key, 8)
        scale = 0.02
        return {'hidden_states': jax.random.normal(ks[0], (B, S, D), jnp.float32), 'gate_W': jax.random.normal(ks[1], (E, D), jnp.float32) * scale, 'w1_e': jax.random.normal(ks[2], (E, D, F), jnp.float32) * scale, 'w3_e': jax.random.normal(ks[3], (E, D, F), jnp.float32) * scale, 'w2_e': jax.random.normal(ks[4], (E, F, D), jnp.float32) * scale, 'w1_s': jax.random.normal(ks[5], (NS, D, FS), jnp.float32) * scale, 'w3_s': jax.random.normal(ks[6], (NS, D, FS), jnp.float32) * scale, 'w2_s': jax.random.normal(ks[7], (NS, FS, D), jnp.float32) * scale}
    _L1_ffn_in = _L1_ffn_setup()
    _d = {'L0_attn_video': _L0_attn_in['video'], 'L0_attn_Wq': _L0_attn_in['Wq'], 'L0_attn_bq': _L0_attn_in['bq'], 'L0_attn_Wk': _L0_attn_in['Wk'], 'L0_attn_bk': _L0_attn_in['bk'], 'L0_attn_Wv': _L0_attn_in['Wv'], 'L0_attn_bv': _L0_attn_in['bv'], 'L0_attn_Wo': _L0_attn_in['Wo'], 'L0_attn_bo': _L0_attn_in['bo'], 'L0_attn_proj': _L0_attn_in['proj'], 'L0_attn_W1': _L0_attn_in['W1'], 'L0_attn_b1': _L0_attn_in['b1'], 'L0_attn_W2': _L0_attn_in['W2'], 'L0_attn_b2': _L0_attn_in['b2'], 'L0_attn_g2': _L0_attn_in['g2'], 'L0_attn_be2': _L0_attn_in['be2'], 'L0_attn_g3': _L0_attn_in['g3'], 'L0_attn_be3': _L0_attn_in['be3'], 'L0_ffn_in_proj_w': _L0_ffn_in['in_proj_w'], 'L0_ffn_in_proj_b': _L0_ffn_in['in_proj_b'], 'L0_ffn_out_proj_w': _L0_ffn_in['out_proj_w'], 'L0_ffn_out_proj_b': _L0_ffn_in['out_proj_b'], 'L0_ffn_gate_w': _L0_ffn_in['gate_w'], 'L0_ffn_gate_b': _L0_ffn_in['gate_b'], 'L0_ffn_expert_w': _L0_ffn_in['expert_w'], 'L0_ffn_expert_b': _L0_ffn_in['expert_b'], 'L0_ffn_ln1_w': _L0_ffn_in['ln1_w'], 'L0_ffn_ln1_b': _L0_ffn_in['ln1_b'], 'L0_ffn_ln2_w': _L0_ffn_in['ln2_w'], 'L0_ffn_ln2_b': _L0_ffn_in['ln2_b'], 'L1_attn_Wq': _L1_attn_in['Wq'], 'L1_attn_Wk': _L1_attn_in['Wk'], 'L1_attn_Wv': _L1_attn_in['Wv'], 'L1_attn_Wo': _L1_attn_in['Wo'], 'L1_attn_We': _L1_attn_in['We'], 'L1_ffn_gate_W': _L1_ffn_in['gate_W'], 'L1_ffn_w1_e': _L1_ffn_in['w1_e'], 'L1_ffn_w3_e': _L1_ffn_in['w3_e'], 'L1_ffn_w2_e': _L1_ffn_in['w2_e'], 'L1_ffn_w1_s': _L1_ffn_in['w1_s'], 'L1_ffn_w3_s': _L1_ffn_in['w3_s'], 'L1_ffn_w2_s': _L1_ffn_in['w2_s']}
    _x0 = _d['L0_attn_video']
    _d['L0_attn_video'] = jax.random.normal(jax.random.fold_in(jax.random.key(seed), 1), (8, 512, 128), dtype=_x0.dtype)
    del _x0
    return _d

def reference(L0_attn_video, L0_attn_Wq, L0_attn_bq, L0_attn_Wk, L0_attn_bk, L0_attn_Wv, L0_attn_bv, L0_attn_Wo, L0_attn_bo, L0_attn_proj, L0_attn_W1, L0_attn_b1, L0_attn_W2, L0_attn_b2, L0_attn_g2, L0_attn_be2, L0_attn_g3, L0_attn_be3, L0_ffn_in_proj_w, L0_ffn_in_proj_b, L0_ffn_out_proj_w, L0_ffn_out_proj_b, L0_ffn_gate_w, L0_ffn_gate_b, L0_ffn_expert_w, L0_ffn_expert_b, L0_ffn_ln1_w, L0_ffn_ln1_b, L0_ffn_ln2_w, L0_ffn_ln2_b, L1_attn_Wq, L1_attn_Wk, L1_attn_Wv, L1_attn_Wo, L1_attn_We, L1_ffn_gate_W, L1_ffn_w1_e, L1_ffn_w3_e, L1_ffn_w2_e, L1_ffn_w1_s, L1_ffn_w3_s, L1_ffn_w2_s):

    def _L0_attn_ref(video, Wq, bq, Wk, bk, Wv, bv, Wo, bo, proj, W1, b1, W2, b2, g2, be2, g3, be3):
        import jax, jax.numpy as jnp
        import numpy as np
        B, N, D_MODEL, HEADS, DFF, M = (4, 512, 128, 16, 512, 32)
        DH = D_MODEL // HEADS
        EPS_K = 0.0001
        LN_EPS = 1e-05

        def softmax_kernel(x, proj, is_query):
            norm = x.shape[-1] ** (-0.25)
            ratio = proj.shape[0] ** (-0.5)
            xp = jnp.einsum('bhnd,md->bhnm', x * norm, proj)
            diag = jnp.sum(jnp.square(x), axis=-1, keepdims=True) * 0.5 * (norm * norm)
            if is_query:
                stab = jnp.max(xp, axis=-1, keepdims=True)
            else:
                stab = jnp.max(xp, axis=(-1, -2), keepdims=True)
            return ratio * (jnp.exp(xp - diag - stab) + EPS_K)

        def layer_norm(x, g, b):
            mu = jnp.mean(x, axis=-1, keepdims=True)
            var = jnp.mean(jnp.square(x - mu), axis=-1, keepdims=True)
            return (x - mu) * jax.lax.rsqrt(var + LN_EPS) * g + b
        b, n, d = video.shape
        split = lambda t: t.reshape(b, n, HEADS, DH).transpose(0, 2, 1, 3)
        q = split(video @ Wq.T + bq)
        k = split(video @ Wk.T + bk)
        v = split(video @ Wv.T + bv)
        qp = softmax_kernel(q, proj, is_query=True)
        kp = softmax_kernel(k, proj, is_query=False)
        k_sum = jnp.sum(kp, axis=2)
        denom = jnp.einsum('bhnm,bhm->bhn', qp, k_sum)
        ctx = jnp.einsum('bhnm,bhnd->bhmd', kp, v)
        out = jnp.einsum('bhnm,bhmd->bhnd', qp, ctx) / denom[..., None]
        attn = out.transpose(0, 2, 1, 3).reshape(b, n, d) @ Wo.T + bo
        x = layer_norm(video + attn, g2, be2)
        ff = jax.nn.relu(x @ W1.T + b1) @ W2.T + b2
        return layer_norm(x + ff, g3, be3)

    def _L0_ffn_ref(x, in_proj_w, in_proj_b, out_proj_w, out_proj_b, gate_w, gate_b, expert_w, expert_b, ln1_w, ln1_b, ln2_w, ln2_b):
        import jax, jax.numpy as jnp
        import numpy as np
        NUM_HEADS = 16
        TOP_K = 2
        ROPE_BASE = 10000.0
        LN_EPS = 1e-05

        def _rope_sin_cos(S, D, dtype):
            inv_freq = 1.0 / ROPE_BASE ** (jnp.arange(0, D, 2, dtype=jnp.float32) / D)
            freqs = jnp.arange(S, dtype=jnp.float32)[:, None] * inv_freq[None, :]
            sin = jnp.sin(freqs).astype(dtype)[None, :, None, :]
            cos = jnp.cos(freqs).astype(dtype)[None, :, None, :]
            return (sin, cos)

        def _apply_rope(x, sin, cos):
            x1, x2 = (x[..., 0::2], x[..., 1::2])
            r1 = x1 * cos - x2 * sin
            r2 = x1 * sin + x2 * cos
            return jnp.stack([r1, r2], axis=-1).reshape(x.shape)

        def _layer_norm(x, w, b):
            mu = jnp.mean(x, axis=-1, keepdims=True)
            var = jnp.mean(jnp.square(x - mu), axis=-1, keepdims=True)
            return (x - mu) * jax.lax.rsqrt(var + LN_EPS) * w + b
        B, S, E = x.shape
        H = NUM_HEADS
        D = E // H
        xh = x.reshape(B, S, H, D)
        sin, cos = _rope_sin_cos(S, D, x.dtype)
        q_in = _apply_rope(xh, sin, cos).reshape(B, S, E)
        k_in = q_in
        v_in = x
        Wq, Wk, Wv = jnp.split(in_proj_w, 3, axis=0)
        bq, bk, bv = jnp.split(in_proj_b, 3, axis=0)
        q = (q_in @ Wq.T + bq).reshape(B, S, H, D)
        k = (k_in @ Wk.T + bk).reshape(B, S, H, D)
        v = (v_in @ Wv.T + bv).reshape(B, S, H, D)
        scale = 1.0 / jnp.sqrt(jnp.asarray(D, dtype=x.dtype))
        scores = jnp.einsum('bqhd,bkhd->bhqk', q, k) * scale
        causal = jnp.tril(jnp.ones((S, S), dtype=bool))
        scores = jnp.where(causal[None, None], scores, jnp.asarray(-jnp.inf, dtype=scores.dtype))
        attn = jax.nn.softmax(scores, axis=-1)
        ctx = jnp.einsum('bhqk,bkhd->bqhd', attn, v).reshape(B, S, E)
        attn_out = ctx @ out_proj_w.T + out_proj_b
        x1 = _layer_norm(x + attn_out, ln1_w, ln1_b)
        gates = jax.nn.softmax(x1 @ gate_w.T + gate_b, axis=-1)
        _, top_idx = jax.lax.top_k(gates, TOP_K)
        top_gates = jnp.take_along_axis(gates, top_idx, axis=-1)
        expert_outputs = jnp.einsum('bsd,efd->bsef', x1, expert_w) + expert_b[None, None]
        sel = jnp.take_along_axis(expert_outputs, top_idx[..., None], axis=2)
        moe_out = jnp.sum(sel * top_gates[..., None], axis=2)
        return _layer_norm(x1 + moe_out, ln2_w, ln2_b)

    def _L1_attn_ref(X, Wq, Wk, Wv, Wo, We):
        import jax, jax.numpy as jnp
        import numpy as np
        B, S, D, H = (2, 128, 128, 16)
        DK = D // H
        DE = D // 8
        SCALE = 1.0 / float(np.sqrt(DK))

        def _reference_tuple_inner(X, Wq, Wk, Wv, Wo, We):
            b, s, d = X.shape
            h, dk = (H, d // H)
            ctx = X @ We.T
            influence = jnp.einsum('bqe,bke->bqk', ctx, ctx)

            def heads(W):
                return (X @ W.T).reshape(b, s, h, dk).transpose(0, 2, 1, 3)
            Q, K, V = (heads(Wq), heads(Wk), heads(Wv))
            scores = jnp.einsum('bhqd,bhkd->bhqk', Q, K) * SCALE + 0.1 * influence[:, None]
            attn = jax.nn.softmax(scores, axis=-1)
            out = jnp.einsum('bhqk,bhkd->bhqd', attn, V)
            out = out.transpose(0, 2, 1, 3).reshape(b, s, d) @ Wo.T
            return (out, attn)
        return _reference_tuple_inner(X, Wq, Wk, Wv, Wo, We)[0]

    def _L1_ffn_ref(hidden_states, gate_W, w1_e, w3_e, w2_e, w1_s, w3_s, w2_s):
        import jax, jax.numpy as jnp
        import numpy as np
        B, S, D, F, E, NS, K = (2, 128, 128, 512, 8, 8, 2)
        FS = F // NS
        b, s, d = hidden_states.shape
        e = gate_W.shape[0]
        flat = hidden_states.reshape(-1, d)
        T = flat.shape[0]
        logits = (flat @ gate_W.T).astype(jnp.float32)
        probs = jax.nn.softmax(logits, axis=-1)
        top_v, top_i = jax.lax.top_k(probs, K)
        gates = jnp.zeros((T, e), probs.dtype).at[jnp.arange(T)[:, None], top_i].set(top_v)
        g = jax.nn.silu(jnp.einsum('td,edf->etf', flat, w1_e))
        u = jnp.einsum('td,edf->etf', flat, w3_e)
        out_e = jnp.einsum('etf,efd->etd', g * u, w2_e)
        routed = jnp.einsum('te,etd->td', gates, out_e).reshape(b, s, d)
        gs = jax.nn.silu(jnp.einsum('bsd,ndf->nbsf', hidden_states, w1_s))
        us = jnp.einsum('bsd,ndf->nbsf', hidden_states, w3_s)
        shared = jnp.einsum('nbsf,nfd->bsd', gs * us, w2_s) / w1_s.shape[0]
        alpha = 0.5
        return alpha * shared + (1.0 - alpha) * routed
    x = L0_attn_video
    x = x + _layernorm(_L0_attn_ref(_layernorm(x, axis=-1), L0_attn_Wq, L0_attn_bq, L0_attn_Wk, L0_attn_bk, L0_attn_Wv, L0_attn_bv, L0_attn_Wo, L0_attn_bo, L0_attn_proj, L0_attn_W1, L0_attn_b1, L0_attn_W2, L0_attn_b2, L0_attn_g2, L0_attn_be2, L0_attn_g3, L0_attn_be3), axis=-1)
    x = x + _layernorm(_L0_ffn_ref(_layernorm(x, axis=-1), L0_ffn_in_proj_w, L0_ffn_in_proj_b, L0_ffn_out_proj_w, L0_ffn_out_proj_b, L0_ffn_gate_w, L0_ffn_gate_b, L0_ffn_expert_w, L0_ffn_expert_b, L0_ffn_ln1_w, L0_ffn_ln1_b, L0_ffn_ln2_w, L0_ffn_ln2_b), axis=-1)
    x = x + _layernorm(_L1_attn_ref(_layernorm(x, axis=-1), L1_attn_Wq, L1_attn_Wk, L1_attn_Wv, L1_attn_Wo, L1_attn_We), axis=-1)
    x = x + _layernorm(_L1_ffn_ref(_layernorm(x, axis=-1), L1_ffn_gate_W, L1_ffn_w1_e, L1_ffn_w3_e, L1_ffn_w2_e, L1_ffn_w1_s, L1_ffn_w3_s, L1_ffn_w2_s), axis=-1)
    return x

_drawn_inputs = setup_inputs


def setup_inputs(seed=0):
    import zlib

    import numpy as np

    out = dict(_drawn_inputs(seed))
    spreads = {'L0_attn_bq': (0.0, 2.0),
     'L0_attn_bk': (0.0, 2.0),
     'L0_attn_bv': (0.0, 0.268),
     'L0_attn_bo': (0.0, 0.1),
     'L0_attn_b1': (0.0, 0.1),
     'L0_attn_b2': (0.0, 0.1),
     'L0_attn_g2': (1.0, 0.2),
     'L0_attn_be2': (0.0, 0.1),
     'L0_attn_g3': (1.0, 0.2),
     'L0_attn_be3': (0.0, 0.1),
     'L0_ffn_in_proj_b': (0.0, 0.311),
     'L0_ffn_out_proj_b': (0.0, 0.1),
     'L0_ffn_gate_b': (0.0, 0.409),
     'L0_ffn_expert_b': (0.0, 0.499),
     'L0_ffn_ln1_w': (1.0, 0.2),
     'L0_ffn_ln1_b': (0.0, 0.1),
     'L0_ffn_ln2_w': (1.0, 0.2),
     'L0_ffn_ln2_b': (0.0, 0.1)}
    factors = {'L0_attn_Wq': 200.0,
     'L0_attn_Wk': 64.0,
     'L0_attn_Wv': 8.0,
     'L0_attn_proj': 200.0,
     'L0_ffn_in_proj_w': 7.341,
     'L0_ffn_out_proj_w': 2.83,
     'L0_ffn_gate_w': 2.898,
     'L1_attn_Wq': 3.775,
     'L1_attn_Wk': 3.705,
     'L1_attn_We': 6.726}
    for name, (base, spread) in spreads.items():
        noise = np.random.default_rng([zlib.crc32(name.encode()), seed]).standard_normal(out[name].shape)
        drawn = base * np.exp(spread * noise) if base else spread * noise
        out[name] = jnp.asarray(drawn.astype(out[name].dtype))
    for name, factor in factors.items():
        out[name] = (out[name] * factor).astype(out[name].dtype)
    return out
```

```python
from contextlib import ExitStack

import concourse.bass as bass
from concourse import mybir

F32 = mybir.dt.float32
F32R = mybir.dt.float32r
BF16 = mybir.dt.bfloat16
ALU = mybir.AluOpType
ACT = mybir.ActivationFunctionType
AXX = mybir.AxisListType.X
RMAX = bass.bass_isa.ReduceOp.max

B, S, D = 8, 512, 128
P = 128
T = S // P
H, DH = 16, 8
M = 32
F = 512
FC = F // P
NE = 8
EPS = 1e-5
EPS_K = 1e-4
SCALE = DH ** -0.5




class Chain:

    def __init__(self, eng, sem, per, passed):
        self.eng, self.sem, self.per, self.passed, self.b, self.n = eng, sem, per, passed, 0, 0

    def start(self, b):
        self.b, self.n = b, 0

    def do(self, ins):
        self.n += 1
        return ins.then_inc(self.sem, 1)

    def sync(self):
        self.eng.wait_ge(self.sem, self.b * self.per + self.n)

    def end(self):
        assert self.n == self.per, f"the chain signals {self.n} times an iteration"


def bc(ap, n):
    return ap.unsqueeze(1).broadcast_to([ap.shape[0], n, ap.shape[1]])


def each(ap, n):
    return ap.unsqueeze(len(ap.shape)).broadcast_to(list(ap.shape) + [n])


def ln_stats(nc, ch, src, stats, mv):
    for t in range(T):
        ch.do(nc.vector.bn_stats(stats[:, t, :], src[:, t, :]))
    ch.sync()
    ch.eng.sem_inc(ch.passed, 1)
    for t in range(T):
        ch.do(nc.vector.bn_aggr(mv[:, t, :], stats[:, t, :]))
    ch.sync()
    return nc.vector.tensor_scalar_add(mv[:, :, 1], mv[:, :, 1], EPS)


def ln_apply(nc, ch, dst, src, mv, rstd):
    for t in range(T):
        ch.do(nc.vector.tensor_scalar(dst[:, t, :], src[:, t, :], mv[:, t, 0:1], rstd[:, t:t + 1],
                                      ALU.subtract, ALU.mult))


def mm3(nc, out, a, b, start=True, stop=True):
    nc.tensor.matmul(out, a[0], b[0], start=start, stop=False)
    nc.tensor.matmul(out, a[0], b[1], start=False, stop=False)
    return nc.tensor.matmul(out, a[1], b[0], start=False, stop=stop)


def clear(nc, sems):
    with nc.Block() as block:
        @block.gpsimd
        def _(pool):
            for sem in sems:
                pool.sem_clear(sem)


def performer_layer(nc, X, ident, w, consts):
    ctx = ExitStack()
    with ctx:
        sb = lambda name, shape, dt=F32: ctx.enter_context(nc.sbuf_tensor("pf_" + name, shape, dt))
        sems = []

        def sem(name):
            sems.append(ctx.enter_context(nc.semaphore("pf_" + name)))
            return sems[-1]

        pb = [ctx.enter_context(nc.psum_tensor(f"pf_pb{i}", [P, 512], F32)) for i in range(8)]

        wq, wk, wv, wo = (sb(n, [P, D]) for n in ("wq", "wk", "wv", "wo"))
        w1 = sb("w1", [P, F])
        w2 = sb("w2", [P, FC, D])
        bq, bk = sb("bq", [P, 1]), sb("bk", [P, 1])
        b1 = sb("b1", [P, FC])
        bv, bo, b2, g2, be2, g3, be3 = (sb(n, [P, D]) for n in ("bv", "bo", "b2", "g2", "be2", "g3", "be3"))
        feats = sb("feats", [P, H * M])
        hsel = sb("hsel", [P, 32])
        bmask = sb("bmask", [P, P])
        ones = sb("ones", [P, 32])
        stats, mv = sb("stats", [P, T, 6]), sb("mv", [P, T, 2])
        half, rstd = sb("half", [P, T]), sb("rstd", [P, T])
        y, yT = sb("y", [P, T, D]), sb("yT", [P, S])
        qT, kT, sqq, sqk = (sb(n, [P, S]) for n in ("qT", "kT", "sqq", "sqk"))
        v = sb("v", [P, T, D])
        dgT, dg = sb("dgT", [64, S]), sb("dg", [P, T, 64])
        kmx, km, stab = sb("kmx", [P, T, H]), sb("km", [P, H]), sb("stab", [P, H])
        ck, qmx, cq = sb("ck", [P, T, H]), sb("qmx", [P, T, H]), sb("cq", [P, T, H])
        kp, qp = sb("kp", [P, T, H * M]), sb("qp", [P, T, H * M])
        cm, cx = sb("cm", [P, 2, P]), sb("cx", [P, 2, P])
        qpT = sb("qpT", [P, T, S])
        rd, oT = sb("rd", [P, S]), sb("oT", [P, S])
        r, x1, x1T = sb("r", [P, T, D]), sb("x1", [P, T, D]), sb("x1T", [P, S])
        hT = sb("hT", [P, FC, S])
        z = sb("z", [P, T, D])

        loaded, projected, init = sem("loaded"), sem("projected"), sem("init")
        var_ready, rstd_ready, half_ready = sem("var_ready"), sem("rstd_ready"), sem("half_ready")
        y_ready, yT_ps, yT_ready = sem("y_ready"), sem("yT_ps"), sem("yT_ready")
        qk_ps, v_ps, qk_ready, v_ready = sem("qk_ps"), sem("v_ps"), sem("qk_ready"), sem("v_ready")
        dg_ps, dgT_ready, dgt_ps, dg_ready = sem("dg_ps"), sem("dgT_ready"), sem("dgt_ps"), sem("dg_ready")
        kx_ps, qx_ps, km_ready, stab_ready = sem("kx_ps"), sem("qx_ps"), sem("km_ready"), sem("stab_ready")
        z_ready, e_ready, kp_ready, qp_ready = sem("z_ready"), sem("e_ready"), sem("kp_ready"), sem("qp_ready")
        cm_ps, cm_ready, cx_ps, cx_ready = sem("cm_ps"), sem("cm_ready"), sem("cx_ps"), sem("cx_ready")
        qpT_ps, qpT_ready, nd_ps, oT_ready = sem("qpT_ps"), sem("qpT_ready"), sem("nd_ps"), sem("oT_ready")
        wo_ps, x1_ready, x1T_ps, x1T_ready = sem("wo_ps"), sem("x1_ready"), sem("x1T_ps"), sem("x1T_ready")
        h_ps, h_ready, w2_ps = sem("h_ps"), sem("h_ready"), sem("w2_ps")
        dve_steps = sem("dve_steps")
        PER = 4 * 3 * T + 2 * T + 11

        loads = [(wq, w["WqT"]), (wk, w["WkT"]), (wv, w["WvT"]), (wo, w["WoT"]), (w1, w["W1T"]), (w2, w["W2T"]),
                 (bq, w["bq"]), (bk, w["bk"]), (b1, w["b1"]), (bv, w["bv"]), (bo, w["bo"]), (b2, w["b2"]),
                 (g2, w["g2"]), (be2, w["be2"]), (g3, w["g3"]), (be3, w["be3"]), (hsel, consts["hsel"]),
                 (bmask, consts["bmask"])]

        passed = sem("passed")
        ctx.callback(clear, nc, sems)
        block = ctx.enter_context(nc.Block())

        @block.sync
        def _(sp):
            for dst, src in loads:
                sp.dma_start(dst[:], src).then_inc(loaded, 16)
            sp.wait_ge(init, 1)
            for h in range(H):
                sp.dma_start(feats[h * DH:(h + 1) * DH, h * M:(h + 1) * M], w["projT"]).then_inc(projected, 16)

        @block.gpsimd
        def _(pool):
            nc.gpsimd.memset(feats[:], 0.0).then_inc(init, 1)
            nc.gpsimd.memset(ones[:], 1.0).then_inc(init, 1)
            nc.gpsimd.memset(half[:], -0.5).then_inc(half_ready, 1)
            pool.wait_ge(half_ready, 1)
            with pool.Fori(0, B) as b:
                def rsqrt(k):
                    pool.wait_ge(var_ready, b * 4 + k + 1)
                    nc.gpsimd.tensor_tensor(rstd[:], mv[:, :, 1], half[:], ALU.pow).then_inc(rstd_ready, 1)
                rsqrt(0)
                pool.wait_ge(km_ready, b + 1)
                pool.sem_inc(passed, 1)
                nc.gpsimd.partition_all_reduce(stab[:], km[:], P, RMAX).then_inc(stab_ready, 1)
                for k in range(1, 4):
                    rsqrt(k)

        @block.vector
        def _(dve):
            ch = Chain(dve, dve_steps, PER, passed)
            dve.wait_ge(loaded, 16 * len(loads))
            dve.wait_ge(projected, 16 * H)
            dve.wait_ge(init, 2)
            nc.vector.tensor_scalar_mul(feats[:], feats[:], DH ** -0.25).then_inc(init, 1)
            with dve.Fori(0, B) as b:
                ch.start(b)

                def layer_norm(k, dst, src):
                    ln_stats(nc, ch, src, stats, mv).then_inc(var_ready, 1)
                    dve.wait_ge(rstd_ready, b * 4 + k + 1)
                    ln_apply(nc, ch, dst, src, mv, rstd)
                    ch.sync()

                x = X[:, bass.ds(b * T, T), :]
                layer_norm(0, y, x)
                dve.sem_inc(y_ready, 1)
                dve.wait_ge(v_ps, b + 1)
                nc.vector.tensor_tensor(v[:], pb[3][:].rearrange("p (t d) -> p t d", t=T), bc(bv[:], T),
                                        ALU.add).then_inc(v_ready, 1)
                dve.wait_ge(dgt_ps, b + 1)
                nc.vector.tensor_copy(dg[:], pb[2][:, 0:T * 64].rearrange("p (t k) -> p t k", t=T)
                                      ).then_inc(dg_ready, 1)
                dve.wait_ge(dg_ready, b + 1)
                feat = lambda bank: bank[:].rearrange("p (h m) -> p h m", m=M)
                for t in range(T):
                    dve.wait_ge(kx_ps, b * T + t + 1)
                    ch.do(nc.vector.tensor_reduce(kmx[:, t, :], feat(pb[4 + t]), AXX, ALU.max))
                ch.sync()
                nc.vector.tensor_reduce(km[:], kmx[:].rearrange("p t h -> p h t"), AXX, ALU.max).then_inc(km_ready, 1)
                for t in range(T):
                    dve.wait_ge(qx_ps, b * T + t + 1)
                    ch.do(nc.vector.tensor_reduce(qmx[:, t, :], feat(pb[t]), AXX, ALU.max))
                ch.sync()
                ch.do(nc.vector.tensor_tensor(cq[:], qmx[:], dg[:, :, 0:H], ALU.add))
                dve.wait_ge(stab_ready, b + 1)
                ch.do(nc.vector.tensor_tensor(ck[:], dg[:, :, 32:32 + H], bc(stab[:], T), ALU.add))
                ch.sync()
                for t in range(T):
                    last = nc.vector.tensor_tensor(kp[:, t, :].rearrange("p (h m) -> p h m", m=M), feat(pb[4 + t]),
                                                   each(ck[:, t, :], M), ALU.subtract)
                last.then_inc(z_ready, 1)
                for t in range(T):
                    last = nc.vector.tensor_tensor(qp[:, t, :].rearrange("p (h m) -> p h m", m=M), feat(pb[t]),
                                                   each(cq[:, t, :], M), ALU.subtract)
                last.then_inc(z_ready, 1)
                for k, (tile, ready) in enumerate(((kp, kp_ready), (qp, qp_ready))):
                    dve.wait_ge(e_ready, b * 2 + k + 1)
                    nc.vector.tensor_scalar(tile[:], tile[:], EPS_K, M ** -0.5, ALU.add, ALU.mult).then_inc(ready, 1)
                dve.wait_ge(cm_ps, b + 1)
                nc.vector.tensor_tensor(cm[:, 0, :], pb[4][:, 0:P], bmask[:], ALU.mult)
                nc.vector.tensor_tensor(cm[:, 1, :], pb[5][:, 0:P], bmask[:], ALU.mult).then_inc(cm_ready, 1)
                dve.wait_ge(nd_ps, b + 1)
                ch.do(nc.vector.reciprocal(rd[:], pb[7][:]))
                ch.sync()
                nc.vector.tensor_tensor(oT[:], pb[6][:], rd[:], ALU.mult).then_inc(oT_ready, 1)
                dve.wait_ge(wo_ps, b + 1)
                ch.do(nc.vector.tensor_tensor(r[:], pb[4][:].rearrange("p (t d) -> p t d", t=T), y[:], ALU.add))
                ch.sync()
                ch.do(nc.vector.tensor_tensor(r[:], r[:], bc(bo[:], T), ALU.add))
                ch.sync()
                layer_norm(1, x1, r)
                ch.do(nc.vector.tensor_tensor(x1[:], x1[:], bc(g2[:], T), ALU.mult))
                ch.sync()
                nc.vector.tensor_tensor(x1[:], x1[:], bc(be2[:], T), ALU.add).then_inc(x1_ready, 1)
                dve.wait_ge(x1_ready, b + 1)
                dve.wait_ge(w2_ps, b + 1)
                ch.do(nc.vector.tensor_tensor(r[:], pb[6][:].rearrange("p (t d) -> p t d", t=T), x1[:], ALU.add))
                ch.sync()
                ch.do(nc.vector.tensor_tensor(r[:], r[:], bc(b2[:], T), ALU.add))
                ch.sync()
                layer_norm(2, z, r)
                ch.do(nc.vector.tensor_tensor(z[:], z[:], bc(g3[:], T), ALU.mult))
                ch.sync()
                ch.do(nc.vector.tensor_tensor(z[:], z[:], bc(be3[:], T), ALU.add))
                ch.sync()
                layer_norm(3, r, z)
                ch.do(nc.vector.tensor_tensor(x, x, r[:], ALU.add))
                ch.sync()
                ch.end()

        @block.scalar
        def _(act):
            act.wait_ge(loaded, 16 * len(loads))
            with act.Fori(0, B) as b:
                act.wait_ge(yT_ps, b + 1)
                nc.scalar.activation(yT[:], pb[0][:], ACT.Copy).then_inc(yT_ready, 1)
                for k, (bank, bias, lin, sq) in enumerate(((pb[1], bq, qT, sqq), (pb[2], bk, kT, sqk))):
                    act.wait_ge(qk_ps, b * 2 + k + 1)
                    nc.scalar.activation(lin[:], bank[:], ACT.Identity, bias=bias[:]).then_inc(qk_ready, 1)
                    nc.scalar.activation(sq[:], bank[:], ACT.Square, bias=bias[:]).then_inc(qk_ready, 1)
                act.wait_ge(dg_ps, b + 1)
                nc.scalar.activation(dgT[:], pb[1][0:64, :], ACT.Copy, scale=0.5 * DH ** -0.5).then_inc(dgT_ready, 1)
                for k, tile in enumerate((kp, qp)):
                    act.wait_ge(z_ready, b * 2 + k + 1)
                    nc.scalar.activation(tile[:], tile[:], ACT.Exp).then_inc(e_ready, 1)
                act.wait_ge(cx_ps, b + 1)
                nc.scalar.activation(cx[:], pb[4][:, 0:2 * P].rearrange("p (k m) -> p k m", k=2),
                                     ACT.Copy).then_inc(cx_ready, 1)
                for g in range(T):
                    act.wait_ge(qpT_ps, b * T + g + 1)
                    nc.scalar.activation(qpT[:, g, :], pb[g][:], ACT.Copy).then_inc(qpT_ready, 1)
                act.wait_ge(x1T_ps, b + 1)
                nc.scalar.activation(x1T[:], pb[5][:], ACT.Copy).then_inc(x1T_ready, 1)
                for c in range(FC):
                    act.wait_ge(h_ps, b * FC + c + 1)
                    nc.scalar.activation(hT[:, c, :], pb[c][:], ACT.Relu, bias=b1[:, c:c + 1]).then_inc(h_ready, 1)

        @block.tensor
        def _(pe):
            pe.wait_ge(loaded, 16 * len(loads))
            pe.wait_ge(init, 3)
            tile = lambda ap, t: ap[:, t * P:(t + 1) * P]

            def transposed(bank, src, signal):
                for t in range(T):
                    last = nc.tensor.transpose(tile(bank, t), src[:, t, :], ident[:])
                last.then_inc(signal, 1)

            with pe.Fori(0, B) as b:
                pe.wait_ge(y_ready, b + 1)
                transposed(pb[0], y, yT_ps)
                pe.wait_ge(yT_ready, b + 1)
                nc.tensor.matmul(pb[1][:], wq[:], yT[:], start=True, stop=True).then_inc(qk_ps, 1)
                nc.tensor.matmul(pb[2][:], wk[:], yT[:], start=True, stop=True).then_inc(qk_ps, 1)
                for t in range(T):
                    last = nc.tensor.matmul(tile(pb[3], t), tile(yT, t), wv[:], start=True, stop=True)
                last.then_inc(v_ps, 1)
                pe.wait_ge(qk_ready, b * 4 + 4)
                nc.tensor.matmul(pb[1][0:32, :], hsel[:], sqq[:], start=True, stop=True)
                nc.tensor.matmul(pb[1][32:64, :], hsel[:], sqk[:], start=True, stop=True).then_inc(dg_ps, 1)
                for t in range(T):
                    nc.tensor.matmul(pb[4 + t][:], tile(kT, t), feats[:], start=True, stop=True).then_inc(kx_ps, 1)
                pe.wait_ge(dgT_ready, b + 1)
                pe.sem_inc(passed, 1)
                for t in range(T):
                    last = nc.tensor.transpose(pb[2][:, t * 64:(t + 1) * 64], dgT[:, t * P:(t + 1) * P],
                                               ident[0:64, 0:64])
                last.then_inc(dgt_ps, 1)
                pe.wait_ge(dg_ready, b + 1)
                pe.wait_ge(v_ready, b + 1)
                for t in range(T):
                    nc.tensor.matmul(pb[t][:], tile(qT, t), feats[:], start=True, stop=True).then_inc(qx_ps, 1)
                pe.wait_ge(kp_ready, b + 1)
                for bank, left in ((pb[4], lambda t, g: v[:, t, 32 * g:32 * g + 32]), (pb[5], lambda t, g: ones[:])):
                    for t in range(T):
                        for g in range(4):
                            last = nc.tensor.matmul(bank[32 * g:32 * g + 32, 0:P], left(t, g),
                                                    kp[:, t, g * P:(g + 1) * P], start=t == 0, stop=t == T - 1)
                last.then_inc(cm_ps, 1)
                pe.wait_ge(qp_ready, b + 1)
                for g in range(4):
                    for t in range(T):
                        last = nc.tensor.transpose(tile(pb[g], t), qp[:, t, g * P:(g + 1) * P], ident[:])
                    last.then_inc(qpT_ps, 1)
                pe.wait_ge(cm_ready, b + 1)
                for k in range(2):
                    last = nc.tensor.transpose(tile(pb[4], k), cm[:, k, :], ident[:])
                last.then_inc(cx_ps, 1)
                pe.wait_ge(cx_ready, b + 1)
                pe.wait_ge(qpT_ready, b * T + T)
                for k in range(2):
                    for g in range(4):
                        last = nc.tensor.matmul(pb[6 + k][32 * g:32 * g + 32, :], cx[:, k, 32 * g:32 * g + 32],
                                                qpT[:, g, :], start=True, stop=True)
                last.then_inc(nd_ps, 1)
                pe.wait_ge(oT_ready, b + 1)
                for t in range(T):
                    last = nc.tensor.matmul(tile(pb[4], t), tile(oT, t), wo[:], start=True, stop=True)
                last.then_inc(wo_ps, 1)
                pe.wait_ge(x1_ready, b + 1)
                transposed(pb[5], x1, x1T_ps)
                pe.wait_ge(x1T_ready, b + 1)
                for c in range(FC):
                    nc.tensor.matmul(pb[c][:], tile(w1, c), x1T[:], start=True, stop=True).then_inc(h_ps, 1)
                pe.wait_ge(h_ready, b * FC + FC)
                for t in range(T):
                    for c in range(FC):
                        last = nc.tensor.matmul(tile(pb[6], t), hT[:, c, t * P:(t + 1) * P], w2[:, c, :],
                                                start=c == 0, stop=c == FC - 1)
                last.then_inc(w2_ps, 1)


GH = 4
NG = H // GH
KS = 96
KM = KS + 2
CE = D // 8


def project_qkv(nc, X, Y, V, ident, w, consts, halves, contexts, rope):
    ctx = ExitStack()
    layer = "rope_" if rope else "ctx_"
    with ctx:
        sb = lambda name, shape, dt=F32: ctx.enter_context(nc.sbuf_tensor(layer + "pr_" + name, shape, dt))
        sems = []

        def sem(name):
            sems.append(ctx.enter_context(nc.semaphore(layer + "pr_" + name)))
            return sems[-1]

        pb = [ctx.enter_context(nc.psum_tensor(f"{layer}pr_pb{i}", [P, 512], F32)) for i in range(8)]
        wq, wk, wv = (sb(n, [P, D]) for n in ("wq", "wk", "wv"))
        loads = [(wq, w["WqT"]), (wk, w["WkT"]), (wv, w["WvT"])]
        if rope:
            bq, bqs, bk, bv = sb("bq", [P, 1]), sb("bqs", [P, 1]), sb("bk", [P, 1]), sb("bv", [P, D])
            cos, sin = sb("cos", [P, T, D]), sb("sin", [P, T, D])
            loads += [(bq, w["bq"]), (bk, w["bk"]), (bv, w["bv"]), (cos, consts["rope_cos"]), (sin, consts["rope_sin"])]
            turned, rot = sb("turned", [P, T, D]), sb("rot", [P, T, D])
        else:
            we = sb("we", [P, CE])
            loads += [(we, w["WeT"])]
            cf, cs = sb("cf", [CE, S]), sb("cs", [CE, S])
            c4 = [sb(f"c4{k}", [CE, S], F32R) for k in range(4)]
        stats, mv = sb("stats", [P, T, 6]), sb("mv", [P, T, 2])
        half, rstd = sb("half", [P, T]), sb("rstd", [P, T])
        y, yT, rT = sb("y", [P, T, D]), sb("yT", [P, S]), sb("rT", [P, S])
        qf, kf = sb("qf", [P, S]), sb("kf", [P, S])
        qk4 = [sb(f"qk4{k}", [P, S], F32R) for k in range(4)]

        loaded, half_ready, bqs_ready = sem("loaded"), sem("half_ready"), sem("bqs_ready")
        var_ready, rstd_ready, y_ready, y_used = sem("var_ready"), sem("rstd_ready"), sem("y_ready"), sem("y_used")
        turn_ready, rot_ready = sem("turn_ready"), sem("rot_ready")
        yT_ps, yT_ready, q_ps, v_ps = sem("yT_ps"), sem("yT_ready"), sem("q_ps"), sem("v_ps")
        full_ready, low_ready, v_ready, stored = sem("full_ready"), sem("low_ready"), sem("v_ready"), sem("stored")
        y_kept, dve_steps = sem("y_kept"), sem("dve_steps")
        NQ = 2 if rope else 3
        NT = 2 if rope else 1
        EVAC = 4 if rope else 8
        PER = 3 * T + (0 if rope else 3)
        passed = sem("passed")
        ctx.callback(clear, nc, sems)
        block = ctx.enter_context(nc.Block())

        @block.sync
        def _(sp):
            for dst, src in loads:
                sp.dma_start(dst[:], src).then_inc(loaded, 16)
            with sp.Fori(0, B) as b:
                sp.wait_ge(low_ready, b * NQ + 2)
                sp.sem_inc(passed, 1)
                for k in range(4):
                    sp.dma_start(halves[b, k], qk4[k][:].bitcast(F32)).then_inc(stored, 16)
                if not rope:
                    sp.wait_ge(low_ready, b * NQ + 4 - 1)
                    sp.sem_inc(passed, 1)
                    for k in range(4):
                        sp.dma_start(contexts[b, k], c4[k][:].bitcast(F32)).then_inc(stored, 16)
                sp.wait_ge(stored, (b + 1) * (64 if rope else 128))
                sp.sem_inc(passed, 1)

        @block.gpsimd
        def _(pool):
            nc.gpsimd.memset(half[:], -0.5).then_inc(half_ready, 1)
            pool.wait_ge(half_ready, 1)
            with pool.Fori(0, B) as b:
                pool.wait_ge(var_ready, b + 1)
                nc.gpsimd.tensor_tensor(rstd[:], mv[:, :, 1], half[:], ALU.pow).then_inc(rstd_ready, 1)
                if rope:
                    pool.wait_ge(y_ready, b + 1)
                    pair = lambda t: t[:].rearrange("p t (k two) -> p (t k) two", two=2)
                    for m in range(2):
                        last = nc.gpsimd.tensor_tensor(pair(turned)[:, :, m], pair(y)[:, :, 1 - m],
                                                       pair(sin)[:, :, m], ALU.mult)
                    last.then_inc(turn_ready, 1)

        @block.vector
        def _(dve):
            ch = Chain(dve, dve_steps, PER, passed)
            dve.wait_ge(loaded, 16 * len(loads))
            if rope:
                nc.vector.tensor_scalar_mul(bqs[:], bq[:], SCALE).then_inc(bqs_ready, 1)

            def normalise(b):
                x = X[:, bass.ds(b * T, T), :]
                ln_stats(nc, ch, x, stats, mv).then_inc(var_ready, 1)
                dve.wait_ge(rstd_ready, b + 1)
                for t in range(T):
                    last = nc.vector.tensor_scalar(y[:, t, :], x[:, t, :], mv[:, t, 0:1], rstd[:, t:t + 1],
                                                   ALU.subtract, ALU.mult)
                    if t < T - 1:
                        ch.do(last)
                last.then_inc(y_ready, 1)
                if rope:
                    dve.wait_ge(y_ready, b + 1)
                    ch.do(nc.vector.tensor_tensor(rot[:], y[:], cos[:], ALU.mult))
                    dve.wait_ge(turn_ready, b + 1)
                    ch.sync()
                    nc.vector.tensor_tensor(rot[:], rot[:], turned[:], ALU.add).then_inc(rot_ready, 1)

            with dve.Fori(0, B) as b:
                ch.start(b)
                normalise(b)
                for k, (full, high, low) in enumerate(((qf, qk4[0], qk4[1]), (kf, qk4[2], qk4[3]))):
                    dve.wait_ge(full_ready, b * EVAC + 2 * k + 2)
                    nc.vector.tensor_tensor(low[:], full[:], high[:].bitcast(F32), ALU.subtract).then_inc(low_ready, 1)
                if not rope:
                    dve.wait_ge(full_ready, b * EVAC + 8)
                    ch.do(nc.vector.tensor_tensor(c4[1][:], cs[:], c4[0][:].bitcast(F32), ALU.subtract))
                    nc.vector.tensor_tensor(c4[3][:], cf[:], c4[2][:].bitcast(F32), ALU.subtract).then_inc(low_ready, 1)
                dve.wait_ge(v_ps, b + 1)
                for t in range(T):
                    dst, src = V[:, b * T + t, :], pb[4][:, t * P:(t + 1) * P]
                    last = nc.vector.tensor_tensor(dst, src, bv[:], ALU.add) if rope else nc.vector.tensor_copy(dst, src)
                    if not rope and t < T - 1:
                        ch.do(last)
                last.then_inc(v_ready, 1)
                dve.wait_ge(v_ready, b + 1)
                if rope:
                    dve.wait_ge(y_kept, b + 1)
                dve.wait_ge(stored, (b + 1) * (64 if rope else 128))
                ch.end()

        @block.scalar
        def _(act):
            act.wait_ge(loaded, 16 * len(loads))
            if rope:
                act.wait_ge(bqs_ready, 1)
            with act.Fori(0, B) as b:
                act.wait_ge(yT_ps, b * NT + 1)
                nc.scalar.activation(yT[:], pb[0][:], ACT.Copy).then_inc(yT_ready, 1)
                if rope:
                    act.wait_ge(yT_ps, b * NT + 2)
                    nc.scalar.activation(rT[:], pb[1][:], ACT.Copy).then_inc(yT_ready, 1)
                    nc.scalar.activation(Y[:, bass.ds(b * T, T), :], y[:], ACT.Copy).then_inc(y_kept, 1)
                act.wait_ge(q_ps, b * NQ + 1)
                for dst in (qf, qk4[0]):
                    bias = dict(bias=bqs[:]) if rope else {}
                    nc.scalar.activation(dst[:], pb[2][:], ACT.Identity, scale=SCALE, **bias).then_inc(full_ready, 1)
                act.wait_ge(q_ps, b * NQ + 2)
                for dst in (kf, qk4[2]):
                    bias = dict(bias=bk[:]) if rope else {}
                    nc.scalar.activation(dst[:], pb[3][:], ACT.Identity, **bias).then_inc(full_ready, 1)
                if not rope:
                    act.wait_ge(q_ps, b * NQ + 3)
                    for dst, scale in ((cs, 0.1), (c4[0], 0.1), (cf, 1.0), (c4[2], 1.0)):
                        nc.scalar.activation(dst[:], pb[5][0:CE, :], ACT.Copy, scale=scale).then_inc(full_ready, 1)

        @block.tensor
        def _(pe):
            pe.wait_ge(loaded, 16 * len(loads))
            with pe.Fori(0, B) as b:
                pe.wait_ge(y_ready, b + 1)
                for t in range(T):
                    last = nc.tensor.transpose(pb[0][:, t * P:(t + 1) * P], y[:, t, :], ident[:])
                last.then_inc(yT_ps, 1)
                if rope:
                    pe.wait_ge(rot_ready, b + 1)
                    for t in range(T):
                        last = nc.tensor.transpose(pb[1][:, t * P:(t + 1) * P], rot[:, t, :], ident[:])
                    last.then_inc(yT_ps, 1)
                pe.wait_ge(yT_ready, b * NT + NT)
                turned_in = rT if rope else yT
                nc.tensor.matmul(pb[2][:], wq[:], turned_in[:], start=True, stop=True).then_inc(q_ps, 1)
                nc.tensor.matmul(pb[3][:], wk[:], turned_in[:], start=True, stop=True).then_inc(q_ps, 1)
                if not rope:
                    nc.tensor.matmul(pb[5][0:CE, :], we[:], yT[:], start=True, stop=True).then_inc(q_ps, 1)
                for t in range(T):
                    last = nc.tensor.matmul(pb[4][:, t * P:(t + 1) * P], yT[:, t * P:(t + 1) * P], wv[:],
                                            start=True, stop=True)
                last.then_inc(v_ps, 1)


def attend(nc, V, ident, consts, halves, contexts, guards, outs, causal):
    ctx = ExitStack()
    layer = "rope_" if causal else "ctx_"
    with ctx:
        sb = lambda name, shape, dt=F32: ctx.enter_context(nc.sbuf_tensor(layer + "at_" + name, shape, dt))
        sems = []

        def sem(name):
            sems.append(ctx.enter_context(nc.semaphore(layer + "at_" + name)))
            return sems[-1]

        ps = lambda name, n: ctx.enter_context(nc.psum_tensor(layer + "at_" + name, [P, n], F32))
        s_bank = [ps(f"s{k}", 512) for k in range(2)]
        st_bank = [ps(f"st{k}", 1024) for k in range(2)]
        o_bank, m_bank = ps("o", 512), ps("m", 512)

        if causal:
            width = [S - P * c for c in range(T)]
            place = [(0, 0), (0, 512), (1, 0), (0, 896)]
            units, order = [1024, 256], [[0, 1, 3], [2]]
        else:
            width = [S] * T
            place = [(0, 0), (0, 512), (1, 0), (1, 512)]
            units, order = [1024, 1024], [[0, 1], [2, 3]]
        PW = sum(units)
        at = lambda c: (units[0] if place[c][0] else 0) + place[c][1]

        kst, qst = sb("kst", [KM, NG, GH, S], F32R), sb("qst", [KM, NG, GH, S], F32R)
        probs = [sb(f"probs{k}", [P, GH, PW]) for k in range(2)]
        vaug = [sb(f"vaug{k}", [P, 2, T, GH, 32]) for k in range(2)]
        nm = sb("nm", [P, T, NG, GH])
        mh, ml = sb("mh", [GH, S], F32R), sb("ml", [GH, S], F32R)
        oe = sb("oe", [P, S])
        if causal:
            maskf, maskb, maskTb, identb = sb("maskf", [P, 2, P]), sb("maskb", [P, P], BF16), sb("maskTb", [P, P], BF16), sb("identb", [P, P], BF16)

        init, masks_loaded, masks_ready = sem("init"), sem("masks_loaded"), sem("masks_ready")
        stack = [sem(f"stack_loaded{g}") for g in range(NG)]
        s_ready, s_used = sem("s_ready"), sem("s_used")
        st_ready, p_ready, pv_done = sem("st_ready"), sem("p_ready"), sem("pv_done")
        mT_ready, mh_ready, ml_ready = sem("mT_ready"), sem("mh_ready"), sem("ml_ready")
        m_stored, m_loaded = sem("m_stored"), sem("m_loaded")
        v_ready, o_ready, o_stored = sem("v_ready"), sem("o_ready"), sem("o_stored")
        NL = 6 if causal else 12
        LAST = B - 1
        passed = sem("passed")
        ctx.callback(clear, nc, sems)
        block = ctx.enter_context(nc.Block())

        def group(b, g):
            return b + g // NG, g % NG

        def within(b):
            return not isinstance(b, int) or 0 <= b < B

        def batches(eng, body):
            body(0)
            with eng.Fori(1, LAST) as b:
                body(b)
            body(LAST)

        @block.sync
        def _(sp):
            if causal:
                sp.dma_start(maskf[:, 0, :], consts["causal"]).then_inc(masks_loaded, 16)
                sp.dma_start(maskf[:, 1, :], consts["causalT"]).then_inc(masks_loaded, 16)
            sp.wait_ge(init, 6)

            def load_stacks(b, g):
                for tile, parts in ((qst, (0, 1, 0)), (kst, (2, 2, 3))):
                    for r, part in enumerate(parts):
                        src = halves[b, part, g * GH * DH:(g + 1) * GH * DH, :].rearrange("(h d) t -> d h t", d=DH)
                        sp.dma_start(tile[r * DH:(r + 1) * DH, g].bitcast(F32), src).then_inc(stack[g], 16)
                    if not causal:
                        for r, part in enumerate(parts):
                            src = contexts[b, part].unsqueeze(1).broadcast_to([CE, GH, S])
                            lo = 3 * DH + r * CE
                            sp.dma_start(tile[lo:lo + CE, g].bitcast(F32), src).then_inc(stack[g], 16)

            def guard(b, g):
                sp.wait_ge(mh_ready, b * NG + g + 1)
                sp.sem_inc(passed, 1)
                sp.wait_ge(ml_ready, b * NG + g + 1)
                sp.sem_inc(passed, 1)
                sp.dma_start(guards[g, 0], mh[:].bitcast(F32)).then_inc(m_stored, 16)
                sp.dma_start(guards[g, 1], ml[:].bitcast(F32)).then_inc(m_stored, 16)
                sp.wait_ge(m_stored, (b * NG + g + 1) * 32)
                sp.sem_inc(passed, 1)
                sp.dma_start(qst[KS:KM, g].bitcast(F32), guards[g]).then_inc(m_loaded, 16)
                sp.wait_ge(m_loaded, (b * NG + g + 1) * 16)
                sp.sem_inc(passed, 1)

            def store_out(b, hf):
                sp.wait_ge(o_ready, b * 2 + hf + 1)
                sp.sem_inc(passed, 1)
                sp.dma_start(outs[b, hf], oe[:]).then_inc(o_stored, 16)

            def body(b):
                for g in range(NG):
                    to, tg = group(b, g + 3)
                    if within(to):
                        if not (isinstance(b, int) and b * NG + g == 0):
                            sp.wait_ge(st_ready, b * NG * GH * 2 + g * GH * 2)
                            sp.sem_inc(passed, 1)
                        load_stacks(to, tg)
                    to, tg = group(b, g + 1)
                    if within(to):
                        guard(to, tg)
                    if g % 2 == 0:
                        to, tg = group(b, g - 1)
                        if within(to):
                            store_out(to, tg // 2)

            for g in range(3):
                load_stacks(0, g)
            guard(0, 0)
            batches(sp, body)
            store_out(LAST, 1)
            sp.wait_ge(o_stored, B * 2 * 16)

        @block.gpsimd
        def _(pool):
            nc.gpsimd.memset(kst[:].bitcast(F32), 0.0).then_inc(init, 1)
            for k in range(2):
                nc.gpsimd.memset(vaug[k][:], 0.0).then_inc(init, 1)
            pool.wait_ge(init, 4)
            nc.gpsimd.memset(kst[KS:KM].bitcast(F32), 1.0).then_inc(init, 1)
            pool.wait_ge(init, 5)
            for k in range(2):
                for s in range(2):
                    last = nc.gpsimd.memset(vaug[k][:, s, :, :, 9 * s + DH], 1.0)
            last.then_inc(init, 1)

            def place_values(b, hf):
                for s in range(2):
                    h0 = (2 * hf + s) * GH
                    src = V[:, bass.ds(b * T, T), h0 * DH:(h0 + GH) * DH].rearrange("p t (j d) -> p t j d", d=DH)
                    last = nc.gpsimd.tensor_copy(vaug[hf][:, s, :, :, 9 * s:9 * s + DH], src)
                last.then_inc(v_ready, 1)

            def body(b):
                for hf in range(2):
                    if not (isinstance(b, int) and b == 0):
                        pool.wait_ge(pv_done, b * NG * T - NG * T + (2 * hf + 2) * T)
                    place_values(b, hf)
            batches(pool, body)

        @block.vector
        def _(dve):
            nc.vector.memset(qst[:].bitcast(F32), 0.0).then_inc(init, 1)
            if causal:
                dve.wait_ge(masks_loaded, 32)
                nc.vector.tensor_copy(maskb[:], maskf[:, 0, :])
                nc.vector.tensor_copy(maskTb[:], maskf[:, 1, :])
                nc.vector.tensor_copy(identb[:], ident[:]).then_inc(masks_ready, 1)

            def largest(b, g, j):
                n = b * 64 + (g * GH + j) * T
                for t in range(T):
                    dve.wait_ge(s_ready, n + t + 1)
                    keys = P * (t + 1) if causal else S
                    nc.vector.tensor_reduce(nm[:, t, g, j:j + 1], s_bank[t % 2][:, 0:keys], AXX, ALU.max,
                                            negate=True).then_inc(s_used, 1)

            def low_guard(b, g):
                dve.wait_ge(mh_ready, b * NG + g + 1)
                nc.vector.tensor_tensor(ml[:], m_bank[0:GH, :], mh[:].bitcast(F32), ALU.subtract).then_inc(ml_ready, 1)

            def body(b):
                for g in range(NG):
                    for j in range(GH):
                        to, tg = group(b, g + 2)
                        if within(to):
                            largest(to, tg, j)
                        if j == 0:
                            to, tg = group(b, g + 1)
                            if within(to):
                                low_guard(to, tg)

            for j in range(GH):
                largest(0, 0, j)
            low_guard(0, 0)
            for j in range(GH):
                largest(0, 1, j)
            batches(dve, body)

        @block.scalar
        def _(act):
            def high_guard(b, g):
                act.wait_ge(mT_ready, b * NG + g + 1)
                if not (isinstance(b, int) and b * NG + g == 0):
                    act.wait_ge(m_stored, (b * NG + g) * 32)
                nc.scalar.activation(mh[:], m_bank[0:GH, :], ACT.Copy).then_inc(mh_ready, 1)

            def exponentials(b, g, j):
                for u in range(2):
                    act.wait_ge(st_ready, b * 32 + (g * GH + j) * 2 + u + 1)
                    nc.scalar.activation(probs[g % 2][:, j, u * units[0]:u * units[0] + units[u]],
                                         st_bank[u][:, 0:units[u]], ACT.Exp).then_inc(p_ready, 1)

            def keep_out(b, hf):
                act.wait_ge(pv_done, b * NG * T + (2 * hf + 2) * T)
                if not (isinstance(b, int) and b * 2 + hf == 0):
                    act.wait_ge(o_stored, (b * 2 + hf) * 16)
                nc.scalar.activation(oe[:], o_bank[:], ACT.Copy).then_inc(o_ready, 1)

            def body(b):
                for g in range(NG):
                    if not (isinstance(b, int) and b * NG + g < 2):
                        act.wait_ge(pv_done, b * NG * T + g * T - T)
                    for j in range(GH):
                        exponentials(b, g, j)
                        if j == 0:
                            to, tg = group(b, g + 1)
                            if within(to):
                                high_guard(to, tg)
                    if g % 2 == 0:
                        to, tg = group(b, g - 1)
                        if within(to):
                            keep_out(to, tg // 2)

            high_guard(0, 0)
            batches(act, body)
            keep_out(LAST, 1)

        @block.tensor
        def _(pe):
            pe.wait_ge(init, 6)
            if causal:
                pe.wait_ge(masks_ready, 1)

            def score(b, g, j, t):
                n = b * 64 + (g * GH + j) * T + t
                if not (isinstance(b, int) and b * 64 + (g * GH + j) * T + t < 2):
                    pe.wait_ge(s_used, n - 1)
                keys = P * (t + 1) if causal else S
                out = s_bank[t % 2]
                last = nc.tensor.matmul(out[:, 0:keys], qst[0:KS, g, j, t * P:(t + 1) * P], kst[0:KS, g, j, 0:keys],
                                        start=True, stop=not causal)
                if causal:
                    last = nc.tensor.matmul(out[:, keys - P:keys], identb[:], maskb[:], start=False, stop=True)
                last.then_inc(s_ready, 1)

            def scores_by_key(b, g, j, u):
                if not (isinstance(b, int) and b * NG * GH + g * GH + j == 0):
                    pe.wait_ge(p_ready, b * 32 + (g * GH + j) * 2 + u - 1)
                for c in order[u]:
                    lo = place[c][1]
                    last = nc.tensor.matmul(st_bank[u][:, lo:lo + width[c]], kst[:, g, j, c * P:(c + 1) * P],
                                            qst[:, g, j, S - width[c]:S], start=True, stop=not causal)
                    if causal:
                        last = nc.tensor.matmul(st_bank[u][:, lo:lo + P], identb[:], maskTb[:], start=False, stop=True)
                last.then_inc(st_ready, 1)

            def weigh_values(b, g, c):
                if c == 0:
                    pe.wait_ge(p_ready, b * 32 + (g + 1) * GH * 2)
                    if g % 2 == 0:
                        pe.wait_ge(v_ready, b * 2 + g // 2 + 1)
                        if not (isinstance(b, int) and b * 2 + g // 2 == 0):
                            pe.wait_ge(o_ready, b * 2 + g // 2)
                s = g % 2
                for j in range(GH):
                    last = nc.tensor.matmul(o_bank[32 * j:32 * j + 32, S - width[c]:S], vaug[g // 2][:, s, c, j, :],
                                            probs[s][:, j, at(c):at(c) + width[c]],
                                            start=s == 0 and c == 0, stop=s == 1 and c == T - 1)
                last.then_inc(pv_done, 1)

            def turn_guard(b, g):
                pe.wait_ge(s_used, b * 64 + (g + 1) * GH * T)
                if not (isinstance(b, int) and b * NG + g == 0):
                    pe.wait_ge(ml_ready, b * NG + g)
                for t in range(T):
                    last = nc.tensor.transpose(m_bank[0:GH, t * P:(t + 1) * P], nm[:, t, g, :], ident[:])
                last.then_inc(mT_ready, 1)

            def body(b):
                for g in range(NG):
                    for j in range(GH):
                        ahead, behind, nxt = group(b, g + 2), group(b, g - 1), group(b, g + 1)
                        if j == 0:
                            pe.wait_ge(m_loaded, (b * NG + g + 1) * 16)
                            if within(ahead[0]):
                                pe.wait_ge(stack[ahead[1]], (ahead[0] + 1) * NL * 16)
                        for u in range(2):
                            if within(ahead[0]):
                                score(*ahead, j, 2 * u)
                            scores_by_key(b, g, j, u)
                            if within(ahead[0]):
                                score(*ahead, j, 2 * u + 1)
                            if u == 0 and within(behind[0]):
                                weigh_values(*behind, j)
                        if j == 0 and within(nxt[0]):
                            turn_guard(*nxt)

            for g in range(2):
                pe.wait_ge(stack[g], NL * 16)
                for j in range(GH):
                    for t in range(T):
                        score(0, g, j, t)
                if g == 0:
                    turn_guard(0, 0)
            batches(pe, body)
            for c in range(T):
                weigh_values(LAST, NG - 1, c)


def attention_out(nc, X, Y, ident, w, outs, rope):
    ctx = ExitStack()
    layer = "rope_" if rope else "ctx_"
    with ctx:
        sb = lambda name, shape, dt=F32: ctx.enter_context(nc.sbuf_tensor(layer + "ao_" + name, shape, dt))
        sems = []

        def sem(name):
            sems.append(ctx.enter_context(nc.semaphore(layer + "ao_" + name)))
            return sems[-1]

        pb = [ctx.enter_context(nc.psum_tensor(f"{layer}ao_pb{i}", [P, 512], F32)) for i in range(4)]
        wo = sb("wo", [P, D])
        loads = [(wo, w["WoT"])]
        if rope:
            bo, gain, shift = sb("bo", [P, D]), sb("gain", [P, D]), sb("shift", [P, D])
            loads += [(bo, w["out_proj_b"]), (gain, w["ln1_w"]), (shift, w["ln1_b"])]
        oe = [sb(f"oe{k}", [P, 2, S]) for k in range(1)]
        rc, o, oT = sb("rc", [P, 2, 2, T, GH]), sb("o", [P, T, D]), sb("oT", [P, S])
        r, z = sb("r", [P, T, D]), sb("z", [P, T, D])
        stats, mv = sb("stats", [P, T, 6]), sb("mv", [P, T, 2])
        half, rstd = sb("half", [P, T]), sb("rstd", [P, T])
        loaded, half_ready, in_ready = sem("loaded"), sem("half_ready"), sem("in_ready")
        turned, o_ready, oT_ps, oT_ready, wo_ps = sem("turned"), sem("o_ready"), sem("oT_ps"), sem("oT_ready"), sem("wo_ps")
        var_ready, rstd_ready, dve_steps, x_ready = sem("var_ready"), sem("rstd_ready"), sem("dve_steps"), sem("x_ready")
        PER = 4 + 3 + 3 * T + (3 if rope else 1)
        passed = sem("passed")
        ctx.callback(clear, nc, sems)
        block = ctx.enter_context(nc.Block())

        @block.sync
        def _(sp):
            for dst, src in loads:
                sp.dma_start(dst[:], src).then_inc(loaded, 16)
            sp.dma_start(oe[0][:], outs[0].rearrange("k p s -> p k s")).then_inc(in_ready, 16)
            with sp.Fori(1, B) as b:
                sp.wait_ge(turned, b * 2)
                sp.sem_inc(passed, 1)
                sp.dma_start(oe[0][:], outs[b].rearrange("k p s -> p k s")).then_inc(in_ready, 16)
            sp.wait_ge(x_ready, B)

        @block.gpsimd
        def _(pool):
            nc.gpsimd.memset(half[:], -0.5).then_inc(half_ready, 1)
            pool.wait_ge(half_ready, 1)
            with pool.Fori(0, B) as b:
                pool.wait_ge(var_ready, b + 1)
                nc.gpsimd.tensor_tensor(rstd[:], mv[:, :, 1], half[:], ALU.pow).then_inc(rstd_ready, 1)

        @block.tensor
        def _(pe):
            pe.wait_ge(loaded, 16 * len(loads))
            with pe.Fori(0, B) as b:
                pe.wait_ge(in_ready, b * 16 + 16)
                for hf in range(2):
                    for t in range(T):
                        last = nc.tensor.transpose(pb[hf][:, t * P:(t + 1) * P], oe[0][:, hf, t * P:(t + 1) * P], ident[:])
                    last.then_inc(turned, 1)
                pe.wait_ge(o_ready, b + 1)
                for t in range(T):
                    last = nc.tensor.transpose(pb[2][:, t * P:(t + 1) * P], o[:, t, :], ident[:])
                last.then_inc(oT_ps, 1)
                pe.wait_ge(oT_ready, b + 1)
                for t in range(T):
                    last = nc.tensor.matmul(pb[3][:, t * P:(t + 1) * P], oT[:, t * P:(t + 1) * P], wo[:],
                                            start=True, stop=True)
                last.then_inc(wo_ps, 1)

        @block.scalar
        def _(act):
            with act.Fori(0, B) as b:
                act.wait_ge(oT_ps, b + 1)
                nc.scalar.activation(oT[:], pb[2][:], ACT.Copy).then_inc(oT_ready, 1)

        @block.vector
        def _(dve):
            ch = Chain(dve, dve_steps, PER, passed)
            dve.wait_ge(loaded, 16 * len(loads))
            with dve.Fori(0, B) as b:
                ch.start(b)
                x = X[:, bass.ds(b * T, T), :]
                for hf in range(2):
                    dve.wait_ge(turned, b * 2 + hf + 1)
                    rows = pb[hf][:].rearrange("p (t j k) -> p t j k", t=T, k=32)
                    for s in range(2):
                        ch.do(nc.vector.reciprocal(rc[:, hf, s], rows[:, :, :, 9 * s + DH]))
                ch.sync()
                for hf in range(2):
                    rows = pb[hf][:].rearrange("p (t j k) -> p t j k", t=T, k=32)
                    for s in range(2):
                        h0 = (2 * hf + s) * GH
                        dst = o[:, :, h0 * DH:(h0 + GH) * DH].rearrange("p t (j d) -> p t j d", d=DH)
                        last = nc.vector.tensor_tensor(dst, rows[:, :, :, 9 * s:9 * s + DH], each(rc[:, hf, s], DH), ALU.mult)
                        if hf * 2 + s < 3:
                            ch.do(last)
                last.then_inc(o_ready, 1)
                dve.wait_ge(wo_ps, b + 1)
                src = pb[3][:].rearrange("p (t d) -> p t d", t=T)
                if rope:
                    ch.do(nc.vector.tensor_tensor(r[:], src, Y[:, bass.ds(b * T, T), :], ALU.add))
                    ch.sync()
                    ch.do(nc.vector.tensor_tensor(r[:], r[:], bc(bo[:], T), ALU.add))
                    ch.sync()
                    src = r
                ln_stats(nc, ch, src, stats, mv).then_inc(var_ready, 1)
                dve.wait_ge(rstd_ready, b + 1)
                ln_apply(nc, ch, z, src, mv, rstd)
                ch.sync()
                if rope:
                    ch.do(nc.vector.tensor_tensor(z[:], z[:], bc(gain[:], T), ALU.mult))
                    ch.sync()
                    last = nc.vector.tensor_tensor(Y[:, bass.ds(b * T, T), :], z[:], bc(shift[:], T), ALU.add)
                else:
                    ch.do(nc.vector.tensor_copy(r[:], z[:]))
                    ch.sync()
                    last = nc.vector.tensor_tensor(x, x, r[:], ALU.add)
                last.then_inc(x_ready, 1)
                dve.wait_ge(x_ready, b + 1)
                ch.end()


def attention_layer(nc, X, Y, ident, w, consts, rope):
    name = "rope" if rope else "ctx"
    halves = nc.dram_tensor(name + "_halves", [B, 4, P, S], F32, kind="Internal").ap()
    contexts = None if rope else nc.dram_tensor(name + "_contexts", [B, 4, CE, S], F32, kind="Internal").ap()
    guards = nc.dram_tensor(name + "_guards", [NG, 2, GH, S], F32, kind="Internal").ap()
    outs = nc.dram_tensor(name + "_outs", [B, 2, P, S], F32, kind="Internal").ap()
    with nc.sbuf_tensor(name + "_V", [P, B * T, D], F32) as V:
        project_qkv(nc, X, Y, V, ident, w, consts, halves, contexts, rope)
        attend(nc, V, ident, consts, halves, contexts, guards, outs, rope)
    attention_out(nc, X, Y, ident, w, outs, rope)


def route(nc, ch, probs, order, tmp, red, hot, gates):
    each8 = lambda ap: each(ap, NE)
    for k in range(2):
        ch.do(nc.vector.tensor_reduce(red[:, :, 0], probs[:] if k == 0 else tmp[:], AXX, ALU.max))
        ch.sync()
        ch.do(nc.vector.tensor_tensor(hot[:, k], probs[:] if k == 0 else tmp[:], each8(red[:, :, 0]), ALU.is_equal))
        ch.sync()
        ch.do(nc.vector.tensor_tensor(hot[:, k], hot[:, k], bc(order[:], T), ALU.mult))
        ch.sync()
        ch.do(nc.vector.tensor_reduce(red[:, :, 1], hot[:, k], AXX, ALU.max))
        ch.sync()
        ch.do(nc.vector.tensor_tensor(hot[:, k], hot[:, k], each8(red[:, :, 1]), ALU.is_equal))
        ch.sync()
        if k == 0:
            ch.do(nc.vector.scalar_tensor_tensor(tmp[:], hot[:, 0], -2.0, probs[:], ALU.mult, ALU.add))
            ch.sync()
    ch.do(nc.vector.tensor_tensor(hot[:, 0], hot[:, 0], hot[:, 1], ALU.add))
    ch.sync()
    return nc.vector.tensor_tensor(gates[:], hot[:, 0], probs[:], ALU.mult)


ROUTE_STEPS = 12


def mixture_layer(nc, X, Y, ident, w, consts):
    ctx = ExitStack()
    with ctx:
        sb = lambda name, shape, dt=F32: ctx.enter_context(nc.sbuf_tensor("mo_" + name, shape, dt))
        sems = []

        def sem(name):
            sems.append(ctx.enter_context(nc.semaphore("mo_" + name)))
            return sems[-1]

        pb = [ctx.enter_context(nc.psum_tensor(f"mo_pb{i}", [P, 1024], F32)) for i in range(3)]
        small, y_bank = (ctx.enter_context(nc.psum_tensor(f"mo_{n}", [P, 512], F32)) for n in ("small", "y_bank"))
        gw, gb, we, eb, order = sb("gw", [P, NE]), sb("gb", [P, NE]), sb("we", [P, NE * D]), sb("eb", [NE, D]), sb("order", [P, NE])
        gain, shift = sb("gain", [P, D]), sb("shift", [P, D])
        loads = [(gw, w["gateT"]), (gb, w["gate_b"]), (we, w["expertT"]), (eb, w["expert_b"]), (order, consts["order"]),
                 (gain, w["ln2_w"]), (shift, w["ln2_b"])]
        y, yT = sb("y", [P, T, D]), sb("yT", [P, S])
        lg, tmp, gates = (sb(n, [P, T, NE]) for n in ("lg", "tmp", "gates"))
        hot, red = sb("hot", [P, 2, T, NE]), sb("red", [P, T, 2])
        gT = sb("gT", [NE, S])
        acc, z = sb("acc", [P, T, D]), sb("z", [P, T, D])
        stats, mv = sb("stats", [P, T, 6]), sb("mv", [P, T, 2])
        half, rstd = sb("half", [P, T]), sb("rstd", [P, T])
        loaded, half_ready, y_ready = sem("loaded"), sem("half_ready"), sem("y_ready")
        yT_ps, yT_ready, gate_ps, lg_ready, e_ready = sem("yT_ps"), sem("yT_ready"), sem("gate_ps"), sem("lg_ready"), sem("e_ready")
        gates_ready, gT_ps, gT_ready, bias_ps = sem("gates_ready"), sem("gT_ps"), sem("gT_ready"), sem("bias_ps")
        ex_ps, ex_used = sem("ex_ps"), sem("ex_used")
        var_ready, rstd_ready, dve_steps = sem("var_ready"), sem("rstd_ready"), sem("dve_steps")
        PER = 5 + ROUTE_STEPS + 1 + T * (NE - 1) + 2 * 3 * T + 3
        passed = sem("passed")
        ctx.callback(clear, nc, sems)
        block = ctx.enter_context(nc.Block())

        @block.sync
        def _(sp):
            for dst, src in loads:
                sp.dma_start(dst[:], src).then_inc(loaded, 16)

        @block.gpsimd
        def _(pool):
            nc.gpsimd.memset(half[:], -0.5).then_inc(half_ready, 1)
            pool.wait_ge(half_ready, 1)
            with pool.Fori(0, B) as b:
                for k in range(2):
                    pool.wait_ge(var_ready, b * 2 + k + 1)
                    nc.gpsimd.tensor_tensor(rstd[:], mv[:, :, 1], half[:], ALU.pow).then_inc(rstd_ready, 1)

        @block.vector
        def _(dve):
            ch = Chain(dve, dve_steps, PER, passed)
            dve.wait_ge(loaded, 16 * len(loads))
            with dve.Fori(0, B) as b:
                ch.start(b)
                x = X[:, bass.ds(b * T, T), :]
                nc.vector.tensor_copy(y[:], Y[:, bass.ds(b * T, T), :]).then_inc(y_ready, 1)
                dve.wait_ge(gate_ps, b + 1)
                ch.do(nc.vector.tensor_tensor(lg[:], small[:, 0:T * NE].rearrange("p (t e) -> p t e", e=NE), bc(gb[:], T), ALU.add))
                ch.sync()
                ch.do(nc.vector.tensor_reduce(red[:, :, 0], lg[:], AXX, ALU.max))
                ch.sync()
                nc.vector.tensor_tensor(lg[:], lg[:], each(red[:, :, 0], NE), ALU.subtract).then_inc(lg_ready, 1)
                dve.wait_ge(e_ready, b + 1)
                ch.do(nc.vector.tensor_reduce(red[:, :, 1], lg[:], AXX, ALU.add))
                ch.sync()
                ch.do(nc.vector.reciprocal(red[:, :, 0], red[:, :, 1]))
                ch.sync()
                ch.do(nc.vector.tensor_tensor(lg[:], lg[:], each(red[:, :, 0], NE), ALU.mult))
                ch.sync()
                route(nc, ch, lg, order, tmp, red, hot, gates).then_inc(gates_ready, 1)
                dve.wait_ge(gates_ready, b + 1)
                dve.wait_ge(bias_ps, b + 1)
                ch.do(nc.vector.tensor_tensor(acc[:], y_bank[:].rearrange("p (t d) -> p t d", t=T), y[:], ALU.add))
                for t in range(T):
                    dve.wait_ge(ex_ps, b * T + t + 1)
                    for e in range(NE):
                        ch.sync()
                        last = nc.vector.scalar_tensor_tensor(acc[:, t, :], pb[t % 3][:, e * D:(e + 1) * D], gates[:, t, e:e + 1],
                                                              acc[:, t, :], ALU.mult, ALU.add)
                        if e < NE - 1:
                            ch.do(last)
                    last.then_inc(ex_used, 1)
                dve.wait_ge(ex_used, b * T + T)

                def layer_norm(k, dst, src):
                    ln_stats(nc, ch, src, stats, mv).then_inc(var_ready, 1)
                    dve.wait_ge(rstd_ready, b * 2 + k + 1)
                    ln_apply(nc, ch, dst, src, mv, rstd)
                    ch.sync()
                layer_norm(0, z, acc)
                ch.do(nc.vector.tensor_tensor(z[:], z[:], bc(gain[:], T), ALU.mult))
                ch.sync()
                ch.do(nc.vector.tensor_tensor(z[:], z[:], bc(shift[:], T), ALU.add))
                ch.sync()
                layer_norm(1, acc, z)
                ch.do(nc.vector.tensor_tensor(x, x, acc[:], ALU.add))
                ch.sync()
                ch.end()

        @block.scalar
        def _(act):
            with act.Fori(0, B) as b:
                act.wait_ge(yT_ps, b + 1)
                nc.scalar.activation(yT[:], y_bank[:], ACT.Copy).then_inc(yT_ready, 1)
                act.wait_ge(lg_ready, b + 1)
                nc.scalar.activation(lg[:], lg[:], ACT.Exp).then_inc(e_ready, 1)
                act.wait_ge(gT_ps, b + 1)
                nc.scalar.activation(gT[:], small[0:NE, :], ACT.Copy).then_inc(gT_ready, 1)

        @block.tensor
        def _(pe):
            pe.wait_ge(loaded, 16 * len(loads))
            with pe.Fori(0, B) as b:
                pe.wait_ge(y_ready, b + 1)
                for t in range(T):
                    last = nc.tensor.transpose(y_bank[:, t * P:(t + 1) * P], y[:, t, :], ident[:])
                last.then_inc(yT_ps, 1)
                pe.wait_ge(yT_ready, b + 1)
                for t in range(T):
                    last = nc.tensor.matmul(small[:, t * NE:(t + 1) * NE], yT[:, t * P:(t + 1) * P], gw[:], start=True, stop=True)
                last.then_inc(gate_ps, 1)

                def experts(t):
                    for k in range(2):
                        last = nc.tensor.matmul(pb[t % 3][:, k * 512:(k + 1) * 512], yT[:, t * P:(t + 1) * P],
                                                we[:, k * 512:(k + 1) * 512], start=True, stop=True)
                    last.then_inc(ex_ps, 1)
                for t in range(3):
                    experts(t)
                pe.wait_ge(gates_ready, b + 1)
                for t in range(T):
                    last = nc.tensor.transpose(small[0:NE, t * P:(t + 1) * P], gates[:, t, :], ident[:])
                last.then_inc(gT_ps, 1)
                pe.wait_ge(gT_ready, b + 1)
                for t in range(T):
                    last = nc.tensor.matmul(y_bank[:, t * P:(t + 1) * P], gT[:, t * P:(t + 1) * P], eb[:], start=True, stop=True)
                last.then_inc(bias_ps, 1)
                pe.wait_ge(ex_used, b * T + 1)
                experts(3)


def swiglu_layer(nc, X, ident, w, consts):
    ctx = ExitStack()
    with ctx:
        sb = lambda name, shape, dt=F32: ctx.enter_context(nc.sbuf_tensor("sw_" + name, shape, dt))
        sems = []

        def sem(name):
            sems.append(ctx.enter_context(nc.semaphore("sw_" + name)))
            return sems[-1]

        g_bank = [ctx.enter_context(nc.psum_tensor(f"sw_g{i}", [P, 512], F32)) for i in range(2)]
        u_bank = [ctx.enter_context(nc.psum_tensor(f"sw_u{i}", [P, 512], F32)) for i in range(2)]
        d_bank = [ctx.enter_context(nc.psum_tensor(f"sw_d{i}", [P, 512], F32)) for i in range(2)]
        small, y_bank = (ctx.enter_context(nc.psum_tensor(f"sw_{n}", [P, 512], F32)) for n in ("small", "y_bank"))
        N = NE + 1
        stage = [sb(f"stage{k}", [P, 3, 512]) for k in range(2)]
        high, low = sb("high", [P, N, 3, 512], F32R), sb("low", [P, N, 3, 512], F32R)
        gw, order = sb("gw", [P, NE]), sb("order", [P, NE])
        y, yf = sb("y", [P, T, D]), sb("yf", [P, S])
        yh, yl = sb("yh", [P, S], F32R), sb("yl", [P, S], F32R)
        lg, tmp = sb("lg", [P, T, NE]), sb("tmp", [P, T, NE])
        gates, routed = sb("gates", [P, T, N]), sb("routed", [P, T, NE])
        hot, red = sb("hot", [P, 2, T, NE]), sb("red", [P, T, 2])
        silu = [sb(f"silu{k}", [P, S]) for k in range(2)]
        hf = [sb(f"hf{k}", [P, S]) for k in range(2)]
        hh = [sb(f"hh{k}", [P, S], F32R) for k in range(2)]
        hl = [sb(f"hl{k}", [P, S], F32R) for k in range(2)]
        dT = sb("dT", [P, S])
        acc = sb("acc", [P, T, D])
        stats, mv = sb("stats", [P, T, 6]), sb("mv", [P, T, 2])
        half, rstd = sb("half", [P, T]), sb("rstd", [P, T])

        staged = [sem(f"staged{k}") for k in range(2)]
        loaded, cut, half_ready = sem("loaded"), sem("cut"), sem("half_ready")
        y_ready, yT_ps, yf_ready, yh_ready, yl_ready = sem("y_ready"), sem("yT_ps"), sem("yf_ready"), sem("yh_ready"), sem("yl_ready")
        gate_ps, lg_ready, e_ready, gates_ready = sem("gate_ps"), sem("lg_ready"), sem("e_ready"), sem("gates_ready")
        g_ps, u_ps, silu_ready, h_ready = sem("g_ps"), sem("u_ps"), sem("silu_ready"), sem("h_ready")
        hh_ready, hl_ready, d_used = sem("hh_ready"), sem("hl_ready"), sem("d_used")
        dT_ready, dt_ps, added = sem("dT_ready"), sem("dt_ps"), sem("added")
        var_ready, rstd_ready, dve_steps = sem("var_ready"), sem("rstd_ready"), sem("dve_steps")
        PER = 2 * 3 * T - 1 + 5 + ROUTE_STEPS + 1 + N * (T - 1) + 2
        passed = sem("passed")
        ctx.callback(clear, nc, sems)
        block = ctx.enter_context(nc.Block())

        @block.sync
        def _(sp):
            sp.dma_start(gw[:], w["gateT"]).then_inc(loaded, 16)
            sp.dma_start(order[:], consts["order"]).then_inc(loaded, 16)
            for e in range(N):
                if e >= 2:
                    sp.wait_ge(cut, 2 * (e - 1))
                sp.dma_start(stage[e % 2][:, 0, :], w["w1"][e]).then_inc(staged[e % 2], 16)
                sp.dma_start(stage[e % 2][:, 1, :], w["w3"][e]).then_inc(staged[e % 2], 16)
                sp.dma_start(stage[e % 2][:, 2, :], w["w2"][e].rearrange("p c d -> p (c d)")).then_inc(staged[e % 2], 16)

        @block.gpsimd
        def _(pool):
            nc.gpsimd.memset(half[:], -0.5).then_inc(half_ready, 1)
            nc.gpsimd.memset(gates[:, :, NE:N], 1.0 / NE).then_inc(half_ready, 1)
            pool.wait_ge(half_ready, 2)
            with pool.Fori(0, B) as b:
                pool.wait_ge(var_ready, b * 2 + 1)
                nc.gpsimd.tensor_tensor(rstd[:], mv[:, :, 1], half[:], ALU.pow).then_inc(rstd_ready, 1)
                for n in range(N * FC):
                    k = n % 2
                    pool.wait_ge(hh_ready, b * N * FC + n + 1)
                    nc.gpsimd.tensor_tensor(hl[k][:], hf[k][:], hh[k][:].bitcast(F32), ALU.subtract).then_inc(hl_ready, 1)
                pool.wait_ge(var_ready, b * 2 + 2)
                nc.gpsimd.tensor_tensor(rstd[:], mv[:, :, 1], half[:], ALU.pow).then_inc(rstd_ready, 1)

        @block.vector
        def _(dve):
            ch = Chain(dve, dve_steps, PER, passed)
            dve.wait_ge(loaded, 32)
            for e in range(N):
                dve.wait_ge(staged[e % 2], 48 * (e // 2 + 1))
                nc.vector.tensor_copy(high[:, e], stage[e % 2][:]).then_inc(cut, 1)
                dve.wait_ge(cut, 2 * e + 1)
                nc.vector.tensor_tensor(low[:, e], stage[e % 2][:], high[:, e].bitcast(F32), ALU.subtract).then_inc(cut, 1)
            dve.wait_ge(cut, 2 * N)
            dve.wait_ge(half_ready, 2)
            with dve.Fori(0, B) as b:
                ch.start(b)
                x = X[:, bass.ds(b * T, T), :]

                def layer_norm(k, dst, src, signal=None):
                    ln_stats(nc, ch, src, stats, mv).then_inc(var_ready, 1)
                    dve.wait_ge(rstd_ready, b * 2 + k + 1)
                    for t in range(T):
                        last = nc.vector.tensor_scalar(dst[:, t, :], src[:, t, :], mv[:, t, 0:1], rstd[:, t:t + 1],
                                                       ALU.subtract, ALU.mult)
                        if signal is None or t < T - 1:
                            ch.do(last)
                    if signal is not None:
                        last.then_inc(signal, 1)
                layer_norm(0, y, x, y_ready)
                dve.wait_ge(yf_ready, b + 1)
                nc.vector.tensor_tensor(yl[:], yf[:], yh[:].bitcast(F32), ALU.subtract).then_inc(yl_ready, 1)
                dve.wait_ge(gate_ps, b + 1)
                ch.do(nc.vector.tensor_copy(lg[:], small[:, 0:T * NE].rearrange("p (t e) -> p t e", e=NE)))
                ch.sync()
                ch.do(nc.vector.tensor_reduce(red[:, :, 0], lg[:], AXX, ALU.max))
                ch.sync()
                nc.vector.tensor_tensor(lg[:], lg[:], each(red[:, :, 0], NE), ALU.subtract).then_inc(lg_ready, 1)
                dve.wait_ge(e_ready, b + 1)
                ch.do(nc.vector.tensor_reduce(red[:, :, 1], lg[:], AXX, ALU.add))
                ch.sync()
                ch.do(nc.vector.reciprocal(red[:, :, 0], red[:, :, 1]))
                ch.sync()
                ch.do(nc.vector.tensor_tensor(lg[:], lg[:], each(red[:, :, 0], NE), ALU.mult))
                ch.sync()
                route(nc, ch, lg, order, tmp, red, hot, routed).then_inc(gates_ready, 1)
                dve.wait_ge(gates_ready, b + 1)
                ch.do(nc.vector.tensor_copy(gates[:, :, 0:NE], routed[:]))

                def gated(e, c):
                    n = e * FC + c
                    dve.wait_ge(silu_ready, b * N * FC + n + 1)
                    dve.wait_ge(u_ps, b * N * FC + n + 1)
                    if n >= 2:
                        dve.wait_ge(hl_ready, b * N * FC + n - 1)
                    nc.vector.tensor_tensor(hf[n % 2][:], silu[n % 2][:], u_bank[n % 2][:], ALU.mult).then_inc(h_ready, 1)

                def add(e):
                    dve.wait_ge(dt_ps, b * N + e + 1)
                    ch.sync()
                    if e:
                        dve.wait_ge(added, b * N + e)
                    for t in range(T):
                        src = small[:, t * P:(t + 1) * P]
                        if e == 0:
                            last = nc.vector.tensor_scalar(acc[:, t, :], src, gates[:, t, 0:1], None, ALU.mult)
                        else:
                            last = nc.vector.scalar_tensor_tensor(acc[:, t, :], src, gates[:, t, e:e + 1], acc[:, t, :],
                                                                  ALU.mult, ALU.add)
                        if t < T - 1:
                            ch.do(last)
                    last.then_inc(added, 1)

                for e in range(N):
                    for c in range(FC):
                        gated(e, c)
                        if c == 2 and e:
                            add(e - 1)
                add(N - 1)
                dve.wait_ge(added, b * N + N)
                ch.do(nc.vector.tensor_scalar_mul(acc[:], acc[:], 0.5))
                ch.sync()
                layer_norm(1, y, acc)
                ch.sync()
                ch.do(nc.vector.tensor_tensor(x, x, y[:], ALU.add))
                ch.sync()
                ch.end()

        @block.scalar
        def _(act):
            with act.Fori(0, B) as b:
                act.wait_ge(yT_ps, b + 1)
                nc.scalar.activation(yf[:], y_bank[:], ACT.Copy).then_inc(yh_ready, 1)
                nc.scalar.activation(yh[:], y_bank[:], ACT.Copy).then_inc(yf_ready, 1)
                act.wait_ge(lg_ready, b + 1)
                nc.scalar.activation(lg[:], lg[:], ACT.Exp).then_inc(e_ready, 1)

                def high_half(n):
                    act.wait_ge(h_ready, b * N * FC + n + 1)
                    if n >= 2:
                        act.wait_ge(d_used, b * N * FC + n - 1)
                    nc.scalar.activation(hh[n % 2][:], hf[n % 2][:], ACT.Copy).then_inc(hh_ready, 1)

                def fetch(e):
                    act.wait_ge(d_used, b * N * FC + (e + 1) * FC)
                    if e:
                        act.wait_ge(dt_ps, b * N + e)
                    nc.scalar.activation(dT[:], d_bank[e % 2][:], ACT.Copy).then_inc(dT_ready, 1)

                for n in range(N * FC):
                    act.wait_ge(g_ps, b * N * FC + n + 1)
                    if n >= 2:
                        act.wait_ge(h_ready, b * N * FC + n - 1)
                    nc.scalar.activation(silu[n % 2][:], g_bank[n % 2][:], ACT.Silu).then_inc(silu_ready, 1)
                    if n:
                        high_half(n - 1)
                    if n % FC == 1 and n > FC:
                        fetch(n // FC - 1)
                high_half(N * FC - 1)
                fetch(N - 1)

        @block.tensor
        def _(pe):
            pe.wait_ge(loaded, 32)
            both = lambda e, k, c: [h[:, e, k, c * P:(c + 1) * P] for h in (high, low)]
            with pe.Fori(0, B) as b:
                pe.wait_ge(y_ready, b + 1)
                for t in range(T):
                    last = nc.tensor.transpose(y_bank[:, t * P:(t + 1) * P], y[:, t, :], ident[:])
                last.then_inc(yT_ps, 1)
                pe.wait_ge(yh_ready, b + 1)
                for t in range(T):
                    last = nc.tensor.matmul(small[:, t * NE:(t + 1) * NE], yf[:, t * P:(t + 1) * P], gw[:], start=True, stop=True)
                last.then_inc(gate_ps, 1)
                pe.wait_ge(yl_ready, b + 1)

                def up(n):
                    e, c = n // FC, n % FC
                    pe.wait_ge(cut, 2 * (e + 1))
                    if n >= 2:
                        pe.wait_ge(silu_ready, b * N * FC + n - 1)
                        pe.wait_ge(h_ready, b * N * FC + n - 1)
                    mm3(nc, g_bank[n % 2][:], both(e, 0, c), (yh[:], yl[:])).then_inc(g_ps, 1)
                    mm3(nc, u_bank[n % 2][:], both(e, 1, c), (yh[:], yl[:])).then_inc(u_ps, 1)

                def down(n):
                    e, c = n // FC, n % FC
                    pe.wait_ge(hl_ready, b * N * FC + n + 1)
                    if c == 0 and e >= 2:
                        pe.wait_ge(dT_ready, b * N + e - 1)
                    last = mm3(nc, d_bank[e % 2][:], both(e, 2, c), (hh[n % 2][:], hl[n % 2][:]), start=c == 0, stop=c == FC - 1)
                    last.then_inc(d_used, 1)

                def turn(e):
                    pe.wait_ge(dT_ready, b * N + e + 1)
                    if e:
                        pe.wait_ge(added, b * N + e)
                    else:
                        pe.wait_ge(lg_ready, b + 1)
                    for t in range(T):
                        last = nc.tensor.transpose(small[:, t * P:(t + 1) * P], dT[:, t * P:(t + 1) * P], ident[:])
                    last.then_inc(dt_ps, 1)

                for n in range(N * FC + 2):
                    if n < N * FC:
                        up(n)
                    if n >= 2:
                        down(n - 2)
                    if n % FC == 3 and n > FC:
                        turn(n // FC - 1)
                turn(N - 1)


def build(nc, dram, out):
    ctx = ExitStack()
    with ctx:
        X = ctx.enter_context(nc.sbuf_tensor("X", [P, B * T, D], F32))
        ident = ctx.enter_context(nc.sbuf_tensor("ident", [P, P], F32))
        x_loaded = ctx.enter_context(nc.semaphore("x_loaded"))
        x_stored = ctx.enter_context(nc.semaphore("x_stored"))
        x_dram = dram["video"].rearrange("b (t p) d -> p (b t) d", p=P)
        with nc.Block() as block:
            @block.sync
            def _(sp):
                sp.dma_start(ident[:], dram["ident"]).then_inc(x_loaded, 16)
                sp.dma_start(X[:], x_dram).then_inc(x_loaded, 16)
                sp.wait_ge(x_loaded, 32)

        w = lambda prefix: {k[len(prefix):]: v for k, v in dram.items() if k.startswith(prefix)}
        performer_layer(nc, X, ident, w("L0_attn_"), dram)
        with nc.sbuf_tensor("Y", [P, B * T, D], F32) as Y:
            attention_layer(nc, X, Y, ident, w("L0_ffn_"), dram, True)
            mixture_layer(nc, X, Y, ident, w("L0_ffn_"), dram)
        attention_layer(nc, X, None, ident, w("L1_attn_"), dram, False)
        swiglu_layer(nc, X, ident, w("L1_ffn_"), dram)
        with nc.Block() as block:
            @block.sync
            def _(sp):
                sp.dma_start(out.rearrange("b (t p) d -> p (b t) d", p=P), X[:]).then_inc(x_stored, 16)
                sp.wait_ge(x_stored, 16)



def layouts(i):
    import numpy as np
    i = {k: np.asarray(v) for k, v in i.items()}
    con = np.ascontiguousarray
    rows = lambda a: con(np.broadcast_to(a.reshape(1, -1), (P, a.size)))
    col = lambda a: con(a.reshape(-1, P).T)
    chunks = lambda a: con(a.reshape(-1, P, a.shape[-1]).transpose(1, 0, 2))
    d = {"video": i["L0_attn_video"]}
    p = "L0_attn_"
    for n in ("Wq", "Wk", "Wv", "Wo", "W1"):
        d[p + n + "T"] = con(i[p + n].T)
    d[p + "W2T"] = chunks(i[p + "W2"].T)
    d[p + "projT"] = con(i[p + "proj"].T)
    for n in ("bq", "bk", "b1"):
        d[p + n] = col(i[p + n])
    for n in ("bv", "bo", "b2", "g2", "be2", "g3", "be3"):
        d[p + n] = rows(i[p + n])
    p = "L0_ffn_"
    for n, k in (("q", 0), ("k", 1), ("v", 2)):
        d[p + "W" + n + "T"] = con(i[p + "in_proj_w"][k * D:(k + 1) * D].T)
        d[p + "b" + n] = (rows if n == "v" else col)(i[p + "in_proj_b"][k * D:(k + 1) * D])
    d[p + "WoT"] = con(i[p + "out_proj_w"].T)
    d[p + "gateT"] = con(i[p + "gate_w"].T)
    d[p + "expertT"] = con(i[p + "expert_w"].transpose(2, 0, 1)).reshape(D, NE * D)
    d[p + "expert_b"] = i[p + "expert_b"]
    for n in ("out_proj_b", "gate_b", "ln1_w", "ln1_b", "ln2_w", "ln2_b"):
        d[p + n] = rows(i[p + n])
    p = "L1_attn_"
    for n in ("Wq", "Wk", "Wv", "Wo", "We"):
        d[p + n + "T"] = con(i[p + n].T)
    p = "L1_ffn_"
    d[p + "gateT"] = con(i[p + "gate_W"].T)
    for n in ("w1", "w3"):
        d[p + n] = con(np.concatenate([i[p + n + "_e"], i[p + n + "_s"].transpose(1, 0, 2).reshape(1, D, F)]))
    d[p + "w2"] = con(np.concatenate([i[p + "w2_e"], i[p + "w2_s"].reshape(1, F, D)])
                      .reshape(NE + 1, FC, P, D).transpose(0, 2, 1, 3))
    f = np.float32
    r = np.arange(P)
    d["ident"] = np.eye(P, dtype=f)
    d["hsel"] = (r[:, None] // DH == np.arange(32)[None]).astype(f)
    d["bmask"] = ((r[:, None] % 32) // DH == r[None] // M).astype(f)
    d["causal"] = np.where(r[None] > r[:, None], f(-1e30), f(0))
    d["causalT"] = con(d["causal"].T)
    d["order"] = np.broadcast_to(np.arange(NE, 0, -1, dtype=f), (P, NE)).copy()
    inv = 1.0 / 10000.0 ** (np.arange(0, DH, 2, dtype=f) / f(DH))
    ang = np.arange(S, dtype=f)[:, None] * inv[None].astype(f)
    cos, sin = np.cos(ang).astype(f), np.sin(ang).astype(f)
    full = lambda a: con(np.tile(a, (1, H)).reshape(T, P, D).transpose(1, 0, 2)).astype(f)
    d["rope_cos"] = full(np.repeat(cos, 2, axis=1))
    d["rope_sin"] = full(np.stack([-sin, sin], axis=-1).reshape(S, DH))
    return d


def kernel(**inputs):
    import numpy as np
    import concourse.bacc as bacc
    from concourse.bass_utils import run_bass_kernel_spmd

    nc = bacc.Bacc("TRN2", target_bir_lowering=False, num_devices=1)
    arrays = layouts(inputs)
    dram = {k: nc.dram_tensor("in_" + k, a.shape, mybir.dt.from_np(a.dtype), kind="ExternalInput").ap()
            for k, a in arrays.items()}
    out = nc.dram_tensor("out", (B, S, D), F32, kind="ExternalOutput").ap()
    build(nc, dram, out)
    r = run_bass_kernel_spmd(nc, [{"in_" + k: a for k, a in arrays.items()}], core_ids=[0])
    return r.results[0]["out"]
```

```python
from contextlib import ExitStack

import concourse.bass as bass
from concourse import mybir

F32 = mybir.dt.float32
F32R = mybir.dt.float32r
BF16 = mybir.dt.bfloat16
ALU = mybir.AluOpType
ACT = mybir.ActivationFunctionType
AXX = mybir.AxisListType.X
RMAX = bass.bass_isa.ReduceOp.max

B, S, D = 8, 512, 128
P = 128
T = S // P
H, DH = 16, 8
M = 32
F = 512
FC = F // P
NE = 8
LANES = 2
WIDE = 4
EPS = 1e-5
EPS_K = 1e-4
SCALE = DH ** -0.5




class Chain:

    def __init__(self, eng, sem, per, passed):
        self.eng, self.sem, self.per, self.passed = eng, sem, per, passed
        self.b, self.n, self.base = 0, 0, 0

    def start(self, b, base=0):
        self.b, self.n, self.base = b, 0, base

    def do(self, ins):
        self.n += 1
        return ins.then_inc(self.sem, 1)

    def sync(self):
        self.eng.wait_ge(self.sem, self.b * self.per + (self.base + self.n))

    def end(self):
        assert self.n == self.per, f"the chain signals {self.n} times an iteration"


def bc(ap, n):
    return ap.unsqueeze(1).broadcast_to([ap.shape[0], n, ap.shape[1]])


def each(ap, n):
    return ap.unsqueeze(len(ap.shape)).broadcast_to(list(ap.shape) + [n])


def ln_stats(nc, ch, src, stats, mv):
    for t in range(T):
        ch.do(nc.vector.bn_stats(stats[:, t, :], src[:, t, :]))
    ch.sync()
    ch.eng.sem_inc(ch.passed, 1)
    for t in range(T):
        ch.do(nc.vector.bn_aggr(mv[:, t, :], stats[:, t, :]))
    ch.sync()
    return nc.vector.tensor_scalar_add(mv[:, :, 1], mv[:, :, 1], EPS)


def ln_apply(nc, ch, dst, src, mv, rstd):
    for t in range(T):
        ch.do(nc.vector.tensor_scalar(dst[:, t, :], src[:, t, :], mv[:, t, 0:1], rstd[:, t:t + 1],
                                      ALU.subtract, ALU.mult))


def mm3(nc, out, a, b, start=True, stop=True):
    nc.tensor.matmul(out, a[0], b[0], start=start, stop=False)
    nc.tensor.matmul(out, a[0], b[1], start=False, stop=False)
    return nc.tensor.matmul(out, a[1], b[0], start=False, stop=stop)


def positive(value):
    return not isinstance(value, int) or value > 0


def clear(nc, sems):
    with nc.Block() as block:
        @block.gpsimd
        def _(pool):
            for sem in sems:
                pool.sem_clear(sem)


def performer_layer(nc, X, ident, w, consts):
    ctx = ExitStack()
    with ctx:
        sems = []

        def sem(name):
            sems.append(ctx.enter_context(nc.semaphore("pf_" + name)))
            return sems[-1]

        sb = lambda name, shape, dt=F32: ctx.enter_context(nc.sbuf_tensor("pf_" + name, shape, dt))
        sb2 = lambda name, shape, dt=F32: [sb(f"{name}{L}", shape, dt) for L in range(LANES)]
        sem2 = lambda name: [sem(f"{name}{L}") for L in range(LANES)]
        banks = [[ctx.enter_context(nc.psum_tensor(f"pf_bank{L}{i}", [P, 512], F32)) for i in range(4)]
                 for L in range(LANES)]

        wq, wk, wv, wo = (sb(n, [P, D]) for n in ("wq", "wk", "wv", "wo"))
        w1 = sb("w1", [P, F])
        w2 = sb("w2", [P, FC, D])
        bq, bk = sb("bq", [P, 1]), sb("bk", [P, 1])
        b1 = sb("b1", [P, FC])
        bv, bo, b2, g2, be2, g3, be3 = (sb(n, [P, D]) for n in ("bv", "bo", "b2", "g2", "be2", "g3", "be3"))
        feats = sb("feats", [P, H * M])
        hsel = sb("hsel", [P, 32])
        bmask = sb("bmask", [P, P])
        ones = sb("ones", [P, 32])
        half = sb("half", [P, T])
        stats, mv, rstd = sb2("stats", [P, T, 6]), sb2("mv", [P, T, 2]), sb2("rstd", [P, T])
        y, yb, yT = sb2("y", [P, T, D]), sb2("yb", [P, T, D]), sb2("yT", [P, S])
        qT, kT, sqq, sqk = (sb2(n, [P, S]) for n in ("qT", "kT", "sqq", "sqk"))
        v = sb2("v", [P, T, D])
        dgT, dg = sb2("dgT", [64, S]), sb2("dg", [P, T, 64])
        kmx, km, stab = sb2("kmx", [P, T, H]), sb2("km", [P, H]), sb2("stab", [P, H])
        ck, qmx, cq = sb2("ck", [P, T, H]), sb2("qmx", [P, T, H]), sb2("cq", [P, T, H])
        kp, qp = sb2("kp", [P, T, H * M]), sb2("qp", [P, T, H * M])
        cm, cx = sb2("cm", [P, 2, P]), sb2("cx", [P, 2, P])
        qpT = sb2("qpT", [P, T, S])
        rd, oT = sb2("rd", [P, S]), sb2("oT", [P, S])
        r, x1, x1b, x1T = sb2("r", [P, T, D]), sb2("x1", [P, T, D]), sb2("x1b", [P, T, D]), sb2("x1T", [P, S])
        hT = sb2("hT", [P, FC, S])

        loaded, projected, init, half_ready = sem("loaded"), sem("projected"), sem("init"), sem("half_ready")
        passed = sem("passed")
        var_ready, rstd_ready = sem2("var_ready"), sem2("rstd_ready")
        y_ready, yb_ready, yT_ps, yT_ready = sem2("y_ready"), sem2("yb_ready"), sem2("yT_ps"), sem2("yT_ready")
        qkv_ps, qk_ready, v_ready = sem2("qkv_ps"), sem2("qk_ready"), sem2("v_ready")
        dg_ps, dgT_ready, dgt_ps, dg_ready = sem2("dg_ps"), sem2("dgT_ready"), sem2("dgt_ps"), sem2("dg_ready")
        kx_ps, kx_used, kx_kept = sem2("kx_ps"), sem2("kx_used"), sem2("kx_kept")
        qx_ps, qx_used = sem2("qx_ps"), sem2("qx_used")
        km_ready, stab_ready, kz_ready = sem2("km_ready"), sem2("stab_ready"), sem2("kz_ready")
        ke_ready, qe_ready, kp_ready, qp_ready = sem2("ke_ready"), sem2("qe_ready"), sem2("kp_ready"), sem2("qp_ready")
        cm_ps, cm_ready, cx_ps, cx_ready = sem2("cm_ps"), sem2("cm_ready"), sem2("cx_ps"), sem2("cx_ready")
        qpT_ps, qpT_ready, nd_ps, oT_ready = sem2("qpT_ps"), sem2("qpT_ready"), sem2("nd_ps"), sem2("oT_ready")
        wo_ps, wo_used, x1_ready, x1b_ready = sem2("wo_ps"), sem2("wo_used"), sem2("x1_ready"), sem2("x1b_ready")
        x1T_ps, x1T_ready, h_ps, h_ready, w2_ps = sem2("x1T_ps"), sem2("x1T_ready"), sem2("h_ps"), sem2("h_ready"), sem2("w2_ps")
        dve_steps = sem2("dve_steps")
        PER = 4 * 3 * T - 1 + 2 * 2 + 7

        loads = [(wq, w["WqT"]), (wk, w["WkT"]), (wv, w["WvT"]), (wo, w["WoT"]), (w1, w["W1T"]), (w2, w["W2T"]),
                 (bq, w["bq"]), (bk, w["bk"]), (b1, w["b1"]), (bv, w["bv"]), (bo, w["bo"]), (b2, w["b2"]),
                 (g2, w["g2"]), (be2, w["be2"]), (g3, w["g3"]), (be3, w["be3"]), (hsel, consts["hsel"]),
                 (bmask, consts["bmask"])]
        lanes = range(LANES)
        feat = lambda ap: ap.rearrange("p (h m) -> p h m", m=M)
        tokens = lambda bank: bank[:].rearrange("p (t d) -> p t d", t=T)

        ctx.callback(clear, nc, sems)
        block = ctx.enter_context(nc.Block())

        @block.sync
        def _(sp):
            for dst, src in loads:
                sp.dma_start(dst[:], src).then_inc(loaded, 16)
            sp.wait_ge(init, 1)
            for h in range(H):
                sp.dma_start(feats[h * DH:(h + 1) * DH, h * M:(h + 1) * M], w["projT"]).then_inc(projected, 16)

        @block.gpsimd
        def _(pool):
            nc.gpsimd.memset(feats[:], 0.0).then_inc(init, 1)
            nc.gpsimd.memset(ones[:], 1.0).then_inc(init, 1)
            nc.gpsimd.memset(half[:], -0.5).then_inc(half_ready, 1)
            pool.wait_ge(half_ready, 1)
            pool.wait_ge(loaded, 16 * len(loads))
            with pool.Fori(0, B // LANES) as i:
                def rsqrt(L, k):
                    pool.wait_ge(var_ready[L], i * 4 + k + 1)
                    nc.gpsimd.tensor_tensor(rstd[L][:], mv[L][:, :, 1], half[:], ALU.pow).then_inc(rstd_ready[L], 1)

                for L in lanes:
                    rsqrt(L, 0)
                for L in lanes:
                    pool.wait_ge(y_ready[L], i + 1)
                    nc.gpsimd.tensor_tensor(yb[L][:], y[L][:], bc(bo[:], T), ALU.add).then_inc(yb_ready[L], 1)
                for L in lanes:
                    pool.wait_ge(km_ready[L], i + 1)
                    pool.sem_inc(passed, 1)
                    nc.gpsimd.partition_all_reduce(stab[L][:], km[L][:], P, RMAX).then_inc(stab_ready[L], 1)
                for tile, exp_ready, ready in ((qp, qe_ready, qp_ready), (kp, ke_ready, kp_ready)):
                    for L in lanes:
                        pool.wait_ge(exp_ready[L], i + 1)
                        pool.sem_inc(passed, 1)
                        nc.gpsimd.tensor_scalar(tile[L][:], tile[L][:], EPS_K, M ** -0.5, ALU.add,
                                                ALU.mult).then_inc(ready[L], 1)
                for L in lanes:
                    rsqrt(L, 1)
                for L in lanes:
                    pool.wait_ge(x1_ready[L], i + 1)
                    nc.gpsimd.tensor_tensor(x1b[L][:], x1[L][:], bc(b2[:], T), ALU.add).then_inc(x1b_ready[L], 1)
                for k in (2, 3):
                    for L in lanes:
                        rsqrt(L, k)

        @block.vector
        def _(dve):
            ch = [Chain(dve, dve_steps[L], PER, passed) for L in lanes]
            dve.wait_ge(loaded, 16 * len(loads))
            dve.wait_ge(projected, 16 * H)
            dve.wait_ge(init, 2)
            nc.vector.tensor_scalar_mul(feats[:], feats[:], DH ** -0.25).then_inc(init, 1)
            with dve.Fori(0, B // LANES) as i:
                for L in lanes:
                    ch[L].start(i)
                x = [X[:, bass.ds((i * LANES + L) * T, T), :] for L in lanes]

                def moments(L, src):
                    ln_stats(nc, ch[L], src, stats[L], mv[L]).then_inc(var_ready[L], 1)

                def normalised(L, k, dst, src):
                    dve.wait_ge(rstd_ready[L], i * 4 + k + 1)
                    ln_apply(nc, ch[L], dst, src, mv[L], rstd[L])
                    ch[L].sync()

                def affine(L, tile, gain, shift):
                    ch[L].do(nc.vector.tensor_tensor(tile[:], tile[:], bc(gain[:], T), ALU.mult))
                    ch[L].sync()
                    return nc.vector.tensor_tensor(tile[:], tile[:], bc(shift[:], T), ALU.add)

                for L in lanes:
                    moments(L, x[L])
                for L in lanes:
                    dve.wait_ge(rstd_ready[L], i * 4 + 1)
                    for t in range(T):
                        last = nc.vector.tensor_scalar(y[L][:, t, :], x[L][:, t, :], mv[L][:, t, 0:1],
                                                       rstd[L][:, t:t + 1], ALU.subtract, ALU.mult)
                        if t < T - 1:
                            ch[L].do(last)
                    last.then_inc(y_ready[L], 1)
                for L in lanes:
                    dve.wait_ge(qkv_ps[L], i * 3 + 3)
                    nc.vector.tensor_tensor(v[L][:], tokens(banks[L][3]), bc(bv[:], T), ALU.add).then_inc(v_ready[L], 1)
                for L in lanes:
                    dve.wait_ge(dgt_ps[L], i + 1)
                    nc.vector.tensor_copy(dg[L][:], banks[L][1][:, 0:T * 64].rearrange("p (t k) -> p t k", t=T)
                                          ).then_inc(dg_ready[L], 1)
                for t in range(T):
                    for L in lanes:
                        dve.wait_ge(kx_ps[L], i * T + t + 1)
                        nc.vector.tensor_reduce(kmx[L][:, t, :], feat(banks[L][2 + t % 2][:]), AXX,
                                                ALU.max).then_inc(kx_used[L], 1)
                for L in lanes:
                    dve.wait_ge(kx_used[L], i * T + T)
                    nc.vector.tensor_reduce(km[L][:], kmx[L][:].rearrange("p t h -> p h t"), AXX,
                                            ALU.max).then_inc(km_ready[L], 1)
                for pair in range(2):
                    for L in lanes:
                        for t in (2 * pair, 2 * pair + 1):
                            dve.wait_ge(qx_ps[L], i * T + t + 1)
                            last = nc.vector.tensor_reduce(qmx[L][:, t, :], feat(banks[L][t % 2][:]), AXX, ALU.max)
                        ch[L].do(last)
                    for L in lanes:
                        ch[L].sync()
                        two = slice(2 * pair, 2 * pair + 2)
                        ch[L].do(nc.vector.tensor_tensor(cq[L][:, two], qmx[L][:, two], dg[L][:, two, 0:H], ALU.add))
                    for L in lanes:
                        ch[L].sync()
                        for t in (2 * pair, 2 * pair + 1):
                            nc.vector.tensor_tensor(feat(qp[L][:, t, :]), feat(banks[L][t % 2][:]), each(cq[L][:, t, :], M),
                                                    ALU.subtract).then_inc(qx_used[L], 1)
                for L in lanes:
                    dve.wait_ge(stab_ready[L], i + 1)
                    ch[L].do(nc.vector.tensor_tensor(ck[L][:], dg[L][:, :, 32:32 + H], bc(stab[L][:], T), ALU.add))
                for L in lanes:
                    ch[L].sync()
                    dve.wait_ge(kx_kept[L], i * T + T)
                    keys = kp[L][:].rearrange("p t (h m) -> p (t h) m", m=M)
                    nc.vector.tensor_tensor(keys, keys, each(ck[L][:].rearrange("p t h -> p (t h)"), M),
                                            ALU.subtract).then_inc(kz_ready[L], 1)
                for L in lanes:
                    dve.wait_ge(cm_ps[L], i + 1)
                    nc.vector.tensor_tensor(cm[L][:, 0, :], banks[L][2][:, 0:P], bmask[:], ALU.mult)
                    nc.vector.tensor_tensor(cm[L][:, 1, :], banks[L][3][:, 0:P], bmask[:], ALU.mult).then_inc(cm_ready[L], 1)
                for L in lanes:
                    dve.wait_ge(nd_ps[L], i + 1)
                    ch[L].do(nc.vector.reciprocal(rd[L][:], banks[L][1][:]))
                for L in lanes:
                    ch[L].sync()
                    nc.vector.tensor_tensor(oT[L][:], banks[L][0][:], rd[L][:], ALU.mult).then_inc(oT_ready[L], 1)
                for L in lanes:
                    dve.wait_ge(wo_ps[L], i + 1)
                    dve.wait_ge(yb_ready[L], i + 1)
                    nc.vector.tensor_tensor(r[L][:], tokens(banks[L][2]), yb[L][:], ALU.add).then_inc(wo_used[L], 1)
                for L in lanes:
                    dve.wait_ge(wo_used[L], i + 1)
                    moments(L, r[L])
                for L in lanes:
                    normalised(L, 1, x1[L], r[L])
                for L in lanes:
                    affine(L, x1[L], g2, be2).then_inc(x1_ready[L], 1)
                for L in lanes:
                    dve.wait_ge(w2_ps[L], i + 1)
                    dve.wait_ge(x1b_ready[L], i + 1)
                    ch[L].do(nc.vector.tensor_tensor(r[L][:], tokens(banks[L][0]), x1b[L][:], ALU.add))
                for L in lanes:
                    ch[L].sync()
                    moments(L, r[L])
                for L in lanes:
                    normalised(L, 2, x1[L], r[L])
                for L in lanes:
                    ch[L].do(affine(L, x1[L], g3, be3))
                for L in lanes:
                    ch[L].sync()
                    moments(L, x1[L])
                for L in lanes:
                    normalised(L, 3, r[L], x1[L])
                for L in lanes:
                    ch[L].do(nc.vector.tensor_tensor(x[L], x[L], r[L][:], ALU.add))
                for L in lanes:
                    ch[L].sync()
                    ch[L].end()

        @block.scalar
        def _(act):
            act.wait_ge(loaded, 16 * len(loads))
            with act.Fori(0, B // LANES) as i:
                for L in lanes:
                    act.wait_ge(yT_ps[L], i + 1)
                    nc.scalar.activation(yT[L][:], banks[L][0][:], ACT.Copy).then_inc(yT_ready[L], 1)
                for L in lanes:
                    for k, (bias, lin, sq) in enumerate(((bq, qT, sqq), (bk, kT, sqk))):
                        act.wait_ge(qkv_ps[L], i * 3 + k + 1)
                        nc.scalar.activation(sq[L][:], banks[L][1 + k][:], ACT.Square, bias=bias[:])
                        nc.scalar.activation(lin[L][:], banks[L][1 + k][:], ACT.Identity, bias=bias[:]).then_inc(qk_ready[L], 1)
                for L in lanes:
                    act.wait_ge(dg_ps[L], i + 1)
                    nc.scalar.activation(dgT[L][:], banks[L][0][0:64, :], ACT.Copy, scale=0.5 * DH ** -0.5).then_inc(dgT_ready[L], 1)
                for t in range(T):
                    for L in lanes:
                        act.wait_ge(kx_used[L], i * T + t + 1)
                        nc.scalar.activation(kp[L][:, t, :], banks[L][2 + t % 2][:], ACT.Copy).then_inc(kx_kept[L], 1)
                for L in lanes:
                    act.wait_ge(qx_used[L], i * T + T)
                    nc.scalar.activation(qp[L][:], qp[L][:], ACT.Exp).then_inc(qe_ready[L], 1)
                for L in lanes:
                    act.wait_ge(kz_ready[L], i + 1)
                    nc.scalar.activation(kp[L][:], kp[L][:], ACT.Exp).then_inc(ke_ready[L], 1)
                for g in range(3):
                    for L in lanes:
                        act.wait_ge(qpT_ps[L], i * T + g + 1)
                        nc.scalar.activation(qpT[L][:, g, :], banks[L][g % 2][:], ACT.Copy).then_inc(qpT_ready[L], 1)
                for L in lanes:
                    act.wait_ge(cx_ps[L], i + 1)
                    nc.scalar.activation(cx[L][:], banks[L][3][:, P:3 * P].rearrange("p (k m) -> p k m", k=2),
                                         ACT.Copy).then_inc(cx_ready[L], 1)
                for L in lanes:
                    act.wait_ge(qpT_ps[L], i * T + T)
                    nc.scalar.activation(qpT[L][:, 3, :], banks[L][1][:], ACT.Copy).then_inc(qpT_ready[L], 1)
                for L in lanes:
                    act.wait_ge(x1T_ps[L], i + 1)
                    nc.scalar.activation(x1T[L][:], banks[L][3][:], ACT.Copy).then_inc(x1T_ready[L], 1)
                for c in range(FC):
                    for L in lanes:
                        act.wait_ge(h_ps[L], i * FC + c + 1)
                        nc.scalar.activation(hT[L][:, c, :], banks[L][c][:], ACT.Relu, bias=b1[:, c:c + 1]).then_inc(h_ready[L], 1)

        @block.tensor
        def _(pe):
            pe.wait_ge(loaded, 16 * len(loads))
            pe.wait_ge(init, 3)
            tile = lambda ap, t: ap[:, t * P:(t + 1) * P]

            def transposed(bank, src, signal):
                for t in range(T):
                    last = nc.tensor.transpose(tile(bank, t), src[:, t, :], ident[:])
                last.then_inc(signal, 1)

            with pe.Fori(0, B // LANES) as i:
                for L in lanes:
                    pe.wait_ge(y_ready[L], i + 1)
                    transposed(banks[L][0], y[L], yT_ps[L])
                for L in lanes:
                    pe.wait_ge(yT_ready[L], i + 1)
                    nc.tensor.matmul(banks[L][1][:], wq[:], yT[L][:], start=True, stop=True).then_inc(qkv_ps[L], 1)
                    nc.tensor.matmul(banks[L][2][:], wk[:], yT[L][:], start=True, stop=True).then_inc(qkv_ps[L], 1)
                    for t in range(T):
                        last = nc.tensor.matmul(tile(banks[L][3], t), tile(yT[L], t), wv[:], start=True, stop=True)
                    last.then_inc(qkv_ps[L], 1)
                for L in lanes:
                    pe.wait_ge(qk_ready[L], i * 2 + 2)
                    nc.tensor.matmul(banks[L][0][0:32, :], hsel[:], sqq[L][:], start=True, stop=True)
                    nc.tensor.matmul(banks[L][0][32:64, :], hsel[:], sqk[L][:], start=True, stop=True).then_inc(dg_ps[L], 1)
                for t in range(2):
                    for L in lanes:
                        if t == 0:
                            pe.wait_ge(v_ready[L], i + 1)
                        nc.tensor.matmul(banks[L][2 + t][:], tile(kT[L], t), feats[:], start=True, stop=True).then_inc(kx_ps[L], 1)
                for L in lanes:
                    pe.wait_ge(dgT_ready[L], i + 1)
                    pe.sem_inc(passed, 1)
                    for t in range(T):
                        last = nc.tensor.transpose(banks[L][1][:, t * 64:(t + 1) * 64], tile(dgT[L], t), ident[0:64, 0:64])
                    last.then_inc(dgt_ps[L], 1)
                for t in range(2, T):
                    for L in lanes:
                        pe.wait_ge(kx_kept[L], i * T + t - 1)
                        nc.tensor.matmul(banks[L][t][:], tile(kT[L], t), feats[:], start=True, stop=True).then_inc(kx_ps[L], 1)
                for t in range(T):
                    for L in lanes:
                        if t == 0:
                            pe.wait_ge(dg_ready[L], i + 1)
                        if t >= 2:
                            pe.wait_ge(qx_used[L], i * T + t - 1)
                        nc.tensor.matmul(banks[L][t % 2][:], tile(qT[L], t), feats[:], start=True, stop=True).then_inc(qx_ps[L], 1)
                for g in range(2):
                    for L in lanes:
                        pe.wait_ge(qp_ready[L], i + 1)
                        for t in range(T):
                            last = nc.tensor.transpose(tile(banks[L][g], t), qp[L][:, t, g * P:(g + 1) * P], ident[:])
                        last.then_inc(qpT_ps[L], 1)
                for L in lanes:
                    pe.wait_ge(kp_ready[L], i + 1)
                    for bank, left in ((banks[L][2], lambda t, g: v[L][:, t, 32 * g:32 * g + 32]), (banks[L][3], lambda t, g: ones[:])):
                        for t in range(T):
                            for g in range(4):
                                last = nc.tensor.matmul(bank[32 * g:32 * g + 32, 0:P], left(t, g),
                                                        kp[L][:, t, g * P:(g + 1) * P], start=t == 0, stop=t == T - 1)
                    last.then_inc(cm_ps[L], 1)
                for L in lanes:
                    pe.wait_ge(qpT_ready[L], i * T + 1)
                    for t in range(T):
                        last = nc.tensor.transpose(tile(banks[L][0], t), qp[L][:, t, 2 * P:3 * P], ident[:])
                    last.then_inc(qpT_ps[L], 1)
                for L in lanes:
                    pe.wait_ge(cm_ready[L], i + 1)
                    for k in range(2):
                        last = nc.tensor.transpose(tile(banks[L][3], k + 1), cm[L][:, k, :], ident[:])
                    last.then_inc(cx_ps[L], 1)
                for L in lanes:
                    pe.wait_ge(qpT_ready[L], i * T + 2)
                    for t in range(T):
                        last = nc.tensor.transpose(tile(banks[L][1], t), qp[L][:, t, 3 * P:4 * P], ident[:])
                    last.then_inc(qpT_ps[L], 1)
                for L in lanes:
                    pe.wait_ge(cx_ready[L], i + 1)
                    pe.wait_ge(qpT_ready[L], i * T + T)
                    for k in range(2):
                        for g in range(4):
                            last = nc.tensor.matmul(banks[L][k][32 * g:32 * g + 32, :], cx[L][:, k, 32 * g:32 * g + 32],
                                                    qpT[L][:, g, :], start=True, stop=True)
                    last.then_inc(nd_ps[L], 1)
                for L in lanes:
                    pe.wait_ge(oT_ready[L], i + 1)
                    for t in range(T):
                        last = nc.tensor.matmul(tile(banks[L][2], t), tile(oT[L], t), wo[:], start=True, stop=True)
                    last.then_inc(wo_ps[L], 1)
                for L in lanes:
                    pe.wait_ge(x1_ready[L], i + 1)
                    transposed(banks[L][3], x1[L], x1T_ps[L])
                for L in lanes:
                    pe.wait_ge(x1T_ready[L], i + 1)
                    for c in range(FC):
                        nc.tensor.matmul(banks[L][c][:], tile(w1, c), x1T[L][:], start=True, stop=True).then_inc(h_ps[L], 1)
                for L in lanes:
                    pe.wait_ge(h_ready[L], i * FC + FC)
                    for t in range(T):
                        for c in range(FC):
                            last = nc.tensor.matmul(tile(banks[L][0], t), hT[L][:, c, t * P:(t + 1) * P], w2[:, c, :],
                                                    start=c == 0, stop=c == FC - 1)
                    last.then_inc(w2_ps[L], 1)


GH = 4
NG = H // GH
KS = 96
SR = 3
KM = KS + 2
CE = D // 8


def project_qkv(nc, X, Y, V, ident, w, consts, halves, contexts, rope):
    ctx = ExitStack()
    layer = "rope_" if rope else "ctx_"
    with ctx:
        sb = lambda name, shape, dt=F32: ctx.enter_context(nc.sbuf_tensor(layer + "pr_" + name, shape, dt))
        sems = []

        def sem(name):
            sems.append(ctx.enter_context(nc.semaphore(layer + "pr_" + name)))
            return sems[-1]

        lanes = range(WIDE)
        sb2 = lambda name, shape, dt=F32: [sb(f"{name}{L}", shape, dt) for L in lanes]
        sem2 = lambda name: [sem(f"{name}{L}") for L in lanes]
        banks = [[ctx.enter_context(nc.psum_tensor(f"{layer}pr_bank{L}{i}", [P, 512], F32)) for i in range(2)] for L in lanes]
        wq, wk, wv = (sb(n, [P, D]) for n in ("wq", "wk", "wv"))
        loads = [(wq, w["WqT"]), (wk, w["WkT"]), (wv, w["WvT"])]
        if rope:
            bq, bqs, bk, bv = sb("bq", [P, 1]), sb("bqs", [P, 1]), sb("bk", [P, 1]), sb("bv", [P, D])
            cos, sin = sb("cos", [P, T, D]), sb("sin", [P, T, D])
            loads += [(bq, w["bq"]), (bk, w["bk"]), (bv, w["bv"]), (cos, consts["rope_cos"]), (sin, consts["rope_sin"])]
            turned, rot = sb2("turned", [P, T, D]), sb2("rot", [P, T, D])
        else:
            we = sb("we", [P, CE])
            loads += [(we, w["WeT"])]
            cf, cs = sb2("cf", [CE, S]), sb2("cs", [CE, S])
            c4 = [[sb(f"c4{L}{k}", [CE, S], F32R) for k in range(4)] for L in lanes]
        stats, mv, rstd = sb2("stats", [P, T, 6]), sb2("mv", [P, T, 2]), sb2("rstd", [P, T])
        half = sb("half", [P, T])
        y, yT = sb2("y", [P, T, D]), sb2("yT", [P, S])
        rT = sb2("rT", [P, S]) if rope else None
        qf, kf = sb2("qf", [P, S]), sb2("kf", [P, S])
        qk4 = [[sb(f"qk4{L}{k}", [P, S], F32R) for k in range(4)] for L in lanes]

        loaded, half_ready, bqs_ready = sem("loaded"), sem("half_ready"), sem("bqs_ready")
        dve_steps, passed = sem("dve_steps"), sem("passed")
        var_ready, rstd_ready, y_ready = sem2("var_ready"), sem2("rstd_ready"), sem2("y_ready")
        turn_ready, rot_ready = sem2("turn_ready"), sem2("rot_ready")
        yT_ps, rT_ps, yT_ready, rT_ready = sem2("yT_ps"), sem2("rT_ps"), sem2("yT_ready"), sem2("rT_ready")
        q_ps, k_ps, v_ps, c_ps = sem2("q_ps"), sem2("k_ps"), sem2("v_ps"), sem2("c_ps")
        q_ready, k_ready, c_ready = sem2("q_ready"), sem2("k_ready"), sem2("c_ready")
        low_ready, v_ready, stored, y_kept = sem2("low_ready"), sem2("v_ready"), sem2("stored"), sem2("y_kept")
        NQ = 2 if rope else 3
        NS = 64 if rope else 128
        PER = WIDE * (3 * T - 1) + WIDE
        ctx.callback(clear, nc, sems)
        block = ctx.enter_context(nc.Block())

        @block.sync
        def _(sp):
            for dst, src in loads:
                sp.dma_start(dst[:], src).then_inc(loaded, 16)
            with sp.Fori(0, B // WIDE) as i:
                for L in lanes:
                    sp.wait_ge(low_ready[L], i * NQ + 2)
                    sp.sem_inc(passed, 1)
                    for k in range(4):
                        sp.dma_start(halves[i * WIDE + L, k], qk4[L][k][:].bitcast(F32)).then_inc(stored[L], 16)
                if not rope:
                    for L in lanes:
                        sp.wait_ge(low_ready[L], i * NQ + 3)
                        sp.sem_inc(passed, 1)
                        for k in range(4):
                            sp.dma_start(contexts[i * WIDE + L, k], c4[L][k][:].bitcast(F32)).then_inc(stored[L], 16)
                for L in lanes:
                    sp.wait_ge(stored[L], (i + 1) * NS)
                    sp.sem_inc(passed, 1)

        @block.gpsimd
        def _(pool):
            nc.gpsimd.memset(half[:], -0.5).then_inc(half_ready, 1)
            pool.wait_ge(half_ready, 1)
            pool.wait_ge(loaded, 16 * len(loads))
            with pool.Fori(0, B // WIDE) as i:
                for L in lanes:
                    pool.wait_ge(var_ready[L], i + 1)
                    nc.gpsimd.tensor_tensor(rstd[L][:], mv[L][:, :, 1], half[:], ALU.pow).then_inc(rstd_ready[L], 1)
                if rope:
                    for L in lanes:
                        pool.wait_ge(y_ready[L], i + 1)
                        pair = lambda t: t[:].rearrange("p t (k two) -> p (t k) two", two=2)
                        for m in range(2):
                            last = nc.gpsimd.tensor_tensor(pair(turned[L])[:, :, m], pair(y[L])[:, :, 1 - m],
                                                           pair(sin)[:, :, m], ALU.mult)
                        last.then_inc(turn_ready[L], 1)

        @block.vector
        def _(dve):
            ch = Chain(dve, dve_steps, PER, passed)
            dve.wait_ge(loaded, 16 * len(loads))
            if rope:
                nc.vector.tensor_scalar_mul(bqs[:], bq[:], SCALE).then_inc(bqs_ready, 1)
            with dve.Fori(0, B // WIDE) as i:
                ch.start(i)
                x = [X[:, bass.ds((i * WIDE + L) * T, T), :] for L in lanes]
                for L in lanes:
                    for t in range(T):
                        ch.do(nc.vector.bn_stats(stats[L][:, t, :], x[L][:, t, :]))
                ch.sync()
                dve.sem_inc(passed, 1)
                for L in lanes:
                    for t in range(T):
                        ch.do(nc.vector.bn_aggr(mv[L][:, t, :], stats[L][:, t, :]))
                ch.sync()
                for L in lanes:
                    nc.vector.tensor_scalar_add(mv[L][:, :, 1], mv[L][:, :, 1], EPS).then_inc(var_ready[L], 1)
                for L in lanes:
                    dve.wait_ge(rstd_ready[L], i + 1)
                    for t in range(T):
                        last = nc.vector.tensor_scalar(y[L][:, t, :], x[L][:, t, :], mv[L][:, t, 0:1], rstd[L][:, t:t + 1],
                                                       ALU.subtract, ALU.mult)
                        if t < T - 1:
                            ch.do(last)
                    last.then_inc(y_ready[L], 1)
                if rope:
                    for L in lanes:
                        dve.wait_ge(y_ready[L], i + 1)
                        ch.do(nc.vector.tensor_tensor(rot[L][:], y[L][:], cos[:], ALU.mult))
                    ch.sync()
                    for L in lanes:
                        dve.wait_ge(turn_ready[L], i + 1)
                        nc.vector.tensor_tensor(rot[L][:], rot[L][:], turned[L][:], ALU.add).then_inc(rot_ready[L], 1)
                for full, k, ready in ((qf, 0, q_ready), (kf, 2, k_ready)):
                    for L in lanes:
                        dve.wait_ge(ready[L], i * 2 + 2)
                        nc.vector.tensor_tensor(qk4[L][k + 1][:], full[L][:], qk4[L][k][:].bitcast(F32),
                                                ALU.subtract).then_inc(low_ready[L], 1)
                for L in lanes:
                    dve.wait_ge(v_ps[L], i + 1)
                    dst, src = V[:, bass.ds((i * WIDE + L) * T, T), :], banks[L][1][:].rearrange("p (t d) -> p t d", t=T)
                    if rope:
                        last = nc.vector.tensor_tensor(dst, src, bc(bv[:], T), ALU.add)
                    else:
                        last = nc.vector.tensor_copy(dst, src)
                    last.then_inc(v_ready[L], 1)
                if not rope:
                    for L in lanes:
                        dve.wait_ge(c_ready[L], i * 4 + 4)
                        ch.do(nc.vector.tensor_tensor(c4[L][1][:], cs[L][:], c4[L][0][:].bitcast(F32), ALU.subtract))
                        nc.vector.tensor_tensor(c4[L][3][:], cf[L][:], c4[L][2][:].bitcast(F32), ALU.subtract).then_inc(low_ready[L], 1)
                for L in lanes:
                    dve.wait_ge(v_ready[L], i + 1)
                    if rope:
                        dve.wait_ge(y_kept[L], i + 1)
                    dve.wait_ge(stored[L], (i + 1) * NS)
                ch.end()

        @block.scalar
        def _(act):
            act.wait_ge(loaded, 16 * len(loads))
            if rope:
                act.wait_ge(bqs_ready, 1)
            with act.Fori(0, B // WIDE) as i:
                for L in lanes:
                    act.wait_ge(yT_ps[L], i + 1)
                    nc.scalar.activation(yT[L][:], banks[L][0][:], ACT.Copy).then_inc(yT_ready[L], 1)
                if rope:
                    for L in lanes:
                        act.wait_ge(rT_ps[L], i + 1)
                        nc.scalar.activation(rT[L][:], banks[L][1][:], ACT.Copy).then_inc(rT_ready[L], 1)
                for L in lanes:
                    act.wait_ge(q_ps[L], i + 1)
                    for dst in (qf[L], qk4[L][0]):
                        bias = dict(bias=bqs[:]) if rope else {}
                        nc.scalar.activation(dst[:], banks[L][1][:], ACT.Identity, scale=SCALE, **bias).then_inc(q_ready[L], 1)
                    act.wait_ge(k_ps[L], i + 1)
                    for dst in (kf[L], qk4[L][2]):
                        bias = dict(bias=bk[:]) if rope else {}
                        nc.scalar.activation(dst[:], banks[L][0][:], ACT.Identity, **bias).then_inc(k_ready[L], 1)
                if rope:
                    for L in lanes:
                        nc.scalar.activation(Y[:, bass.ds((i * WIDE + L) * T, T), :], y[L][:], ACT.Copy).then_inc(y_kept[L], 1)
                else:
                    for L in lanes:
                        act.wait_ge(c_ps[L], i + 1)
                        for dst, scale in ((cs[L], 0.1), (c4[L][0], 0.1), (cf[L], 1.0), (c4[L][2], 1.0)):
                            nc.scalar.activation(dst[:], banks[L][0][0:CE, :], ACT.Copy, scale=scale).then_inc(c_ready[L], 1)

        @block.tensor
        def _(pe):
            pe.wait_ge(loaded, 16 * len(loads))
            with pe.Fori(0, B // WIDE) as i:
                def transposed(bank, src, signal):
                    for t in range(T):
                        last = nc.tensor.transpose(bank[:, t * P:(t + 1) * P], src[:, t, :], ident[:])
                    last.then_inc(signal, 1)

                for L in lanes:
                    pe.wait_ge(y_ready[L], i + 1)
                    transposed(banks[L][0], y[L], yT_ps[L])
                if rope:
                    for L in lanes:
                        pe.wait_ge(rot_ready[L], i + 1)
                        transposed(banks[L][1], rot[L], rT_ps[L])
                for L in lanes:
                    pe.wait_ge(yT_ready[L], i + 1)
                    if rope:
                        pe.wait_ge(rT_ready[L], i + 1)
                    turned_in = rT[L] if rope else yT[L]
                    nc.tensor.matmul(banks[L][1][:], wq[:], turned_in[:], start=True, stop=True).then_inc(q_ps[L], 1)
                    nc.tensor.matmul(banks[L][0][:], wk[:], turned_in[:], start=True, stop=True).then_inc(k_ps[L], 1)
                for L in lanes:
                    pe.wait_ge(q_ready[L], i * 2 + 2)
                    for t in range(T):
                        last = nc.tensor.matmul(banks[L][1][:, t * P:(t + 1) * P], yT[L][:, t * P:(t + 1) * P], wv[:],
                                                start=True, stop=True)
                    last.then_inc(v_ps[L], 1)
                    if not rope:
                        pe.wait_ge(k_ready[L], i * 2 + 2)
                        nc.tensor.matmul(banks[L][0][0:CE, :], we[:], yT[L][:], start=True, stop=True).then_inc(c_ps[L], 1)


def attend(nc, V, ident, consts, halves, contexts, guards, outs, causal):
    ctx = ExitStack()
    layer = "rope_" if causal else "ctx_"
    with ctx:
        sb = lambda name, shape, dt=F32: ctx.enter_context(nc.sbuf_tensor(layer + "at_" + name, shape, dt))
        sems = []

        def sem(name):
            sems.append(ctx.enter_context(nc.semaphore(layer + "at_" + name)))
            return sems[-1]

        ps = lambda name, n: ctx.enter_context(nc.psum_tensor(layer + "at_" + name, [P, n], F32))
        s_bank = [ps(f"s{k}", 512) for k in range(SR)]
        st_bank = [ps(f"st{k}", 1024) for k in range(2)]
        o_bank = ps("o", 512)

        if causal:
            width = [S - P * c for c in range(T)]
            place = [(0, 0), (0, 512), (1, 0), (0, 896)]
            units, order = [1024, 256], [[0, 1, 3], [2]]
        else:
            width = [S] * T
            place = [(0, 0), (0, 512), (1, 0), (1, 512)]
            units, order = [1024, 1024], [[0, 1], [2, 3]]
        PW = sum(units)
        at = lambda c: (units[0] if place[c][0] else 0) + place[c][1]

        kst, qst = sb("kst", [KM, NG, GH, S], F32R), sb("qst", [KM, NG, GH, S], F32R)
        probs = [sb(f"probs{k}", [P, GH, PW]) for k in range(2)]
        vaug = [sb(f"vaug{k}", [P, 2, T, GH, 32]) for k in range(2)]
        nm = sb("nm", [P, NG, GH * T])
        cut, cutT = sb("cut", [P, 2, GH * T], F32R), sb("cutT", [P, 32], F32R)
        oe = sb("oe", [P, S])
        if causal:
            maskf, maskb, identb = sb("maskf", [P, P]), sb("maskb", [P, P], BF16), sb("identb", [P, P], BF16)

        masked = sem("masked")
        q_clear, k_clear = sem("q_clear"), sem("k_clear")
        init, masks_loaded, masks_ready = sem("init"), sem("masks_loaded"), sem("masks_ready")
        stack = [sem(f"stack_loaded{g}") for g in range(NG)]
        s_ready, s_used = sem("s_ready"), sem("s_used")
        st_ready, p_ready, pv_done = sem("st_ready"), sem("p_ready"), sem("pv_done")
        mh_ready, ml_ready, mT_ready = sem("mh_ready"), sem("ml_ready"), sem("mT_ready")
        m_stored, m_loaded = sem("m_stored"), sem("m_loaded")
        v_ready, o_ready, o_stored = sem("v_ready"), sem("o_ready"), sem("o_stored")
        NL = 6 if causal else 12
        LAST = B - 1
        passed = sem("passed")
        ctx.callback(clear, nc, sems)
        block = ctx.enter_context(nc.Block())

        def group(b, g):
            return b + g // NG, g % NG

        def within(b):
            return not isinstance(b, int) or 0 <= b < B

        def batches(eng, body):
            body(0)
            with eng.Fori(1, LAST) as b:
                body(b)
            body(LAST)

        @block.sync
        def _(sp):
            if causal:
                sp.dma_start(maskf[:], consts["causal"]).then_inc(masks_loaded, 16)
            def load_stack(b, g, tile, parts):
                for r, part in enumerate(parts):
                    src = halves[b, part, g * GH * DH:(g + 1) * GH * DH, :].rearrange("(h d) t -> d h t", d=DH)
                    sp.dma_start(tile[r * DH:(r + 1) * DH, g].bitcast(F32), src).then_inc(stack[g], 16)
                if not causal:
                    for r, part in enumerate(parts):
                        src = contexts[b, part].unsqueeze(1).broadcast_to([CE, GH, S])
                        lo = 3 * DH + r * CE
                        sp.dma_start(tile[lo:lo + CE, g].bitcast(F32), src).then_inc(stack[g], 16)

            def load_stacks(b, g):
                load_stack(b, g, qst, (0, 1, 0))
                load_stack(b, g, kst, (2, 2, 3))

            def store_guard(b, g):
                sp.wait_ge(mT_ready, b * NG + g + 1)
                sp.sem_inc(passed, 1)
                sp.dma_start(guards[g], cutT[:].bitcast(F32)).then_inc(m_stored, 16)

            def load_guard(b, g):
                sp.wait_ge(m_stored, (b * NG + g + 1) * 16)
                sp.sem_inc(passed, 1)
                blocks = guards[g].rearrange("(k n) i -> n k i", k=P // 32)
                for part in range(2):
                    src = blocks[part * GH * T:(part + 1) * GH * T].unsqueeze(0)
                    dst = qst[KS + part:KS + part + 1, g].rearrange("o j (t k i) -> o (j t) k i", t=T, i=32)
                    sp.dma_start(dst.bitcast(F32), src).then_inc(m_loaded, 16)

            def store_out(b, hf):
                sp.wait_ge(o_ready, b * 2 + hf + 1)
                sp.sem_inc(passed, 1)
                sp.dma_start(outs[b, hf], oe[:]).then_inc(o_stored, 16)

            def body(b):
                for g in range(NG):
                    ahead, nxt = group(b, g + 3), group(b, g + 1)
                    if within(ahead[0]):
                        if positive(b * NG + g):
                            sp.wait_ge(st_ready, b * NG * GH * 2 + g * GH * 2)
                            sp.sem_inc(passed, 1)
                        load_stack(*ahead, qst, (0, 1, 0))
                    if within(nxt[0]):
                        if positive(b * NG + g):
                            sp.wait_ge(m_loaded, (b * NG + g) * 32)
                            sp.sem_inc(passed, 1)
                        store_guard(*nxt)
                    if within(ahead[0]):
                        load_stack(*ahead, kst, (2, 2, 3))
                    if within(nxt[0]):
                        load_guard(*nxt)
                    if g % 2 == 0:
                        to, tg = group(b, g - 1)
                        if within(to):
                            store_out(to, tg // 2)

            for g in range(3):
                sp.wait_ge(q_clear, g + 1)
                sp.wait_ge(k_clear, g + 1)
                load_stacks(0, g)
            sp.wait_ge(q_clear, NG)
            sp.wait_ge(k_clear, NG)
            store_guard(0, 0)
            load_guard(0, 0)
            batches(sp, body)
            store_out(LAST, 1)
            sp.wait_ge(o_stored, B * 2 * 16)

        @block.gpsimd
        def _(pool):
            for g in range(NG):
                nc.gpsimd.memset(kst[0:KS, g].bitcast(F32), 0.0).then_inc(k_clear, 1)
            pool.wait_ge(k_clear, NG)
            nc.gpsimd.memset(kst[KS:KM].bitcast(F32), 1.0).then_inc(init, 1)
            pool.wait_ge(init, 1)
            for k in range(2):
                nc.gpsimd.memset(vaug[k][:], 0.0).then_inc(init, 1)
            pool.wait_ge(init, 3)
            for k in range(2):
                for s in range(2):
                    last = nc.gpsimd.memset(vaug[k][:, s, :, :, 9 * s + DH], 1.0)
            last.then_inc(init, 1)

            def place_values(b, hf):
                for s in range(2):
                    h0 = (2 * hf + s) * GH
                    src = V[:, bass.ds(b * T, T), h0 * DH:(h0 + GH) * DH].rearrange("p t (j d) -> p t j d", d=DH)
                    last = nc.gpsimd.tensor_copy(vaug[hf][:, s, :, :, 9 * s:9 * s + DH], src)
                last.then_inc(v_ready, 1)

            def hide_future(b, g, j):
                pool.wait_ge(p_ready, b * 32 + (g * GH + j) * 2 + 2)
                pool.sem_inc(passed, 1)
                row = probs[g % 2][:, j]
                for blocks in (row[:, 0:1024].rearrange("p (two w) -> p two w", two=2)[:, :, 0:P],
                               row[:, 896:896 + 2 * P].rearrange("p (two w) -> p two w", two=2)):
                    last = nc.gpsimd.affine_select(blocks, blocks, [[0, 2], [1, P]], compare_op=ALU.is_ge, fill=0.0,
                                                   base=0, channel_multiplier=-1)
                last.then_inc(masked, 1)

            def body(b):
                for g in range(NG):
                    if g < 2:
                        if positive(b):
                            pool.wait_ge(pv_done, b * NG * T - NG * T + (2 * g + 2) * T)
                        place_values(b, g)
                    if causal:
                        for j in range(GH):
                            hide_future(b, g, j)
            batches(pool, body)

        @block.vector
        def _(dve):
            for g in range(NG):
                nc.vector.memset(qst[0:KS, g].bitcast(F32), 0.0).then_inc(q_clear, 1)
            if causal:
                dve.wait_ge(masks_loaded, 16)
                nc.vector.tensor_copy(maskb[:], maskf[:])
                nc.vector.tensor_copy(identb[:], ident[:]).then_inc(masks_ready, 1)

            def largest(b, g, j, t):
                n = (g * GH + j) * T + t
                dve.wait_ge(s_ready, b * 64 + n + 1)
                keys = P * (t + 1) if causal else S
                nc.vector.tensor_reduce(nm[:, g, j * T + t:j * T + t + 1], s_bank[n % SR][:, 0:keys], AXX, ALU.max,
                                        negate=True).then_inc(s_used, 1)

            def cut_guard(b, g, step):
                n = b * NG + g
                if step == 0:
                    dve.wait_ge(s_used, b * 64 + (g + 1) * GH * T)
                    if positive(n):
                        dve.wait_ge(mT_ready, n)
                    nc.vector.tensor_copy(cut[:, 0], nm[:, g]).then_inc(mh_ready, 1)
                if step == 1:
                    dve.wait_ge(mh_ready, n + 1)
                    nc.vector.tensor_tensor(cut[:, 1], nm[:, g], cut[:, 0].bitcast(F32), ALU.subtract).then_inc(ml_ready, 1)
                if step == 2:
                    dve.wait_ge(ml_ready, n + 1)
                    if positive(n):
                        dve.wait_ge(m_stored, n * 16)
                    nc.vector.transpose(cutT[:].bitcast(F32), cut[:].rearrange("p h n -> p (h n)").bitcast(F32)).then_inc(mT_ready, 1)

            def body(b):
                for g in range(NG):
                    for j in range(GH):
                        for t in range(T):
                            to, tg = group(b, g + 2)
                            if within(to):
                                largest(to, tg, j, t)
                            to, tg = group(b, g + 1)
                            if within(to) and j == 0:
                                cut_guard(to, tg, t)

            for g in range(2):
                for j in range(GH):
                    for t in range(T):
                        largest(0, g, j, t)
                        if g == 1 and j == 0:
                            cut_guard(0, 0, t)
            batches(dve, body)

        @block.scalar
        def _(act):
            def exponentials(b, g, j):
                for u in range(2):
                    act.wait_ge(st_ready, b * 32 + (g * GH + j) * 2 + u + 1)
                    nc.scalar.activation(probs[g % 2][:, j, u * units[0]:u * units[0] + units[u]],
                                         st_bank[u][:, 0:units[u]], ACT.Exp).then_inc(p_ready, 1)

            def keep_out(b, hf):
                act.wait_ge(pv_done, b * NG * T + (2 * hf + 2) * T)
                if not (isinstance(b, int) and b * 2 + hf == 0):
                    act.wait_ge(o_stored, (b * 2 + hf) * 16)
                nc.scalar.activation(oe[:], o_bank[:], ACT.Copy).then_inc(o_ready, 1)

            def body(b):
                for g in range(NG):
                    if not (isinstance(b, int) and b * NG + g < 2):
                        act.wait_ge(pv_done, b * NG * T + g * T - T)
                    for j in range(GH):
                        exponentials(b, g, j)
                    if g % 2 == 0:
                        to, tg = group(b, g - 1)
                        if within(to):
                            keep_out(to, tg // 2)

            batches(act, body)
            keep_out(LAST, 1)

        @block.tensor
        def _(pe):
            pe.wait_ge(init, 4)
            if causal:
                pe.wait_ge(masks_ready, 1)

            def score(b, g, j, t):
                n = (g * GH + j) * T + t
                before = b * 64 + (n if n == 0 else n - SR + 1)
                if positive(before):
                    pe.wait_ge(s_used, before)
                keys = P * (t + 1) if causal else S
                out = s_bank[n % SR]
                last = nc.tensor.matmul(out[:, 0:keys], qst[0:KS, g, j, t * P:(t + 1) * P], kst[0:KS, g, j, 0:keys],
                                        start=True, stop=not causal)
                if causal:
                    last = nc.tensor.matmul(out[:, keys - P:keys], identb[:], maskb[:], start=False, stop=True)
                last.then_inc(s_ready, 1)

            def scores_by_key(b, g, j, u):
                if not (isinstance(b, int) and b * NG * GH + g * GH + j == 0):
                    pe.wait_ge(p_ready, b * 32 + (g * GH + j) * 2 + u - 1)
                for c in order[u]:
                    lo = place[c][1]
                    last = nc.tensor.matmul(st_bank[u][:, lo:lo + width[c]], kst[:, g, j, c * P:(c + 1) * P],
                                            qst[:, g, j, S - width[c]:S], start=True, stop=True)
                last.then_inc(st_ready, 1)

            def weigh_values(b, g, c):
                if c == 0:
                    if causal:
                        pe.wait_ge(masked, b * NG * GH + (g + 1) * GH)
                    else:
                        pe.wait_ge(p_ready, b * 32 + (g + 1) * GH * 2)
                    if g % 2 == 0:
                        pe.wait_ge(v_ready, b * 2 + g // 2 + 1)
                        if not (isinstance(b, int) and b * 2 + g // 2 == 0):
                            pe.wait_ge(o_ready, b * 2 + g // 2)
                s = g % 2
                for j in range(GH):
                    last = nc.tensor.matmul(o_bank[32 * j:32 * j + 32, S - width[c]:S], vaug[g // 2][:, s, c, j, :],
                                            probs[s][:, j, at(c):at(c) + width[c]],
                                            start=s == 0 and c == 0, stop=s == 1 and c == T - 1)
                last.then_inc(pv_done, 1)

            def body(b):
                for g in range(NG):
                    for j in range(GH):
                        ahead, behind = group(b, g + 2), group(b, g - 1)
                        if j == 0:
                            pe.wait_ge(m_loaded, (b * NG + g + 1) * 32)
                            if within(ahead[0]):
                                pe.wait_ge(stack[ahead[1]], (ahead[0] + 1) * NL * 16)
                        for u in range(2):
                            if within(ahead[0]):
                                score(*ahead, j, 2 * u)
                            scores_by_key(b, g, j, u)
                            if within(ahead[0]):
                                score(*ahead, j, 2 * u + 1)
                            if within(behind[0]) and (j and u == 0 or j == GH - 1):
                                weigh_values(*behind, j - 1 + u)

            for g in range(2):
                pe.wait_ge(stack[g], NL * 16)
                for j in range(GH):
                    for t in range(T):
                        score(0, g, j, t)
            batches(pe, body)
            for c in range(T):
                weigh_values(LAST, NG - 1, c)


def attention_out(nc, X, Y, ident, w, outs, rope):
    ctx = ExitStack()
    layer = "rope_" if rope else "ctx_"
    with ctx:
        sb = lambda name, shape, dt=F32: ctx.enter_context(nc.sbuf_tensor(layer + "ao_" + name, shape, dt))
        sems = []

        def sem(name):
            sems.append(ctx.enter_context(nc.semaphore(layer + "ao_" + name)))
            return sems[-1]

        lanes = range(WIDE)
        sb2 = lambda name, shape, dt=F32: [sb(f"{name}{L}", shape, dt) for L in lanes]
        sem2 = lambda name: [sem(f"{name}{L}") for L in lanes]
        banks = [[ctx.enter_context(nc.psum_tensor(f"{layer}ao_bank{L}{i}", [P, 512], F32)) for i in range(2)] for L in lanes]
        wo = sb("wo", [P, D])
        loads = [(wo, w["WoT"])]
        if rope:
            bo, gain, shift = sb("bo", [P, D]), sb("gain", [P, D]), sb("shift", [P, D])
            loads += [(bo, w["out_proj_b"]), (gain, w["ln1_w"]), (shift, w["ln1_b"])]
            yb = sb2("yb", [P, T, D])
        oe, rc = sb2("oe", [P, 2, S]), sb2("rc", [P, 2, 2, T, GH])
        o, oT, r, z = sb2("o", [P, T, D]), sb2("oT", [P, S]), sb2("r", [P, T, D]), sb2("z", [P, T, D])
        stats, mv, rstd = sb2("stats", [P, T, 6]), sb2("mv", [P, T, 2]), sb2("rstd", [P, T])
        half = sb("half", [P, T])
        loaded, half_ready, dve_steps, passed = sem("loaded"), sem("half_ready"), sem("dve_steps"), sem("passed")
        in_ready, turned, o_ready, yb_ready = sem2("in_ready"), sem2("turned"), sem2("o_ready"), sem2("yb_ready")
        oT_ps, oT_ready, wo_ps, x_ready = sem2("oT_ps"), sem2("oT_ready"), sem2("wo_ps"), sem2("x_ready")
        var_ready, rstd_ready = sem2("var_ready"), sem2("rstd_ready")
        PER = WIDE * (4 + 3 + 3 * T + (2 if rope else 0))
        ctx.callback(clear, nc, sems)
        block = ctx.enter_context(nc.Block())

        @block.sync
        def _(sp):
            for dst, src in loads:
                sp.dma_start(dst[:], src).then_inc(loaded, 16)
            for L in lanes:
                sp.dma_start(oe[L][:], outs[L].rearrange("k p s -> p k s")).then_inc(in_ready[L], 16)
            with sp.Fori(1, B // WIDE) as i:
                for L in lanes:
                    sp.wait_ge(turned[L], i * 2)
                    sp.sem_inc(passed, 1)
                    sp.dma_start(oe[L][:], outs[i * WIDE + L].rearrange("k p s -> p k s")).then_inc(in_ready[L], 16)
            for L in lanes:
                sp.wait_ge(x_ready[L], B // WIDE)

        @block.gpsimd
        def _(pool):
            nc.gpsimd.memset(half[:], -0.5).then_inc(half_ready, 1)
            pool.wait_ge(half_ready, 1)
            pool.wait_ge(loaded, 16 * len(loads))
            with pool.Fori(0, B // WIDE) as i:
                if rope:
                    for L in lanes:
                        nc.gpsimd.tensor_tensor(yb[L][:], Y[:, bass.ds((i * WIDE + L) * T, T), :], bc(bo[:], T),
                                                ALU.add).then_inc(yb_ready[L], 1)
                for L in lanes:
                    pool.wait_ge(var_ready[L], i + 1)
                    nc.gpsimd.tensor_tensor(rstd[L][:], mv[L][:, :, 1], half[:], ALU.pow).then_inc(rstd_ready[L], 1)

        @block.tensor
        def _(pe):
            pe.wait_ge(loaded, 16 * len(loads))
            with pe.Fori(0, B // WIDE) as i:
                for L in lanes:
                    pe.wait_ge(in_ready[L], i * 16 + 16)
                    for hf in range(2):
                        for t in range(T):
                            last = nc.tensor.transpose(banks[L][hf][:, t * P:(t + 1) * P], oe[L][:, hf, t * P:(t + 1) * P], ident[:])
                        last.then_inc(turned[L], 1)
                for L in lanes:
                    pe.wait_ge(o_ready[L], i + 1)
                    for t in range(T):
                        last = nc.tensor.transpose(banks[L][0][:, t * P:(t + 1) * P], o[L][:, t, :], ident[:])
                    last.then_inc(oT_ps[L], 1)
                for L in lanes:
                    pe.wait_ge(oT_ready[L], i + 1)
                    for t in range(T):
                        last = nc.tensor.matmul(banks[L][1][:, t * P:(t + 1) * P], oT[L][:, t * P:(t + 1) * P], wo[:],
                                                start=True, stop=True)
                    last.then_inc(wo_ps[L], 1)
                for L in lanes:
                    pe.wait_ge(x_ready[L], i + 1)

        @block.scalar
        def _(act):
            with act.Fori(0, B // WIDE) as i:
                for L in lanes:
                    act.wait_ge(oT_ps[L], i + 1)
                    nc.scalar.activation(oT[L][:], banks[L][0][:], ACT.Copy).then_inc(oT_ready[L], 1)

        @block.vector
        def _(dve):
            ch = Chain(dve, dve_steps, PER, passed)
            dve.wait_ge(loaded, 16 * len(loads))
            with dve.Fori(0, B // WIDE) as i:
                ch.start(i)
                own = [bass.ds((i * WIDE + L) * T, T) for L in lanes]
                rows = [[bank[:].rearrange("p (t j k) -> p t j k", t=T, k=32) for bank in banks[L]] for L in lanes]
                for L in lanes:
                    for hf in range(2):
                        dve.wait_ge(turned[L], i * 2 + hf + 1)
                        for s in range(2):
                            ch.do(nc.vector.reciprocal(rc[L][:, hf, s], rows[L][hf][:, :, :, 9 * s + DH]))
                ch.sync()
                for L in lanes:
                    for hf in range(2):
                        for s in range(2):
                            h0 = (2 * hf + s) * GH
                            dst = o[L][:, :, h0 * DH:(h0 + GH) * DH].rearrange("p t (j d) -> p t j d", d=DH)
                            last = nc.vector.tensor_tensor(dst, rows[L][hf][:, :, :, 9 * s:9 * s + DH], each(rc[L][:, hf, s], DH),
                                                           ALU.mult)
                            if hf * 2 + s < 3:
                                ch.do(last)
                    last.then_inc(o_ready[L], 1)
                src = [r[L] if rope else banks[L][1][:].rearrange("p (t d) -> p t d", t=T) for L in lanes]
                for L in lanes:
                    dve.wait_ge(wo_ps[L], i + 1)
                    if rope:
                        dve.wait_ge(yb_ready[L], i + 1)
                        ch.do(nc.vector.tensor_tensor(r[L][:], banks[L][1][:].rearrange("p (t d) -> p t d", t=T), yb[L][:], ALU.add))
                if rope:
                    ch.sync()
                for L in lanes:
                    for t in range(T):
                        ch.do(nc.vector.bn_stats(stats[L][:, t, :], src[L][:, t, :]))
                ch.sync()
                dve.sem_inc(passed, 1)
                for L in lanes:
                    for t in range(T):
                        ch.do(nc.vector.bn_aggr(mv[L][:, t, :], stats[L][:, t, :]))
                ch.sync()
                for L in lanes:
                    nc.vector.tensor_scalar_add(mv[L][:, :, 1], mv[L][:, :, 1], EPS).then_inc(var_ready[L], 1)
                for L in lanes:
                    dve.wait_ge(rstd_ready[L], i + 1)
                    ln_apply(nc, ch, z[L], src[L], mv[L], rstd[L])
                ch.sync()
                if rope:
                    for L in lanes:
                        ch.do(nc.vector.tensor_tensor(z[L][:], z[L][:], bc(gain[:], T), ALU.mult))
                    ch.sync()
                for L in lanes:
                    if rope:
                        last = nc.vector.tensor_tensor(Y[:, own[L], :], z[L][:], bc(shift[:], T), ALU.add)
                    else:
                        x = X[:, own[L], :]
                        last = nc.vector.tensor_tensor(x, x, z[L][:], ALU.add)
                    last.then_inc(x_ready[L], 1)
                for L in lanes:
                    dve.wait_ge(x_ready[L], i + 1)
                ch.end()


def attention_layer(nc, X, Y, ident, w, consts, rope):
    name = "rope" if rope else "ctx"
    halves = nc.dram_tensor(name + "_halves", [B, 4, P, S], F32, kind="Internal").ap()
    contexts = None if rope else nc.dram_tensor(name + "_contexts", [B, 4, CE, S], F32, kind="Internal").ap()
    guards = nc.dram_tensor(name + "_guards", [NG, P, 32], F32, kind="Internal").ap()
    outs = nc.dram_tensor(name + "_outs", [B, 2, P, S], F32, kind="Internal").ap()
    with nc.sbuf_tensor(name + "_V", [P, B * T, D], F32) as V:
        project_qkv(nc, X, Y, V, ident, w, consts, halves, contexts, rope)
        attend(nc, V, ident, consts, halves, contexts, guards, outs, rope)
    attention_out(nc, X, Y, ident, w, outs, rope)


def gate_tokens(nc, SRC, ident, w, consts, GATES, prefix, experts=None, halves=None, values=None):
    ctx = ExitStack()
    with ctx:
        sb = lambda name, shape, dt=F32: ctx.enter_context(nc.sbuf_tensor(prefix + name, shape, dt))
        sems = []
        lanes = range(WIDE)
        IT = B // WIDE

        def sem(name):
            sems.append(ctx.enter_context(nc.semaphore(prefix + name)))
            return sems[-1]

        sb2 = lambda name, shape, dt=F32: [sb(f"{name}{L}", shape, dt) for L in lanes]
        sem2 = lambda name: [sem(f"{name}{L}") for L in lanes]
        y_bank = [ctx.enter_context(nc.psum_tensor(f"{prefix}y_bank{L}", [P, 512], F32)) for L in lanes]
        small = [ctx.enter_context(nc.psum_tensor(f"{prefix}small{L}", [P, 512], F32)) for L in lanes]
        gw, order = sb("gw", [P, NE]), sb("order", [P, NE])
        loads = [(gw, w["gateT"]), (order, consts["order"])]
        if halves is None:
            gb, eb = sb("gb", [P, NE]), sb("eb", [NE, D])
            loads += [(gb, w["gate_b"]), (eb, w["expert_b"])]
            gl, gT = sb2("gl", [P, T, NE]), sb2("gT", [NE, S])
        else:
            stage = [sb(f"stage{k}", [P, 3, 512]) for k in range(2)]
            high, low = experts
        y, yf = sb2("y", [P, T, D]), sb2("yf", [P, S])
        stats, mv, rstd = sb2("stats", [P, T, 6]), sb2("mv", [P, T, 2]), sb2("rstd", [P, T])
        half = sb("half", [P, T])
        lg, tmp = sb("lg", [P, B * T, NE]), sb("tmp", [P, B * T, NE])
        hot, red = sb("hot", [P, 2, B * T, NE]), sb("red", [P, B * T, 2])

        loaded, half_ready, passed, dve_steps = sem("loaded"), sem("half_ready"), sem("passed"), sem("dve_steps")
        staged = [sem(f"staged{k}") for k in range(2)]
        high_ready, low_ready = sem("high_ready"), sem("low_ready")
        var_ready, rstd_ready, y_ready = sem2("var_ready"), sem2("rstd_ready"), sem2("y_ready")
        yT_ps, yf_ready, yT_kept, gate_ps = sem2("yT_ps"), sem2("yf_ready"), sem2("yT_kept"), sem2("gate_ps")
        lg_ready, e_ready, gates_ready = sem("lg_ready"), sem("e_ready"), sem("gates_ready")
        gl_ready, gT_ps, gT_ready, bias_ps, biased = sem2("gl_ready"), sem2("gT_ps"), sem2("gT_ready"), sem2("bias_ps"), sem2("biased")
        PER = (WIDE * (3 * T - 1) + WIDE if halves else 0) + WIDE
        ctx.callback(clear, nc, sems)
        block = ctx.enter_context(nc.Block())

        @block.sync
        def _(sp):
            for dst, src in loads:
                sp.dma_start(dst[:], src).then_inc(loaded, 16)

            def stage_in(e, k):
                sp.dma_start(stage[k][:, 0, :], w["w1"][e]).then_inc(staged[k], 16)
                sp.dma_start(stage[k][:, 1, :], w["w3"][e]).then_inc(staged[k], 16)
                sp.dma_start(stage[k][:, 2, :], w["w2"][e].rearrange("p c d -> p (c d)")).then_inc(staged[k], 16)
            if halves:
                stage_in(0, 0)
                stage_in(1, 1)
                for e in range(2, NE + 1):
                    sp.wait_ge(high_ready, e - 1)
                    sp.wait_ge(low_ready, e - 1)
                    stage_in(e, e % 2)

        @block.gpsimd
        def _(pool):
            nc.gpsimd.memset(half[:], -0.5).then_inc(half_ready, 1)
            pool.wait_ge(half_ready, 1)
            if halves:
                nc.gpsimd.memset(GATES[:, :, NE:NE + 1], 1.0 / NE).then_inc(half_ready, 1)
                with pool.Fori(0, IT) as i:
                    for L in lanes:
                        pool.wait_ge(var_ready[L], i + 1)
                        nc.gpsimd.tensor_tensor(rstd[L][:], mv[L][:, :, 1], half[:], ALU.pow).then_inc(rstd_ready[L], 1)

        @block.scalar
        def _(act):
            def cut_high(e, k, turn):
                act.wait_ge(staged[k], 48 * turn)
                nc.scalar.activation(high[:, bass.ds(e, 1)], stage[k][:].unsqueeze(1), ACT.Copy).then_inc(high_ready, 1)

            with act.Fori(0, IT) as i:
                for L in lanes:
                    to = bass.ds((i * WIDE + L) * S, S)
                    act.wait_ge(yT_ps[L], i + 1)
                    nc.scalar.activation(yf[L][:], y_bank[L][:], ACT.Copy).then_inc(yf_ready[L], 1)
                    kept = halves[0][:, to] if halves else values[:, to]
                    nc.scalar.activation(kept, y_bank[L][:], ACT.Copy).then_inc(yT_kept[L], 1)
                if halves:
                    for L in lanes:
                        cut_high(i * WIDE + L, L % 2, i * 2 + L // 2 + 1)
            if halves:
                cut_high(NE, 0, NE // 2 + 1)
            act.wait_ge(lg_ready, 1)
            nc.scalar.activation(lg[:], lg[:], ACT.Exp).then_inc(e_ready, 1)
            if not halves:
                with act.Fori(0, IT) as i:
                    for L in lanes:
                        act.wait_ge(gT_ps[L], i + 1)
                        nc.scalar.activation(gT[L][:], small[L][0:NE, :], ACT.Copy).then_inc(gT_ready[L], 1)

        @block.vector
        def _(dve):
            ch = Chain(dve, dve_steps, PER, passed)
            dve.wait_ge(loaded, 16 * len(loads))

            def cut_low(e, k):
                dve.wait_ge(high_ready, e + 1)
                nc.vector.tensor_tensor(low[:, bass.ds(e, 1)], stage[k][:].unsqueeze(1), high[:, bass.ds(e, 1)].bitcast(F32),
                                        ALU.subtract).then_inc(low_ready, 1)

            with dve.Fori(0, IT) as i:
                ch.start(i)
                tiles = [bass.ds((i * WIDE + L) * T, T) for L in lanes]
                if halves:
                    for L in lanes:
                        x = SRC[:, tiles[L], :]
                        for t in range(T):
                            ch.do(nc.vector.bn_stats(stats[L][:, t, :], x[:, t, :]))
                    ch.sync()
                    dve.sem_inc(passed, 1)
                    for L in lanes:
                        for t in range(T):
                            ch.do(nc.vector.bn_aggr(mv[L][:, t, :], stats[L][:, t, :]))
                    ch.sync()
                    for L in lanes:
                        nc.vector.tensor_scalar_add(mv[L][:, :, 1], mv[L][:, :, 1], EPS).then_inc(var_ready[L], 1)
                    for L in lanes:
                        x = SRC[:, tiles[L], :]
                        dve.wait_ge(rstd_ready[L], i + 1)
                        for t in range(T):
                            last = nc.vector.tensor_scalar(y[L][:, t, :], x[:, t, :], mv[L][:, t, 0:1], rstd[L][:, t:t + 1],
                                                           ALU.subtract, ALU.mult)
                            if t < T - 1:
                                ch.do(last)
                        last.then_inc(y_ready[L], 1)
                    for L in lanes:
                        to = bass.ds((i * WIDE + L) * S, S)
                        dve.wait_ge(yT_kept[L], i + 1)
                        ch.do(nc.vector.tensor_tensor(halves[1][:, to], yf[L][:], halves[0][:, to].bitcast(F32), ALU.subtract))
                    for L in lanes:
                        cut_low(i * WIDE + L, L % 2)
                else:
                    for L in lanes:
                        nc.vector.tensor_copy(y[L][:], SRC[:, tiles[L], :]).then_inc(y_ready[L], 1)
                for L in lanes:
                    dve.wait_ge(gate_ps[L], i + 1)
                    logits = small[L][:, 0:T * NE].rearrange("p (t e) -> p t e", e=NE)
                    if halves:
                        ch.do(nc.vector.tensor_copy(lg[:, tiles[L], :], logits))
                    else:
                        ch.do(nc.vector.tensor_tensor(lg[:, tiles[L], :], logits, bc(gb[:], T), ALU.add))
                ch.sync()
                ch.end()
            if halves:
                cut_low(NE, 0)
                dve.wait_ge(half_ready, 2)
            ch.start(0, IT * PER)
            ch.sync()
            ch.do(nc.vector.tensor_reduce(red[:, :, 0], lg[:], AXX, ALU.max))
            ch.sync()
            nc.vector.tensor_tensor(lg[:], lg[:], each(red[:, :, 0], NE), ALU.subtract).then_inc(lg_ready, 1)
            dve.wait_ge(e_ready, 1)
            ch.do(nc.vector.tensor_reduce(red[:, :, 1], lg[:], AXX, ALU.add))
            ch.sync()
            ch.do(nc.vector.reciprocal(red[:, :, 0], red[:, :, 1]))
            ch.sync()
            ch.do(nc.vector.tensor_tensor(lg[:], lg[:], each(red[:, :, 0], NE), ALU.mult))
            ch.sync()
            route(nc, ch, lg, order, tmp, red, hot, GATES).then_inc(gates_ready, 1)
            if not halves:
                dve.wait_ge(gates_ready, 1)
                with dve.Fori(0, IT) as i:
                    for L in lanes:
                        nc.vector.tensor_copy(gl[L][:], GATES[:, bass.ds((i * WIDE + L) * T, T), :]).then_inc(gl_ready[L], 1)
                    for L in lanes:
                        own = SRC[:, bass.ds((i * WIDE + L) * T, T), :]
                        dve.wait_ge(bias_ps[L], i + 1)
                        nc.vector.tensor_tensor(own, y_bank[L][:].rearrange("p (t d) -> p t d", t=T), own, ALU.add).then_inc(biased[L], 1)

        @block.tensor
        def _(pe):
            pe.wait_ge(loaded, 16 * len(loads))
            with pe.Fori(0, IT) as i:
                for L in lanes:
                    pe.wait_ge(y_ready[L], i + 1)
                    for t in range(T):
                        last = nc.tensor.transpose(y_bank[L][:, t * P:(t + 1) * P], y[L][:, t, :], ident[:])
                    last.then_inc(yT_ps[L], 1)
                for L in lanes:
                    pe.wait_ge(yf_ready[L], i + 1)
                    for t in range(T):
                        last = nc.tensor.matmul(small[L][:, t * NE:(t + 1) * NE], yf[L][:, t * P:(t + 1) * P], gw[:],
                                                start=True, stop=True)
                    last.then_inc(gate_ps[L], 1)
                for L in lanes:
                    pe.wait_ge(yT_kept[L], i + 1)
            if not halves:
                pe.wait_ge(lg_ready, 1)
                with pe.Fori(0, IT) as i:
                    for L in lanes:
                        pe.wait_ge(gl_ready[L], i + 1)
                        for t in range(T):
                            last = nc.tensor.transpose(small[L][0:NE, t * P:(t + 1) * P], gl[L][:, t, :], ident[:])
                        last.then_inc(gT_ps[L], 1)
                    for L in lanes:
                        pe.wait_ge(gT_ready[L], i + 1)
                        for t in range(T):
                            last = nc.tensor.matmul(y_bank[L][:, t * P:(t + 1) * P], gT[L][:, t * P:(t + 1) * P], eb[:],
                                                    start=True, stop=True)
                        last.then_inc(bias_ps[L], 1)
                    for L in lanes:
                        pe.wait_ge(biased[L], i + 1)


def route(nc, ch, probs, order, tmp, red, hot, gates):
    each8 = lambda ap: each(ap, NE)
    for k in range(2):
        ch.do(nc.vector.tensor_reduce(red[:, :, 0], probs[:] if k == 0 else tmp[:], AXX, ALU.max))
        ch.sync()
        ch.do(nc.vector.tensor_tensor(hot[:, k], probs[:] if k == 0 else tmp[:], each8(red[:, :, 0]), ALU.is_equal))
        ch.sync()
        ch.do(nc.vector.tensor_tensor(hot[:, k], hot[:, k], bc(order[:], probs.shape[1]), ALU.mult))
        ch.sync()
        ch.do(nc.vector.tensor_reduce(red[:, :, 1], hot[:, k], AXX, ALU.max))
        ch.sync()
        ch.do(nc.vector.tensor_tensor(hot[:, k], hot[:, k], each8(red[:, :, 1]), ALU.is_equal))
        ch.sync()
        if k == 0:
            ch.do(nc.vector.scalar_tensor_tensor(tmp[:], hot[:, 0], -2.0, probs[:], ALU.mult, ALU.add))
            ch.sync()
    ch.do(nc.vector.tensor_tensor(hot[:, 0], hot[:, 0], hot[:, 1], ALU.add))
    ch.sync()
    return nc.vector.tensor_tensor(gates[:, :, 0:NE], hot[:, 0], probs[:], ALU.mult)


ROUTE_STEPS = 12


def mixture_layer(nc, X, Y, ident, w, consts):
    ctx = ExitStack()
    with ctx:
        gates = ctx.enter_context(nc.sbuf_tensor("mo_gates", [P, B * T, NE], F32))
        YT = ctx.enter_context(nc.sbuf_tensor("mo_YT", [P, B * S], F32))
        gate_tokens(nc, Y, ident, w, consts, gates, "mg_", values=YT)
        sems = []

        def sem(name):
            sems.append(ctx.enter_context(nc.semaphore("mo_" + name)))
            return sems[-1]

        lanes = range(LANES)
        sb = lambda name, shape, dt=F32: ctx.enter_context(nc.sbuf_tensor("mo_" + name, shape, dt))
        sb2 = lambda name, shape, dt=F32: [sb(f"{name}{L}", shape, dt) for L in lanes]
        sem2 = lambda name: [sem(f"{name}{L}") for L in lanes]
        pb = [[ctx.enter_context(nc.psum_tensor(f"mo_pb{L}{i}", [P, 1024], F32)) for i in range(2)] for L in lanes]
        we, gain, shift = sb("we", [P, NE * D]), sb("gain", [P, D]), sb("shift", [P, D])
        loads = [(we, w["expertT"]), (gain, w["ln2_w"]), (shift, w["ln2_b"])]
        yT, g = sb2("yT", [P, S]), sb2("g", [P, T, NE])
        acc, z = sb2("acc", [P, T, D]), sb2("z", [P, T, D])
        stats, mv, rstd = sb2("stats", [P, T, 6]), sb2("mv", [P, T, 2]), sb2("rstd", [P, T])
        half = sb("half", [P, T])
        loaded, half_ready, passed = sem("loaded"), sem("half_ready"), sem("passed")
        yT_ready, ex_ps, ex_used, dve_steps = sem2("yT_ready"), sem2("ex_ps"), sem2("ex_used"), sem2("dve_steps")
        var_ready, rstd_ready, z_ready, z_done = sem2("var_ready"), sem2("rstd_ready"), sem2("z_ready"), sem2("z_done")
        scaled = sem2("scaled")
        PER = 1 + T * NE - 2 + 6 * T - 1 + 1
        ctx.callback(clear, nc, sems)
        block = ctx.enter_context(nc.Block())

        @block.sync
        def _(sp):
            for dst, src in loads:
                sp.dma_start(dst[:], src).then_inc(loaded, 16)

        @block.gpsimd
        def _(pool):
            nc.gpsimd.memset(half[:], -0.5).then_inc(half_ready, 1)
            pool.wait_ge(half_ready, 1)
            pool.wait_ge(loaded, 16 * len(loads))
            with pool.Fori(0, B // LANES) as i:
                def rsqrt(L, k):
                    pool.wait_ge(var_ready[L], i * 2 + k + 1)
                    nc.gpsimd.tensor_tensor(rstd[L][:], mv[L][:, :, 1], half[:], ALU.pow).then_inc(rstd_ready[L], 1)
                for L in lanes:
                    rsqrt(L, 0)
                for L in lanes:
                    pool.wait_ge(z_ready[L], i + 1)
                    nc.gpsimd.tensor_tensor(z[L][:], z[L][:], bc(gain[:], T), ALU.mult).then_inc(scaled[L], 1)
                    pool.wait_ge(scaled[L], i + 1)
                    nc.gpsimd.tensor_tensor(z[L][:], z[L][:], bc(shift[:], T), ALU.add).then_inc(z_done[L], 1)
                for L in lanes:
                    rsqrt(L, 1)

        @block.vector
        def _(dve):
            ch = [Chain(dve, dve_steps[L], PER, passed) for L in lanes]
            dve.wait_ge(loaded, 16 * len(loads))
            with dve.Fori(0, B // LANES) as i:
                tiles = [bass.ds((i * LANES + L) * T, T) for L in lanes]

                def combine(pair):
                    for L in lanes:
                        dve.wait_ge(ex_ps[L], i * 2 + pair + 1)
                    for e in range(NE):
                        for L in lanes:
                            ch[L].sync()
                            for k in range(2):
                                t = 2 * pair + k
                                before = Y[:, tiles[L], :][:, t, :] if e == 0 else acc[L][:, t, :]
                                last = nc.vector.scalar_tensor_tensor(acc[L][:, t, :], pb[L][k][:, e * D:(e + 1) * D],
                                                                      g[L][:, t, e:e + 1], before, ALU.mult, ALU.add)
                                if k == 0 or e < NE - 1:
                                    ch[L].do(last)
                            if e == NE - 1:
                                last.then_inc(ex_used[L], 1)

                for L in lanes:
                    ch[L].start(i)
                    ch[L].do(nc.vector.tensor_copy(g[L][:], gates[:, tiles[L], :]))
                combine(0)
                combine(1)

                for L in lanes:
                    dve.wait_ge(ex_used[L], i * 2 + 2)
                    ln_stats(nc, ch[L], acc[L], stats[L], mv[L]).then_inc(var_ready[L], 1)
                for L in lanes:
                    dve.wait_ge(rstd_ready[L], i * 2 + 1)
                    for t in range(T):
                        last = nc.vector.tensor_scalar(z[L][:, t, :], acc[L][:, t, :], mv[L][:, t, 0:1], rstd[L][:, t:t + 1],
                                                       ALU.subtract, ALU.mult)
                        if t < T - 1:
                            ch[L].do(last)
                    last.then_inc(z_ready[L], 1)
                for L in lanes:
                    dve.wait_ge(z_done[L], i + 1)
                    ln_stats(nc, ch[L], z[L], stats[L], mv[L]).then_inc(var_ready[L], 1)
                for L in lanes:
                    dve.wait_ge(rstd_ready[L], i * 2 + 2)
                    ln_apply(nc, ch[L], acc[L], z[L], mv[L], rstd[L])
                for L in lanes:
                    ch[L].sync()
                    x = X[:, tiles[L], :]
                    ch[L].do(nc.vector.tensor_tensor(x, x, acc[L][:], ALU.add))
                for L in lanes:
                    ch[L].sync()
                    ch[L].end()

        @block.scalar
        def _(act):
            with act.Fori(0, B // LANES) as i:
                for L in lanes:
                    nc.scalar.activation(yT[L][:], YT[:, bass.ds((i * LANES + L) * S, S)], ACT.Copy).then_inc(yT_ready[L], 1)
                for L in lanes:
                    act.wait_ge(ex_ps[L], i * 2 + 2)

        @block.tensor
        def _(pe):
            pe.wait_ge(loaded, 16 * len(loads))
            with pe.Fori(0, B // LANES) as i:
                for pair in range(2):
                    for L in lanes:
                        if pair == 0:
                            pe.wait_ge(yT_ready[L], i + 1)
                        else:
                            pe.wait_ge(ex_used[L], i * 2 + 1)
                        for k in range(2):
                            t = 2 * pair + k
                            for half_row in range(2):
                                cols = slice(half_row * 512, (half_row + 1) * 512)
                                last = nc.tensor.matmul(pb[L][k][:, cols], yT[L][:, t * P:(t + 1) * P], we[:, cols],
                                                        start=True, stop=True)
                        last.then_inc(ex_ps[L], 1)
                for L in lanes:
                    pe.wait_ge(ex_used[L], i * 2 + 2)


def swiglu_layer(nc, X, ident, w, consts):
    N = NE + 1
    RING, LAG = 4, 3
    FINISH = 7
    ER = 3
    ctx = ExitStack()
    with ctx:
        sb = lambda name, shape, dt=F32: ctx.enter_context(nc.sbuf_tensor("sw_" + name, shape, dt))
        high, low = sb("high", [P, N, 3, 512], F32R), sb("low", [P, N, 3, 512], F32R)
        YH, YL = sb("YH", [P, B * S], F32R), sb("YL", [P, B * S], F32R)
        GATES = sb("GATES", [P, B * T, N])
        gate_tokens(nc, X, ident, w, consts, GATES, "sg_", experts=(high, low), halves=(YH, YL))
        sems = []

        def sem(name):
            sems.append(ctx.enter_context(nc.semaphore("sw_" + name)))
            return sems[-1]

        ps = lambda name: ctx.enter_context(nc.psum_tensor("sw_" + name, [P, 512], F32))
        g_bank, u_bank = [ps(f"g{k}") for k in range(2)], [ps(f"u{k}") for k in range(2)]
        d_bank, turned = [ps(f"d{k}") for k in range(ER)], ps("turned")
        silu = [sb(f"silu{k}", [P, S]) for k in range(2)]
        hf = [sb(f"hf{k}", [P, S]) for k in range(RING)]
        hh = [sb(f"hh{k}", [P, S], F32R) for k in range(RING)]
        hl = [sb(f"hl{k}", [P, S], F32R) for k in range(RING)]
        gates, dT = sb("gates", [P, T, N]), sb("dT", [P, S])
        acc, y = sb("acc", [P, T, D]), sb("y", [P, T, D])
        stats, mv = sb("stats", [P, T, 6]), sb("mv", [P, T, 2])
        half, rstd = sb("half", [P, T]), sb("rstd", [P, T])

        half_ready, passed = sem("half_ready"), sem("passed")
        g_ps, u_ps, silu_ready, h_ready = sem("g_ps"), sem("u_ps"), sem("silu_ready"), sem("h_ready")
        hh_ready, hl_ready, d_used = sem("hh_ready"), sem("hl_ready"), sem("d_used")
        dT_ready, dt_ps, added = sem("dT_ready"), sem("dt_ps"), sem("added")
        var_ready, rstd_ready, dve_steps = sem("var_ready"), sem("rstd_ready"), sem("dve_steps")
        NC = N * FC
        assert NC % RING == 0 and NC % 2 == 0 and N % ER == 0

        def batches(eng, body):
            body(0)
            with eng.Fori(1, B) as b:
                body(b)

        ctx.callback(clear, nc, sems)
        block = ctx.enter_context(nc.Block())

        @block.gpsimd
        def _(pool):
            nc.gpsimd.memset(half[:], -0.5).then_inc(half_ready, 1)
            pool.wait_ge(half_ready, 1)

            def rsqrt(b):
                pool.wait_ge(var_ready, b + 1)
                nc.gpsimd.tensor_tensor(rstd[:], mv[:, :, 1], half[:], ALU.pow).then_inc(rstd_ready, 1)

            def body(b):
                for n in range(NC):
                    pool.wait_ge(hh_ready, b * NC + n + 1)
                    nc.gpsimd.tensor_tensor(hl[n % RING][:], hf[n % RING][:], hh[n % RING][:].bitcast(F32),
                                            ALU.subtract).then_inc(hl_ready, 1)
                    if n == FINISH and not isinstance(b, int):
                        rsqrt(b - 1)
            batches(pool, body)
            rsqrt(B - 1)

        @block.scalar
        def _(act):
            def high_half(m, k):
                act.wait_ge(h_ready, m + 1)
                if positive(m - RING + 1):
                    act.wait_ge(d_used, m - RING + 1)
                nc.scalar.activation(hh[k][:], hf[k][:], ACT.Copy).then_inc(hh_ready, 1)

            def fetch(e, k):
                act.wait_ge(d_used, e * FC + FC)
                if positive(e):
                    act.wait_ge(dt_ps, e)
                nc.scalar.activation(dT[:], d_bank[k][:], ACT.Copy).then_inc(dT_ready, 1)

            def body(b):
                for n in range(NC):
                    m, e = b * NC + n, b * N + n // FC
                    act.wait_ge(g_ps, m + 1)
                    if positive(m - 1):
                        act.wait_ge(h_ready, m - 1)
                    nc.scalar.activation(silu[n % 2][:], g_bank[n % 2][:], ACT.Silu).then_inc(silu_ready, 1)
                    if positive(m):
                        high_half(m - 1, (n - 1) % RING)
                    if n % FC == 3 and positive(e):
                        fetch(e - 1, (n // FC - 1) % ER)
            batches(act, body)
            high_half(B * NC - 1, (NC - 1) % RING)
            fetch(B * N - 1, (N - 1) % ER)

        @block.vector
        def _(dve):
            first = 1 + (N - 2) * (T - 1)
            per = 1 + N * (T - 1) + 3 * T + 2
            ch = Chain(dve, dve_steps, per, passed)
            dve.wait_ge(half_ready, 1)

            def gated(m, n):
                dve.wait_ge(silu_ready, m + 1)
                dve.wait_ge(u_ps, m + 1)
                if positive(m - RING + 1):
                    dve.wait_ge(hl_ready, m - RING + 1)
                nc.vector.tensor_tensor(hf[n % RING][:], silu[n % 2][:], u_bank[n % 2][:], ALU.mult).then_inc(h_ready, 1)

            def add(b, e):
                dve.wait_ge(dt_ps, b * N + e + 1)
                if positive(b * N + e):
                    dve.wait_ge(added, b * N + e)
                if e == 0:
                    ch.do(nc.vector.tensor_copy(gates[:], GATES[:, bass.ds(b * T, T), :]))
                if not isinstance(b, int) or ch.n or ch.base:
                    ch.sync()
                for t in range(T):
                    src = turned[:, t * P:(t + 1) * P]
                    if e == 0:
                        last = nc.vector.tensor_scalar(acc[:, t, :], src, gates[:, t, 0:1], None, ALU.mult)
                    else:
                        last = nc.vector.scalar_tensor_tensor(acc[:, t, :], src, gates[:, t, e:e + 1], acc[:, t, :],
                                                              ALU.mult, ALU.add)
                    if t < T - 1:
                        ch.do(last)
                last.then_inc(added, 1)

            def moments(b):
                dve.wait_ge(added, b * N + N)
                ch.do(nc.vector.tensor_scalar_mul(acc[:], acc[:], 0.5))
                ch.sync()
                ln_stats(nc, ch, acc, stats, mv).then_inc(var_ready, 1)

            def normalised(b):
                dve.wait_ge(rstd_ready, b + 1)
                ln_apply(nc, ch, y, acc, mv, rstd)

            def residual(b):
                x = X[:, bass.ds(b * T, T), :]
                ch.sync()
                ch.do(nc.vector.tensor_tensor(x, x, y[:], ALU.add))

            def body(b):
                inner = not isinstance(b, int)
                for n in range(NC):
                    gated(b * NC + n, n)
                    e = n // FC - 2
                    if n % FC == 2 and (inner or e >= 0):
                        add(b if e >= 0 else b - 1, e % N)
                    if inner and n == FINISH:
                        moments(b - 1)
                    if inner and n == FINISH + 2:
                        normalised(b - 1)
                    if inner and n == FINISH + 4:
                        residual(b - 1)
            ch.start(0)
            body(0)
            assert ch.n == first
            with dve.Fori(1, B) as b:
                ch.start(b, first - per)
                body(b)
                ch.end()
            ch.start(0, first + (B - 1) * per)
            add(B - 1, N - 2)
            add(B - 1, N - 1)
            moments(B - 1)
            normalised(B - 1)
            residual(B - 1)

        @block.tensor
        def _(pe):
            both = lambda e, k, c: [h[:, e, k, c * P:(c + 1) * P] for h in (high, low)]

            def up(b, n):
                m = b * NC + n
                if positive(m - 1):
                    pe.wait_ge(silu_ready, m - 1)
                    pe.wait_ge(h_ready, m - 1)
                tokens = [half[:, bass.ds(b * S, S)] for half in (YH, YL)]
                mm3(nc, g_bank[n % 2][:], both(n // FC, 0, n % FC), tokens).then_inc(g_ps, 1)
                mm3(nc, u_bank[n % 2][:], both(n // FC, 1, n % FC), tokens).then_inc(u_ps, 1)

            def down(b, n):
                e, c = n % NC // FC, n % FC
                pe.wait_ge(hl_ready, b * NC + n + 1)
                if c == 0 and positive(b * N + n // FC - ER + 1):
                    pe.wait_ge(dT_ready, b * N + n // FC - ER + 1)
                mm3(nc, d_bank[e % ER][:], both(e, 2, c), (hh[n % RING][:], hl[n % RING][:]), start=c == 0,
                    stop=c == FC - 1).then_inc(d_used, 1)

            def turn(e):
                pe.wait_ge(dT_ready, e + 1)
                if positive(e):
                    pe.wait_ge(added, e)
                for t in range(T):
                    last = nc.tensor.transpose(turned[:, t * P:(t + 1) * P], dT[:, t * P:(t + 1) * P], ident[:])
                last.then_inc(dt_ps, 1)

            def body(b):
                inner = not isinstance(b, int)
                for n in range(NC):
                    up(b, n)
                    if inner or n >= LAG:
                        down(b, n - LAG)
                    if n % FC == 0 and (inner or n >= 2 * FC):
                        turn(b * N + n // FC - 2)
            batches(pe, body)
            for n in range(NC, NC + LAG):
                down(B - 1, n - LAG)
            turn(B * N - 2)
            turn(B * N - 1)


def build(nc, dram, out):
    ctx = ExitStack()
    with ctx:
        X = ctx.enter_context(nc.sbuf_tensor("X", [P, B * T, D], F32))
        ident = ctx.enter_context(nc.sbuf_tensor("ident", [P, P], F32))
        x_loaded = ctx.enter_context(nc.semaphore("x_loaded"))
        x_stored = ctx.enter_context(nc.semaphore("x_stored"))
        x_dram = dram["video"].rearrange("b (t p) d -> p (b t) d", p=P)
        with nc.Block() as block:
            @block.sync
            def _(sp):
                sp.dma_start(ident[:], dram["ident"]).then_inc(x_loaded, 16)
                sp.dma_start(X[:], x_dram).then_inc(x_loaded, 16)
                sp.wait_ge(x_loaded, 32)

        w = lambda prefix: {k[len(prefix):]: v for k, v in dram.items() if k.startswith(prefix)}
        performer_layer(nc, X, ident, w("L0_attn_"), dram)
        with nc.sbuf_tensor("Y", [P, B * T, D], F32) as Y:
            attention_layer(nc, X, Y, ident, w("L0_ffn_"), dram, True)
            mixture_layer(nc, X, Y, ident, w("L0_ffn_"), dram)
        attention_layer(nc, X, None, ident, w("L1_attn_"), dram, False)
        swiglu_layer(nc, X, ident, w("L1_ffn_"), dram)
        with nc.Block() as block:
            @block.sync
            def _(sp):
                sp.dma_start(out.rearrange("b (t p) d -> p (b t) d", p=P), X[:]).then_inc(x_stored, 16)
                sp.wait_ge(x_stored, 16)



def layouts(i):
    import numpy as np
    i = {k: np.asarray(v) for k, v in i.items()}
    con = np.ascontiguousarray
    rows = lambda a: con(np.broadcast_to(a.reshape(1, -1), (P, a.size)))
    col = lambda a: con(a.reshape(-1, P).T)
    chunks = lambda a: con(a.reshape(-1, P, a.shape[-1]).transpose(1, 0, 2))
    d = {"video": i["L0_attn_video"]}
    p = "L0_attn_"
    for n in ("Wq", "Wk", "Wv", "Wo", "W1"):
        d[p + n + "T"] = con(i[p + n].T)
    d[p + "W2T"] = chunks(i[p + "W2"].T)
    d[p + "projT"] = con(i[p + "proj"].T)
    for n in ("bq", "bk", "b1"):
        d[p + n] = col(i[p + n])
    for n in ("bv", "bo", "b2", "g2", "be2", "g3", "be3"):
        d[p + n] = rows(i[p + n])
    p = "L0_ffn_"
    for n, k in (("q", 0), ("k", 1), ("v", 2)):
        d[p + "W" + n + "T"] = con(i[p + "in_proj_w"][k * D:(k + 1) * D].T)
        d[p + "b" + n] = (rows if n == "v" else col)(i[p + "in_proj_b"][k * D:(k + 1) * D])
    d[p + "WoT"] = con(i[p + "out_proj_w"].T)
    d[p + "gateT"] = con(i[p + "gate_w"].T)
    d[p + "expertT"] = con(i[p + "expert_w"].transpose(2, 0, 1)).reshape(D, NE * D)
    d[p + "expert_b"] = i[p + "expert_b"]
    for n in ("out_proj_b", "gate_b", "ln1_w", "ln1_b", "ln2_w", "ln2_b"):
        d[p + n] = rows(i[p + n])
    p = "L1_attn_"
    for n in ("Wq", "Wk", "Wv", "Wo", "We"):
        d[p + n + "T"] = con(i[p + n].T)
    p = "L1_ffn_"
    d[p + "gateT"] = con(i[p + "gate_W"].T)
    for n in ("w1", "w3"):
        d[p + n] = con(np.concatenate([i[p + n + "_e"], i[p + n + "_s"].transpose(1, 0, 2).reshape(1, D, F)]))
    d[p + "w2"] = con(np.concatenate([i[p + "w2_e"], i[p + "w2_s"].reshape(1, F, D)])
                      .reshape(NE + 1, FC, P, D).transpose(0, 2, 1, 3))
    f = np.float32
    r = np.arange(P)
    d["ident"] = np.eye(P, dtype=f)
    d["hsel"] = (r[:, None] // DH == np.arange(32)[None]).astype(f)
    d["bmask"] = ((r[:, None] % 32) // DH == r[None] // M).astype(f)
    d["causal"] = np.where(r[None] > r[:, None], f(-1e30), f(0))
    d["order"] = np.broadcast_to(np.arange(NE, 0, -1, dtype=f), (P, NE)).copy()
    inv = 1.0 / 10000.0 ** (np.arange(0, DH, 2, dtype=f) / f(DH))
    ang = np.arange(S, dtype=f)[:, None] * inv[None].astype(f)
    cos, sin = np.cos(ang).astype(f), np.sin(ang).astype(f)
    full = lambda a: con(np.tile(a, (1, H)).reshape(T, P, D).transpose(1, 0, 2)).astype(f)
    d["rope_cos"] = full(np.repeat(cos, 2, axis=1))
    d["rope_sin"] = full(np.stack([-sin, sin], axis=-1).reshape(S, DH))
    return d


def kernel(**inputs):
    import numpy as np
    import concourse.bacc as bacc
    from concourse.bass_utils import run_bass_kernel_spmd

    nc = bacc.Bacc("TRN2", target_bir_lowering=False, num_devices=1)
    arrays = layouts(inputs)
    dram = {k: nc.dram_tensor("in_" + k, a.shape, mybir.dt.from_np(a.dtype), kind="ExternalInput").ap()
            for k, a in arrays.items()}
    out = nc.dram_tensor("out", (B, S, D), F32, kind="ExternalOutput").ap()
    build(nc, dram, out)
    r = run_bass_kernel_spmd(nc, [{"in_" + k: a for k, a in arrays.items()}], core_ids=[0])
    return r.results[0]["out"]
```

```python
from contextlib import ExitStack

import concourse.bass as bass
from concourse import mybir

F32 = mybir.dt.float32
F32R = mybir.dt.float32r
BF16 = mybir.dt.bfloat16
ALU = mybir.AluOpType
ACT = mybir.ActivationFunctionType
AXX = mybir.AxisListType.X
RMAX = bass.bass_isa.ReduceOp.max

B, S, D = 8, 512, 128
P = 128
T = S // P
H, DH = 16, 8
M = 32
F = 512
FC = F // P
NE = 8
LANES = 2
WIDE = 4
EPS = 1e-5
EPS_K = 1e-4
SCALE = DH ** -0.5




class Chain:

    def __init__(self, eng, sem, per, passed):
        self.eng, self.sem, self.per, self.passed = eng, sem, per, passed
        self.b, self.n, self.base = 0, 0, 0

    def start(self, b, base=0):
        self.b, self.n, self.base = b, 0, base

    def do(self, ins):
        self.n += 1
        return ins.then_inc(self.sem, 1)

    def sync(self, but=0):
        self.eng.wait_ge(self.sem, self.b * self.per + (self.base + self.n - but))

    def end(self):
        assert self.n == self.per, f"the chain signals {self.n} times an iteration"


def bc(ap, n):
    return ap.unsqueeze(1).broadcast_to([ap.shape[0], n, ap.shape[1]])


def each(ap, n):
    return ap.unsqueeze(len(ap.shape)).broadcast_to(list(ap.shape) + [n])


def ln_stats(nc, ch, src, stats, mv):
    for t in range(T):
        ch.do(nc.vector.bn_stats(stats[:, t, :], src[:, t, :]))
    ch.sync()
    ch.eng.sem_inc(ch.passed, 1)
    for t in range(T):
        ch.do(nc.vector.bn_aggr(mv[:, t, :], stats[:, t, :]))
    ch.sync()
    return nc.vector.tensor_scalar_add(mv[:, :, 1], mv[:, :, 1], EPS)


def wide_stats(nc, ch, src, stats, mv):
    n = len(src)
    for L in range(n + 1):
        if L < n:
            for t in range(T):
                ch.do(nc.vector.bn_stats(stats[L][:, t, :], src[L][:, t, :]))
        if L:
            ch.sync(but=T if L < n else 0)
            ch.eng.sem_inc(ch.passed, 1)
            for t in range(T):
                ch.do(nc.vector.bn_aggr(mv[L - 1][:, t, :], stats[L - 1][:, t, :]))
            ch.sync()
            yield nc.vector.tensor_scalar_add(mv[L - 1][:, :, 1], mv[L - 1][:, :, 1], EPS)


def ln_apply(nc, ch, dst, src, mv, rstd):
    for t in range(T):
        ch.do(nc.vector.tensor_scalar(dst[:, t, :], src[:, t, :], mv[:, t, 0:1], rstd[:, t:t + 1],
                                      ALU.subtract, ALU.mult))


def mm3(nc, out, a, b, start=True, stop=True):
    nc.tensor.matmul(out, a[0], b[0], start=start, stop=False)
    nc.tensor.matmul(out, a[0], b[1], start=False, stop=False)
    return nc.tensor.matmul(out, a[1], b[0], start=False, stop=stop)


def positive(value):
    return not isinstance(value, int) or value > 0


def clear(nc, sems):
    with nc.Block() as block:
        @block.gpsimd
        def _(pool):
            numbers = sorted(sem.num for sem in sems)
            start = 0
            for n in range(1, len(numbers) + 1):
                if n == len(numbers) or numbers[n] != numbers[n - 1] + 1:
                    pool.sem_clear(range(numbers[start], numbers[n - 1] + 1))
                    start = n


def performer_layer(nc, X, ident, w, consts):
    ctx = ExitStack()
    with ctx:
        sems = []

        def sem(name):
            sems.append(ctx.enter_context(nc.semaphore("pf_" + name)))
            return sems[-1]

        sb = lambda name, shape, dt=F32: ctx.enter_context(nc.sbuf_tensor("pf_" + name, shape, dt))
        sb2 = lambda name, shape, dt=F32: [sb(f"{name}{L}", shape, dt) for L in range(LANES)]
        sem2 = lambda name: [sem(f"{name}{L}") for L in range(LANES)]
        banks = [[ctx.enter_context(nc.psum_tensor(f"pf_bank{L}{i}", [P, 512], F32)) for i in range(4)]
                 for L in range(LANES)]

        wq, wk, wv, wo = (sb(n, [P, D]) for n in ("wq", "wk", "wv", "wo"))
        w1 = sb("w1", [P, F])
        w2 = sb("w2", [P, FC, D])
        bq, bk = sb("bq", [P, 1]), sb("bk", [P, 1])
        b1 = sb("b1", [P, FC])
        bv, bo, b2, g2, be2, g3, be3 = (sb(n, [P, D]) for n in ("bv", "bo", "b2", "g2", "be2", "g3", "be3"))
        feats = sb("feats", [P, H * M])
        hsel = sb("hsel", [P, 32])
        bmask = sb("bmask", [P, P])
        ones = sb("ones", [P, 32])
        half = sb("half", [P, T])
        stats, mv, rstd = sb2("stats", [P, T, 6]), sb2("mv", [P, T, 2]), sb2("rstd", [P, T])
        y, yb, yT = sb2("y", [P, T, D]), sb2("yb", [P, T, D]), sb2("yT", [P, S])
        qT, kT, sqq, sqk = (sb2(n, [P, S]) for n in ("qT", "kT", "sqq", "sqk"))
        v = sb2("v", [P, T, D])
        dgT, dg = sb2("dgT", [64, S]), sb2("dg", [P, T, 64])
        kmx, km, stab = sb2("kmx", [P, T, H]), sb2("km", [P, H]), sb2("stab", [P, H])
        ck, qmx, cq = sb2("ck", [P, T, H]), sb2("qmx", [P, T, H]), sb2("cq", [P, T, H])
        kp, qp = sb2("kp", [P, T, H * M]), sb2("qp", [P, T, H * M])
        cm, cx = sb2("cm", [P, 2, P]), sb2("cx", [P, 2, P])
        qpT = sb2("qpT", [P, T, S])
        rd, oT = sb2("rd", [P, S]), sb2("oT", [P, S])
        r, x1, x1b, x1T = sb2("r", [P, T, D]), sb2("x1", [P, T, D]), sb2("x1b", [P, T, D]), sb2("x1T", [P, S])
        hT = sb2("hT", [P, FC, S])

        first_loaded, x_loaded = sem("first_loaded"), sem("x_loaded")
        loaded, projected, init, half_ready = sem("loaded"), sem("projected"), sem("init"), sem("half_ready")
        passed = sem("passed")
        var_ready, rstd_ready = sem2("var_ready"), sem2("rstd_ready")
        y_ready, yb_ready, yT_ps, yT_ready = sem2("y_ready"), sem2("yb_ready"), sem2("yT_ps"), sem2("yT_ready")
        qkv_ps, qk_ready, v_ready = sem2("qkv_ps"), sem2("qk_ready"), sem2("v_ready")
        dg_ps, dgT_ready, dgt_ps, dg_ready = sem2("dg_ps"), sem2("dgT_ready"), sem2("dgt_ps"), sem2("dg_ready")
        kx_ps, kx_used, kx_kept = sem2("kx_ps"), sem2("kx_used"), sem2("kx_kept")
        qx_ps, qx_used = sem2("qx_ps"), sem2("qx_used")
        km_ready, stab_ready, kz_ready = sem2("km_ready"), sem2("stab_ready"), sem2("kz_ready")
        ke_ready, qe_ready, kp_ready, qp_ready = sem2("ke_ready"), sem2("qe_ready"), sem2("kp_ready"), sem2("qp_ready")
        cm_ps, cm_ready, cx_ps, cx_ready = sem2("cm_ps"), sem2("cm_ready"), sem2("cx_ps"), sem2("cx_ready")
        qpT_ps, qpT_ready, nd_ps, oT_ready = sem2("qpT_ps"), sem2("qpT_ready"), sem2("nd_ps"), sem2("oT_ready")
        wo_ps, wo_used, x1_ready, x1b_ready = sem2("wo_ps"), sem2("wo_used"), sem2("x1_ready"), sem2("x1b_ready")
        x1T_ps, x1T_ready, h_ps, h_ready, w2_ps = sem2("x1T_ps"), sem2("x1T_ready"), sem2("h_ps"), sem2("h_ready"), sem2("w2_ps")
        dve_steps, r_ready = sem2("dve_steps"), sem2("r_ready")
        PER = 4 * 3 * T - 1 + 2 * 2 + 6

        first_loads = [(wq, w["WqT"]), (wk, w["WkT"]), (wv, w["WvT"]), (bq, w["bq"]), (bk, w["bk"]),
                       (hsel, consts["hsel"]), (bv, w["bv"])]
        loads = [(bo, w["bo"]), (bmask, consts["bmask"]), (wo, w["WoT"]), (g2, w["g2"]), (be2, w["be2"]),
                 (w1, w["W1T"]), (b1, w["b1"]), (w2, w["W2T"]), (b2, w["b2"]), (g3, w["g3"]), (be3, w["be3"])]
        lanes = range(LANES)
        feat = lambda ap: ap.rearrange("p (h m) -> p h m", m=M)
        tokens = lambda bank: bank[:].rearrange("p (t d) -> p t d", t=T)

        STEPS = B // LANES

        def ahead(i):
            return 0 if isinstance(i, int) else 1

        def steps(eng, body):
            with eng.Fori(0, STEPS - 1) as i:
                body(i)
            body(STEPS - 1)

        ctx.callback(clear, nc, sems)
        block = ctx.enter_context(nc.Block())

        @block.sync
        def _(sp):
            late = slice(LANES * T, B * T)
            sp.dma_start(X[:, late, :], consts["video"].rearrange("b (t p) d -> p (b t) d", p=P)[:, late, :]).then_inc(x_loaded, 16)
            for dst, src in first_loads:
                sp.dma_start(dst[:], src).then_inc(first_loaded, 16)
            sp.wait_ge(init, 1)
            for h in range(H):
                sp.dma_start(feats[h * DH:(h + 1) * DH, h * M:(h + 1) * M], w["projT"]).then_inc(projected, 16)
            for dst, src in loads:
                sp.dma_start(dst[:], src).then_inc(loaded, 16)

        @block.gpsimd
        def _(pool):
            nc.gpsimd.memset(feats[:], 0.0).then_inc(init, 1)
            nc.gpsimd.memset(ones[:], 1.0).then_inc(init, 1)
            nc.gpsimd.memset(half[:], -0.5).then_inc(half_ready, 1)
            pool.wait_ge(half_ready, 1)

            def rsqrt(L, norm):
                pool.wait_ge(var_ready[L], norm + 1)
                nc.gpsimd.tensor_tensor(rstd[L][:], mv[L][:, :, 1], half[:], ALU.pow).then_inc(rstd_ready[L], 1)

            def body(i):
                pool.wait_ge(loaded, 16 * len(loads))
                for L in lanes:
                    pool.wait_ge(y_ready[L], i + 1)
                    nc.gpsimd.tensor_tensor(yb[L][:], y[L][:], bc(bo[:], T), ALU.add).then_inc(yb_ready[L], 1)
                for L in lanes:
                    pool.wait_ge(km_ready[L], i + 1)
                    pool.sem_inc(passed, 1)
                    nc.gpsimd.partition_all_reduce(stab[L][:], km[L][:], P, RMAX).then_inc(stab_ready[L], 1)
                for pair in range(2):
                    two = slice(2 * pair, 2 * pair + 2)
                    pool.wait_ge(qe_ready[0], i * 2 + pair + 1)
                    pool.sem_inc(passed, 1)
                    last = nc.gpsimd.tensor_scalar(qp[0][:, two], qp[0][:, two], EPS_K, M ** -0.5, ALU.add, ALU.mult)
                last.then_inc(qp_ready[0], 1)
                pool.wait_ge(ke_ready[0], i + 1)
                pool.sem_inc(passed, 1)
                nc.gpsimd.tensor_scalar(kp[0][:], kp[0][:], EPS_K, M ** -0.5, ALU.add, ALU.mult).then_inc(kp_ready[0], 1)
                for L in lanes:
                    rsqrt(L, i * 4 + 1)
                if ahead(i):
                    for L in lanes:
                        rsqrt(L, i * 4 + 2)
                for L in lanes:
                    pool.wait_ge(x1_ready[L], i + 1)
                    nc.gpsimd.tensor_tensor(x1b[L][:], x1[L][:], bc(b2[:], T), ALU.add).then_inc(x1b_ready[L], 1)
                for k in range(2):
                    for L in lanes:
                        rsqrt(L, i * 4 + 2 + ahead(i) + k)

            for L in lanes:
                rsqrt(L, 0)
            steps(pool, body)

        @block.vector
        def _(dve):
            ch = [Chain(dve, dve_steps[L], PER, passed) for L in lanes]
            def moments(L, src):
                ln_stats(nc, ch[L], src, stats[L], mv[L]).then_inc(var_ready[L], 1)

            def normalised(L, norm, dst, src):
                dve.wait_ge(rstd_ready[L], norm + 1)
                ln_apply(nc, ch[L], dst, src, mv[L], rstd[L])
                ch[L].sync()

            def kept(tile, exp_ready, count, ready):
                dve.wait_ge(exp_ready[1], count)
                nc.vector.tensor_scalar(tile[1][:], tile[1][:], EPS_K, M ** -0.5, ALU.add, ALU.mult).then_inc(ready[1], 1)

            def first_norm(i, norm):
                x = [X[:, bass.ds((i * LANES + L) * T, T), :] for L in lanes]
                for L in lanes:
                    moments(L, x[L])
                for L in lanes:
                    dve.wait_ge(rstd_ready[L], norm + 1)
                    for t in range(T):
                        last = nc.vector.tensor_scalar(y[L][:, t, :], x[L][:, t, :], mv[L][:, t, 0:1],
                                                       rstd[L][:, t:t + 1], ALU.subtract, ALU.mult)
                        if t < T - 1:
                            ch[L].do(last)
                    last.then_inc(y_ready[L], 1)

            def body(i):
                for L in lanes:
                    ch[L].start(i, BEFORE)
                x = [X[:, bass.ds((i * LANES + L) * T, T), :] for L in lanes]

                def affine(L, tile, gain, shift):
                    ch[L].do(nc.vector.tensor_tensor(tile[:], tile[:], bc(gain[:], T), ALU.mult))
                    ch[L].sync()
                    return nc.vector.tensor_tensor(tile[:], tile[:], bc(shift[:], T), ALU.add)

                for L in lanes:
                    dve.wait_ge(qkv_ps[L], i * 3 + 3)
                    nc.vector.tensor_tensor(v[L][:], tokens(banks[L][3]), bc(bv[:], T), ALU.add).then_inc(v_ready[L], 1)
                dve.wait_ge(loaded, 16 * len(loads))
                for L in lanes:
                    dve.wait_ge(dgt_ps[L], i + 1)
                    nc.vector.tensor_copy(dg[L][:], banks[L][1][:, 0:T * 64].rearrange("p (t k) -> p t k", t=T)
                                          ).then_inc(dg_ready[L], 1)
                for t in range(T):
                    for L in lanes:
                        dve.wait_ge(kx_ps[L], i * T + t + 1)
                        nc.vector.tensor_reduce(kmx[L][:, t, :], feat(banks[L][2 + t % 2][:]), AXX,
                                                ALU.max).then_inc(kx_used[L], 1)
                for L in lanes:
                    dve.wait_ge(kx_used[L], i * T + T)
                    nc.vector.tensor_reduce(km[L][:], kmx[L][:].rearrange("p t h -> p h t"), AXX,
                                            ALU.max).then_inc(km_ready[L], 1)
                for pair in range(2):
                    for L in lanes:
                        for t in (2 * pair, 2 * pair + 1):
                            dve.wait_ge(qx_ps[L], i * T + t + 1)
                            last = nc.vector.tensor_reduce(qmx[L][:, t, :], feat(banks[L][t % 2][:]), AXX, ALU.max)
                        ch[L].do(last)
                    for L in lanes:
                        ch[L].sync()
                        two = slice(2 * pair, 2 * pair + 2)
                        ch[L].do(nc.vector.tensor_tensor(cq[L][:, two], qmx[L][:, two], dg[L][:, two, 0:H], ALU.add))
                    for L in lanes:
                        ch[L].sync()
                        for t in (2 * pair, 2 * pair + 1):
                            nc.vector.tensor_tensor(feat(qp[L][:, t, :]), feat(banks[L][t % 2][:]), each(cq[L][:, t, :], M),
                                                    ALU.subtract).then_inc(qx_used[L], 1)
                for L in lanes:
                    dve.wait_ge(stab_ready[L], i + 1)
                    ch[L].do(nc.vector.tensor_tensor(ck[L][:], dg[L][:, :, 32:32 + H], bc(stab[L][:], T), ALU.add))
                for L in lanes:
                    ch[L].sync()
                    dve.wait_ge(kx_kept[L], i * T + T)
                    keys = kp[L][:].rearrange("p t (h m) -> p (t h) m", m=M)
                    nc.vector.tensor_tensor(keys, keys, each(ck[L][:].rearrange("p t h -> p (t h)"), M),
                                            ALU.subtract).then_inc(kz_ready[L], 1)
                    if L == 0:
                        kept(qp, qe_ready, i * 2 + 2, qp_ready)
                kept(kp, ke_ready, i + 1, kp_ready)
                for L in lanes:
                    dve.wait_ge(cm_ps[L], i + 1)
                    nc.vector.tensor_tensor(cm[L][:, 0, :], banks[L][2][:, 0:P], bmask[:], ALU.mult)
                    nc.vector.tensor_tensor(cm[L][:, 1, :], banks[L][3][:, 0:P], bmask[:], ALU.mult).then_inc(cm_ready[L], 1)
                for L in lanes:
                    dve.wait_ge(nd_ps[L], i + 1)
                    ch[L].do(nc.vector.reciprocal(rd[L][:], banks[L][1][:]))
                    ch[L].sync()
                    nc.vector.tensor_tensor(oT[L][:], banks[L][0][:], rd[L][:], ALU.mult).then_inc(oT_ready[L], 1)
                for L in lanes:
                    dve.wait_ge(wo_ps[L], i + 1)
                    dve.wait_ge(yb_ready[L], i + 1)
                    nc.vector.tensor_tensor(r[L][:], tokens(banks[L][2]), yb[L][:], ALU.add).then_inc(wo_used[L], 1)
                for L in lanes:
                    dve.wait_ge(wo_used[L], i + 1)
                    moments(L, r[L])
                for L in lanes:
                    normalised(L, i * 4 + 1, x1[L], r[L])
                for L in lanes:
                    affine(L, x1[L], g2, be2).then_inc(x1_ready[L], 1)
                if ahead(i):
                    dve.wait_ge(x_loaded, 16)
                    first_norm(i + 1, i * 4 + 2)
                for L in lanes:
                    dve.wait_ge(w2_ps[L], i + 1)
                    dve.wait_ge(x1b_ready[L], i + 1)
                    nc.vector.tensor_tensor(r[L][:], tokens(banks[L][0]), x1b[L][:], ALU.add).then_inc(r_ready[L], 1)
                for L in lanes:
                    dve.wait_ge(r_ready[L], i + 2)
                    moments(L, r[L])
                for L in lanes:
                    normalised(L, i * 4 + 2 + ahead(i), x1[L], r[L])
                for L in lanes:
                    ch[L].do(affine(L, x1[L], g3, be3))
                for L in lanes:
                    ch[L].sync()
                    moments(L, x1[L])
                for L in lanes:
                    normalised(L, i * 4 + 3 + ahead(i), r[L], x1[L])
                for L in lanes:
                    ch[L].do(nc.vector.tensor_tensor(x[L], x[L], r[L][:], ALU.add))
                for L in lanes:
                    ch[L].sync()
                    if ahead(i):
                        ch[L].end()

            for L in lanes:
                ch[L].start(0)
                dve.sem_inc(r_ready[L], 1)
            first_norm(0, 0)
            BEFORE = ch[0].n
            dve.wait_ge(first_loaded, 16 * len(first_loads))
            dve.wait_ge(projected, 16 * H)
            dve.wait_ge(init, 2)
            nc.vector.tensor_scalar_mul(feats[:], feats[:], DH ** -0.25).then_inc(init, 1)
            steps(dve, body)

        @block.scalar
        def _(act):
            act.wait_ge(first_loaded, 16 * len(first_loads))

            def body(i):
                for L in lanes:
                    act.wait_ge(yT_ps[L], i + 1)
                    nc.scalar.activation(yT[L][:], banks[L][3][:], ACT.Copy).then_inc(yT_ready[L], 1)
                for L in lanes:
                    for k, (bias, lin, sq) in enumerate(((bq, qT, sqq), (bk, kT, sqk))):
                        act.wait_ge(qkv_ps[L], i * 3 + k + 1)
                        nc.scalar.activation(sq[L][:], banks[L][1 + k][:], ACT.Square, bias=bias[:])
                        nc.scalar.activation(lin[L][:], banks[L][1 + k][:], ACT.Identity, bias=bias[:]).then_inc(qk_ready[L], 1)
                for L in lanes:
                    act.wait_ge(dg_ps[L], i + 1)
                    nc.scalar.activation(dgT[L][:], banks[L][0][0:64, :], ACT.Copy, scale=0.5 * DH ** -0.5).then_inc(dgT_ready[L], 1)
                for t in range(T):
                    for L in lanes:
                        act.wait_ge(kx_used[L], i * T + t + 1)
                        nc.scalar.activation(kp[L][:, t, :], banks[L][2 + t % 2][:], ACT.Copy).then_inc(kx_kept[L], 1)
                for pair in range(2):
                    for L in lanes:
                        two = slice(2 * pair, 2 * pair + 2)
                        act.wait_ge(qx_used[L], i * T + 2 * pair + 2)
                        nc.scalar.activation(qp[L][:, two], qp[L][:, two], ACT.Exp).then_inc(qe_ready[L], 1)
                for L in lanes:
                    act.wait_ge(kz_ready[L], i + 1)
                    nc.scalar.activation(kp[L][:], kp[L][:], ACT.Exp).then_inc(ke_ready[L], 1)
                for g in range(3):
                    for L in lanes:
                        act.wait_ge(qpT_ps[L], i * T + g + 1)
                        nc.scalar.activation(qpT[L][:, g, :], banks[L][g % 2][:], ACT.Copy).then_inc(qpT_ready[L], 1)
                for L in lanes:
                    act.wait_ge(cx_ps[L], i + 1)
                    nc.scalar.activation(cx[L][:], banks[L][3][:, P:3 * P].rearrange("p (k m) -> p k m", k=2),
                                         ACT.Copy).then_inc(cx_ready[L], 1)
                for L in lanes:
                    act.wait_ge(qpT_ps[L], i * T + T)
                    nc.scalar.activation(qpT[L][:, 3, :], banks[L][1][:], ACT.Copy).then_inc(qpT_ready[L], 1)
                for L in lanes:
                    act.wait_ge(x1T_ps[L], i + 1)
                    nc.scalar.activation(x1T[L][:], banks[L][3][:], ACT.Copy).then_inc(x1T_ready[L], 1)
                act.wait_ge(loaded, 16 * len(loads))
                for c in range(FC):
                    for L in lanes:
                        act.wait_ge(h_ps[L], i * FC + c + 1)
                        nc.scalar.activation(hT[L][:, c, :], banks[L][c][:], ACT.Relu, bias=b1[:, c:c + 1]).then_inc(h_ready[L], 1)

            steps(act, body)

        @block.tensor
        def _(pe):
            pe.wait_ge(first_loaded, 16 * len(first_loads))
            pe.wait_ge(init, 2)
            tile = lambda ap, t: ap[:, t * P:(t + 1) * P]

            def transposed(bank, src, signal):
                for t in range(T):
                    last = nc.tensor.transpose(tile(bank, t), src[:, t, :], ident[:])
                last.then_inc(signal, 1)

            def body(i):
                for L in lanes:
                    pe.wait_ge(y_ready[L], i + 1)
                    transposed(banks[L][3], y[L], yT_ps[L])
                for L in lanes:
                    pe.wait_ge(yT_ready[L], i + 1)
                    nc.tensor.matmul(banks[L][1][:], wq[:], yT[L][:], start=True, stop=True).then_inc(qkv_ps[L], 1)
                    nc.tensor.matmul(banks[L][2][:], wk[:], yT[L][:], start=True, stop=True).then_inc(qkv_ps[L], 1)
                    for t in range(T):
                        last = nc.tensor.matmul(tile(banks[L][3], t), tile(yT[L], t), wv[:], start=True, stop=True)
                    last.then_inc(qkv_ps[L], 1)
                for L in lanes:
                    pe.wait_ge(qk_ready[L], i * 2 + 2)
                    pe.wait_ge(r_ready[L], i + 1)
                    nc.tensor.matmul(banks[L][0][0:32, :], hsel[:], sqq[L][:], start=True, stop=True)
                    nc.tensor.matmul(banks[L][0][32:64, :], hsel[:], sqk[L][:], start=True, stop=True).then_inc(dg_ps[L], 1)
                pe.wait_ge(init, 3)
                for t in range(2):
                    for L in lanes:
                        if t == 0:
                            pe.wait_ge(v_ready[L], i + 1)
                        nc.tensor.matmul(banks[L][2 + t][:], tile(kT[L], t), feats[:], start=True, stop=True).then_inc(kx_ps[L], 1)
                for L in lanes:
                    pe.wait_ge(dgT_ready[L], i + 1)
                    pe.sem_inc(passed, 1)
                    for t in range(T):
                        last = nc.tensor.transpose(banks[L][1][:, t * 64:(t + 1) * 64], tile(dgT[L], t), ident[0:64, 0:64])
                    last.then_inc(dgt_ps[L], 1)
                for t in range(2, T):
                    for L in lanes:
                        pe.wait_ge(kx_kept[L], i * T + t - 1)
                        nc.tensor.matmul(banks[L][t][:], tile(kT[L], t), feats[:], start=True, stop=True).then_inc(kx_ps[L], 1)
                for t in range(T):
                    for L in lanes:
                        if t == 0:
                            pe.wait_ge(dg_ready[L], i + 1)
                        if t >= 2:
                            pe.wait_ge(qx_used[L], i * T + t - 1)
                        nc.tensor.matmul(banks[L][t % 2][:], tile(qT[L], t), feats[:], start=True, stop=True).then_inc(qx_ps[L], 1)
                for g in range(2):
                    for L in lanes:
                        pe.wait_ge(qp_ready[L], i + 1)
                        for t in range(T):
                            last = nc.tensor.transpose(tile(banks[L][g], t), qp[L][:, t, g * P:(g + 1) * P], ident[:])
                        last.then_inc(qpT_ps[L], 1)
                for L in lanes:
                    pe.wait_ge(kp_ready[L], i + 1)
                    for bank, left in ((banks[L][2], lambda t, g: v[L][:, t, 32 * g:32 * g + 32]), (banks[L][3], lambda t, g: ones[:])):
                        for t in range(T):
                            for g in range(4):
                                last = nc.tensor.matmul(bank[32 * g:32 * g + 32, 0:P], left(t, g),
                                                        kp[L][:, t, g * P:(g + 1) * P], start=t == 0, stop=t == T - 1)
                    last.then_inc(cm_ps[L], 1)
                for L in lanes:
                    pe.wait_ge(qpT_ready[L], i * T + 1)
                    for t in range(T):
                        last = nc.tensor.transpose(tile(banks[L][0], t), qp[L][:, t, 2 * P:3 * P], ident[:])
                    last.then_inc(qpT_ps[L], 1)
                for L in lanes:
                    pe.wait_ge(cm_ready[L], i + 1)
                    for k in range(2):
                        last = nc.tensor.transpose(tile(banks[L][3], k + 1), cm[L][:, k, :], ident[:])
                    last.then_inc(cx_ps[L], 1)
                for L in lanes:
                    pe.wait_ge(qpT_ready[L], i * T + 2)
                    for t in range(T):
                        last = nc.tensor.transpose(tile(banks[L][1], t), qp[L][:, t, 3 * P:4 * P], ident[:])
                    last.then_inc(qpT_ps[L], 1)
                for L in lanes:
                    pe.wait_ge(cx_ready[L], i + 1)
                    pe.wait_ge(qpT_ready[L], i * T + T)
                    for k in range(2):
                        for g in range(4):
                            last = nc.tensor.matmul(banks[L][k][32 * g:32 * g + 32, :], cx[L][:, k, 32 * g:32 * g + 32],
                                                    qpT[L][:, g, :], start=True, stop=True)
                    last.then_inc(nd_ps[L], 1)
                pe.wait_ge(loaded, 16 * len(loads))
                for L in lanes:
                    pe.wait_ge(oT_ready[L], i + 1)
                    for t in range(T):
                        last = nc.tensor.matmul(tile(banks[L][2], t), tile(oT[L], t), wo[:], start=True, stop=True)
                    last.then_inc(wo_ps[L], 1)
                for L in lanes:
                    pe.wait_ge(x1_ready[L], i + 1)
                    transposed(banks[L][3], x1[L], x1T_ps[L])
                for L in lanes:
                    pe.wait_ge(x1T_ready[L], i + 1)
                    for c in range(FC):
                        nc.tensor.matmul(banks[L][c][:], tile(w1, c), x1T[L][:], start=True, stop=True).then_inc(h_ps[L], 1)
                for L in lanes:
                    pe.wait_ge(h_ready[L], i * FC + FC)
                    for t in range(T):
                        for c in range(FC):
                            last = nc.tensor.matmul(tile(banks[L][0], t), hT[L][:, c, t * P:(t + 1) * P], w2[:, c, :],
                                                    start=c == 0, stop=c == FC - 1)
                    last.then_inc(w2_ps[L], 1)
            steps(pe, body)


GH = 4
NG = H // GH
KS = 96
SR = 3
KM = KS + 2
CE = D // 8


def project_qkv(nc, X, Y, V, ident, w, consts, halves, contexts, rope):
    ctx = ExitStack()
    layer = "rope_" if rope else "ctx_"
    with ctx:
        sb = lambda name, shape, dt=F32: ctx.enter_context(nc.sbuf_tensor(layer + "pr_" + name, shape, dt))
        sems = []

        def sem(name):
            sems.append(ctx.enter_context(nc.semaphore(layer + "pr_" + name)))
            return sems[-1]

        lanes = range(WIDE)
        sb2 = lambda name, shape, dt=F32: [sb(f"{name}{L}", shape, dt) for L in lanes]
        sem2 = lambda name: [sem(f"{name}{L}") for L in lanes]
        banks = [[ctx.enter_context(nc.psum_tensor(f"{layer}pr_bank{L}{i}", [P, 512], F32)) for i in range(2)] for L in lanes]
        wq, wk, wv = (sb(n, [P, D]) for n in ("wq", "wk", "wv"))
        loads = [(wq, w["WqT"]), (wk, w["WkT"]), (wv, w["WvT"])]
        if rope:
            bq, bk, bv = sb("bq", [P, 1]), sb("bk", [P, 1]), sb("bv", [P, D])
            cos, sin = sb("cos", [P, T, D]), sb("sin", [P, T, D])
            loads += [(bq, w["bq"]), (bk, w["bk"]), (bv, w["bv"]), (cos, consts["rope_cos"]), (sin, consts["rope_sin"])]
            turned, rot = sb2("turned", [P, T, D]), sb2("rot", [P, T, D])
        else:
            we = sb("we", [P, CE])
            loads += [(we, w["WeT"])]
            c4 = sb2("c4", [CE, 4, S], F32R)
        stats, mv, rstd = sb2("stats", [P, T, 6]), sb2("mv", [P, T, 2]), sb2("rstd", [P, T])
        half = sb("half", [P, T])
        y, yT = sb2("y", [P, T, D]), sb2("yT", [P, S])
        rT = sb2("rT", [P, S]) if rope else None
        qk4 = sb2("qk4", [P, 4, S], F32R)

        loaded, half_ready = sem("loaded"), sem("half_ready")
        dve_steps, passed, free = sem("dve_steps"), sem("passed"), sem2("free")
        var_ready, rstd_ready, y_ready = sem2("var_ready"), sem2("rstd_ready"), sem2("y_ready")
        turn_ready, rot_ready = sem2("turn_ready"), sem2("rot_ready")
        yT_ps, rT_ps, yT_ready, rT_ready = sem2("yT_ps"), sem2("rT_ps"), sem2("yT_ready"), sem2("rT_ready")
        q_ps, k_ps, v_ps, c_ps = sem2("q_ps"), sem2("k_ps"), sem2("v_ps"), sem2("c_ps")
        q_ready, k_ready, c_ready = sem2("q_ready"), sem2("k_ready"), sem2("c_ready")
        low_ready, v_ready, stored, y_kept = sem2("low_ready"), sem2("v_ready"), sem2("stored"), sem2("y_kept")
        NQ = 2 if rope else 3
        NS = 16 if rope else 32
        PER = WIDE * (3 * T - 1) + WIDE
        ctx.callback(clear, nc, sems)
        block = ctx.enter_context(nc.Block())

        @block.sync
        def _(sp):
            for dst, src in loads:
                sp.dma_start(dst[:], src).then_inc(loaded, 16)
            for L in lanes:
                sp.sem_inc(free[L], 1)
            with sp.Fori(0, B // WIDE) as i:
                for L in lanes:
                    sp.wait_ge(low_ready[L], i * NQ + 2)
                    sp.sem_inc(passed, 1)
                    sp.dma_start(halves[i * WIDE + L].rearrange("k p s -> p k s"), qk4[L][:].bitcast(F32)).then_inc(stored[L], 16)
                if not rope:
                    for L in lanes:
                        sp.wait_ge(low_ready[L], i * NQ + 3)
                        sp.sem_inc(passed, 1)
                        sp.dma_start(contexts[i * WIDE + L].rearrange("k p s -> p k s"), c4[L][:].bitcast(F32)).then_inc(stored[L], 16)
                for L in lanes:
                    sp.wait_ge(stored[L], (i + 1) * NS)
                    sp.sem_inc(free[L], 1)

        @block.gpsimd
        def _(pool):
            nc.gpsimd.memset(half[:], -0.5).then_inc(half_ready, 1)
            pool.wait_ge(half_ready, 1)
            with pool.Fori(0, B // WIDE) as i:
                for L in lanes:
                    pool.wait_ge(var_ready[L], i + 1)
                    nc.gpsimd.tensor_tensor(rstd[L][:], mv[L][:, :, 1], half[:], ALU.pow).then_inc(rstd_ready[L], 1)
                if rope:
                    pool.wait_ge(loaded, 16 * len(loads))
                    for L in lanes:
                        pool.wait_ge(y_ready[L], i + 1)
                        pair = lambda t: t[:].rearrange("p t (k two) -> p (t k) two", two=2)
                        for m in range(2):
                            last = nc.gpsimd.tensor_tensor(pair(turned[L])[:, :, m], pair(y[L])[:, :, 1 - m],
                                                           pair(sin)[:, :, m], ALU.mult)
                        last.then_inc(turn_ready[L], 1)

        @block.vector
        def _(dve):
            ch = Chain(dve, dve_steps, PER, passed)
            with dve.Fori(0, B // WIDE) as i:
                ch.start(i)
                x = [X[:, bass.ds((i * WIDE + L) * T, T), :] for L in lanes]
                for L, last in enumerate(wide_stats(nc, ch, x, stats, mv)):
                    last.then_inc(var_ready[L], 1)
                for L in lanes:
                    dve.wait_ge(rstd_ready[L], i + 1)
                    for t in range(T):
                        last = nc.vector.tensor_scalar(y[L][:, t, :], x[L][:, t, :], mv[L][:, t, 0:1], rstd[L][:, t:t + 1],
                                                       ALU.subtract, ALU.mult)
                        if t < T - 1:
                            ch.do(last)
                    last.then_inc(y_ready[L], 1)
                dve.wait_ge(loaded, 16 * len(loads))
                if rope:
                    for L in lanes:
                        dve.wait_ge(y_ready[L], i + 1)
                        ch.do(nc.vector.tensor_tensor(rot[L][:], y[L][:], cos[:], ALU.mult))
                    ch.sync()
                    for L in lanes:
                        dve.wait_ge(turn_ready[L], i + 1)
                        nc.vector.tensor_tensor(rot[L][:], rot[L][:], turned[L][:], ALU.add).then_inc(rot_ready[L], 1)
                for k, ready in ((0, q_ready), (2, k_ready)):
                    for L in lanes:
                        dve.wait_ge(free[L], i + 1)
                        dve.wait_ge(ready[L], i + 1)
                        bank, high = banks[L][0 if k else 1], qk4[L][:, k].bitcast(F32)
                        if rope:
                            low = nc.vector.scalar_tensor_tensor(qk4[L][:, k + 1], bank[:], bk[:] if k else bq[:], high,
                                                                 ALU.add, ALU.subtract)
                        else:
                            low = nc.vector.scalar_tensor_tensor(qk4[L][:, k + 1], bank[:], 1.0 if k else SCALE, high,
                                                                 ALU.mult, ALU.subtract)
                        low.then_inc(low_ready[L], 1)
                for L in lanes:
                    dve.wait_ge(v_ps[L], i + 1)
                    dst, src = V[:, bass.ds((i * WIDE + L) * T, T), :], banks[L][1][:].rearrange("p (t d) -> p t d", t=T)
                    if rope:
                        last = nc.vector.tensor_tensor(dst, src, bc(bv[:], T), ALU.add)
                    else:
                        last = nc.vector.tensor_copy(dst, src)
                    last.then_inc(v_ready[L], 1)
                if not rope:
                    for L in lanes:
                        dve.wait_ge(c_ready[L], i * 2 + 2)
                        bank = banks[L][0][0:CE, :]
                        ch.do(nc.vector.scalar_tensor_tensor(c4[L][:, 1], bank, 0.1, c4[L][:, 0].bitcast(F32), ALU.mult, ALU.subtract))
                        nc.vector.scalar_tensor_tensor(c4[L][:, 3], bank, 1.0, c4[L][:, 2].bitcast(F32), ALU.mult,
                                                       ALU.subtract).then_inc(low_ready[L], 1)
                for L in lanes:
                    dve.wait_ge(v_ready[L], i + 1)
                    if rope:
                        dve.wait_ge(y_kept[L], i + 1)
                ch.end()

        @block.scalar
        def _(act):
            act.wait_ge(loaded, 16 * len(loads))
            with act.Fori(0, B // WIDE) as i:
                for L in lanes:
                    act.wait_ge(yT_ps[L], i + 1)
                    nc.scalar.activation(yT[L][:], banks[L][0][:], ACT.Copy).then_inc(yT_ready[L], 1)
                if rope:
                    for L in lanes:
                        act.wait_ge(rT_ps[L], i + 1)
                        nc.scalar.activation(rT[L][:], banks[L][1][:], ACT.Copy).then_inc(rT_ready[L], 1)
                if rope:
                    for L in lanes:
                        nc.scalar.activation(Y[:, bass.ds((i * WIDE + L) * T, T), :], y[L][:], ACT.Copy).then_inc(y_kept[L], 1)
                for L in lanes:
                    act.wait_ge(free[L], i + 1)
                    act.wait_ge(q_ps[L], i + 1)
                    if rope:
                        high = nc.scalar.activation(qk4[L][:, 0], banks[L][1][:], ACT.Identity, bias=bq[:])
                    else:
                        high = nc.scalar.activation(qk4[L][:, 0], banks[L][1][:], ACT.Identity, scale=SCALE)
                    high.then_inc(q_ready[L], 1)
                    act.wait_ge(k_ps[L], i + 1)
                    bias = dict(bias=bk[:]) if rope else {}
                    nc.scalar.activation(qk4[L][:, 2], banks[L][0][:], ACT.Identity, **bias).then_inc(k_ready[L], 1)
                if not rope:
                    for L in lanes:
                        act.wait_ge(c_ps[L], i + 1)
                        for dst, scale in ((c4[L][:, 0], 0.1), (c4[L][:, 2], 1.0)):
                            nc.scalar.activation(dst, banks[L][0][0:CE, :], ACT.Copy, scale=scale).then_inc(c_ready[L], 1)

        @block.tensor
        def _(pe):
            pe.wait_ge(loaded, 16 * len(loads))
            with pe.Fori(0, B // WIDE) as i:
                def transposed(bank, src, signal):
                    for t in range(T):
                        last = nc.tensor.transpose(bank[:, t * P:(t + 1) * P], src[:, t, :], ident[:])
                    last.then_inc(signal, 1)

                for L in lanes:
                    pe.wait_ge(y_ready[L], i + 1)
                    transposed(banks[L][0], y[L], yT_ps[L])
                if rope:
                    for L in lanes:
                        pe.wait_ge(rot_ready[L], i + 1)
                        transposed(banks[L][1], rot[L], rT_ps[L])
                for L in lanes:
                    pe.wait_ge(yT_ready[L], i + 1)
                    if rope:
                        pe.wait_ge(rT_ready[L], i + 1)
                    turned_in = rT[L] if rope else yT[L]
                    nc.tensor.matmul(banks[L][1][:], wq[:], turned_in[:], start=True, stop=True).then_inc(q_ps[L], 1)
                    nc.tensor.matmul(banks[L][0][:], wk[:], turned_in[:], start=True, stop=True).then_inc(k_ps[L], 1)
                for L in lanes:
                    pe.wait_ge(low_ready[L], i * NQ + 1)
                    for t in range(T):
                        last = nc.tensor.matmul(banks[L][1][:, t * P:(t + 1) * P], yT[L][:, t * P:(t + 1) * P], wv[:],
                                                start=True, stop=True)
                    last.then_inc(v_ps[L], 1)
                    if not rope:
                        pe.wait_ge(low_ready[L], i * NQ + 2)
                        nc.tensor.matmul(banks[L][0][0:CE, :], we[:], yT[L][:], start=True, stop=True).then_inc(c_ps[L], 1)


def attend(nc, V, ident, consts, halves, contexts, guards, outs, causal):
    ctx = ExitStack()
    layer = "rope_" if causal else "ctx_"
    with ctx:
        sb = lambda name, shape, dt=F32: ctx.enter_context(nc.sbuf_tensor(layer + "at_" + name, shape, dt))
        sems = []

        def sem(name):
            sems.append(ctx.enter_context(nc.semaphore(layer + "at_" + name)))
            return sems[-1]

        ps = lambda name, n: ctx.enter_context(nc.psum_tensor(layer + "at_" + name, [P, n], F32))
        s_bank = [ps(f"s{k}", 512) for k in range(SR)]
        st_bank = [ps(f"st{k}", 1024) for k in range(2)]
        o_bank = ps("o", 512)

        if causal:
            width = [S - P * c for c in range(T)]
            place = [(0, 0), (0, 512), (1, 0), (0, 896)]
            units, order = [1024, 256], [[0, 1, 3], [2]]
        else:
            width = [S] * T
            place = [(0, 0), (0, 512), (1, 0), (1, 512)]
            units, order = [1024, 1024], [[0, 1], [2, 3]]
        PW = sum(units)
        at = lambda c: (units[0] if place[c][0] else 0) + place[c][1]

        kst, qst = sb("kst", [KM, NG, GH, S], F32R), sb("qst", [KM, NG, GH, S], F32R)
        probs = [sb(f"probs{k}", [P, GH, PW]) for k in range(2)]
        vaug = [sb(f"vaug{k}", [P, 2, T, GH, 32]) for k in range(2)]
        nm = sb("nm", [P, NG, GH * T])
        cut, cutT = sb("cut", [P, 2, GH * T], F32R), sb("cutT", [P, 32], F32R)
        oe = sb("oe", [P, S])
        if causal:
            maskf, maskb, identb = sb("maskf", [P, P]), sb("maskb", [P, P], BF16), sb("identb", [P, P], BF16)

        masked = sem("masked")
        q_clear, k_clear = sem("q_clear"), sem("k_clear")
        init, masks_loaded, masks_ready = sem("init"), sem("masks_loaded"), sem("masks_ready")
        stack = [sem(f"stack_loaded{g}") for g in range(NG)]
        s_ready, s_used = sem("s_ready"), sem("s_used")
        st_ready, p_ready, pv_done = sem("st_ready"), sem("p_ready"), sem("pv_done")
        mh_ready, ml_ready, mT_ready = sem("mh_ready"), sem("ml_ready"), sem("mT_ready")
        m_stored, m_loaded = sem("m_stored"), sem("m_loaded")
        v_ready, o_ready, o_stored = sem("v_ready"), sem("o_ready"), sem("o_stored")
        NL = 6 if causal else 12
        LAST = B - 1
        passed = sem("passed")
        ctx.callback(clear, nc, sems)
        block = ctx.enter_context(nc.Block())

        def group(b, g):
            return b + g // NG, g % NG

        def within(b):
            return not isinstance(b, int) or 0 <= b < B

        def batches(eng, body):
            body(0)
            with eng.Fori(1, LAST) as b:
                body(b)
            body(LAST)

        @block.sync
        def _(sp):
            if causal:
                sp.dma_start(maskf[:], consts["causal"]).then_inc(masks_loaded, 16)
            def load_stack(b, g, tile, parts):
                for r, part in enumerate(parts):
                    src = halves[b, part, g * GH * DH:(g + 1) * GH * DH, :].rearrange("(h d) t -> d h t", d=DH)
                    sp.dma_start(tile[r * DH:(r + 1) * DH, g].bitcast(F32), src).then_inc(stack[g], 16)
                if not causal:
                    for r, part in enumerate(parts):
                        src = contexts[b, part].unsqueeze(1).broadcast_to([CE, GH, S])
                        lo = 3 * DH + r * CE
                        sp.dma_start(tile[lo:lo + CE, g].bitcast(F32), src).then_inc(stack[g], 16)

            def load_stacks(b, g):
                load_stack(b, g, qst, (0, 1, 0))
                load_stack(b, g, kst, (2, 2, 3))

            def store_guard(b, g):
                sp.wait_ge(mT_ready, b * NG + g + 1)
                sp.sem_inc(passed, 1)
                sp.dma_start(guards[g], cutT[:].bitcast(F32)).then_inc(m_stored, 16)

            def load_guard(b, g):
                sp.wait_ge(m_stored, (b * NG + g + 1) * 16)
                sp.sem_inc(passed, 1)
                blocks = guards[g].rearrange("(k n) i -> n k i", k=P // 32)
                for part in range(2):
                    src = blocks[part * GH * T:(part + 1) * GH * T].unsqueeze(0)
                    dst = qst[KS + part:KS + part + 1, g].rearrange("o j (t k i) -> o (j t) k i", t=T, i=32)
                    sp.dma_start(dst.bitcast(F32), src).then_inc(m_loaded, 16)

            def store_out(b, hf):
                sp.wait_ge(o_ready, b * 2 + hf + 1)
                sp.sem_inc(passed, 1)
                sp.dma_start(outs[b, hf], oe[:]).then_inc(o_stored, 16)

            def body(b):
                for g in range(NG):
                    ahead, nxt = group(b, g + 3), group(b, g + 1)
                    if within(ahead[0]):
                        if positive(b * NG + g):
                            sp.wait_ge(st_ready, b * NG * GH * 2 + g * GH * 2)
                            sp.sem_inc(passed, 1)
                        load_stack(*ahead, qst, (0, 1, 0))
                    if within(nxt[0]):
                        if positive(b * NG + g):
                            sp.wait_ge(m_loaded, (b * NG + g) * 32)
                            sp.sem_inc(passed, 1)
                        store_guard(*nxt)
                    if within(ahead[0]):
                        load_stack(*ahead, kst, (2, 2, 3))
                    if within(nxt[0]):
                        load_guard(*nxt)
                    if g % 2 == 0:
                        to, tg = group(b, g - 1)
                        if within(to):
                            store_out(to, tg // 2)

            for g in range(3):
                sp.wait_ge(q_clear, g + 1)
                sp.wait_ge(k_clear, g + 1)
                load_stacks(0, g)
            sp.wait_ge(q_clear, NG)
            sp.wait_ge(k_clear, NG)
            store_guard(0, 0)
            load_guard(0, 0)
            batches(sp, body)
            store_out(LAST, 1)
            sp.wait_ge(o_stored, B * 2 * 16)

        @block.gpsimd
        def _(pool):
            for g in range(NG):
                nc.gpsimd.memset(kst[0:KS, g].bitcast(F32), 0.0).then_inc(k_clear, 1)
            pool.wait_ge(k_clear, NG)
            nc.gpsimd.memset(kst[KS:KM].bitcast(F32), 1.0).then_inc(init, 1)
            pool.wait_ge(init, 1)
            for k in range(2):
                nc.gpsimd.memset(vaug[k][:], 0.0).then_inc(init, 1)
            pool.wait_ge(init, 3)
            for k in range(2):
                for s in range(2):
                    last = nc.gpsimd.memset(vaug[k][:, s, :, :, 9 * s + DH], 1.0)
            last.then_inc(init, 1)

            def place_values(b, hf):
                for s in range(2):
                    h0 = (2 * hf + s) * GH
                    src = V[:, bass.ds(b * T, T), h0 * DH:(h0 + GH) * DH].rearrange("p t (j d) -> p t j d", d=DH)
                    last = nc.gpsimd.tensor_copy(vaug[hf][:, s, :, :, 9 * s:9 * s + DH], src)
                last.then_inc(v_ready, 1)

            def hide_future(b, g, j):
                pool.wait_ge(p_ready, b * 32 + (g * GH + j) * 2 + 2)
                pool.sem_inc(passed, 1)
                row = probs[g % 2][:, j]
                for blocks in (row[:, 0:1024].rearrange("p (two w) -> p two w", two=2)[:, :, 0:P],
                               row[:, 896:896 + 2 * P].rearrange("p (two w) -> p two w", two=2)):
                    last = nc.gpsimd.affine_select(blocks, blocks, [[0, 2], [1, P]], compare_op=ALU.is_ge, fill=0.0,
                                                   base=0, channel_multiplier=-1)
                last.then_inc(masked, 1)

            def body(b):
                for g in range(NG):
                    if g < 2:
                        if positive(b):
                            pool.wait_ge(pv_done, b * NG * T - NG * T + (2 * g + 2) * T)
                        place_values(b, g)
                    if causal:
                        for j in range(GH):
                            hide_future(b, g, j)
            batches(pool, body)

        @block.vector
        def _(dve):
            for g in range(NG):
                nc.vector.memset(qst[0:KS, g].bitcast(F32), 0.0).then_inc(q_clear, 1)
            if causal:
                dve.wait_ge(masks_loaded, 16)
                nc.vector.tensor_copy(maskb[:], maskf[:])
                nc.vector.tensor_copy(identb[:], ident[:]).then_inc(masks_ready, 1)

            def largest(b, g, j, t):
                n = (g * GH + j) * T + t
                dve.wait_ge(s_ready, b * 64 + n + 1)
                keys = P * (t + 1) if causal else S
                nc.vector.tensor_reduce(nm[:, g, j * T + t:j * T + t + 1], s_bank[n % SR][:, 0:keys], AXX, ALU.max,
                                        negate=True).then_inc(s_used, 1)

            def cut_guard(b, g, step):
                n = b * NG + g
                if step == 0:
                    dve.wait_ge(s_used, b * 64 + (g + 1) * GH * T)
                    if positive(n):
                        dve.wait_ge(mT_ready, n)
                    nc.vector.tensor_copy(cut[:, 0], nm[:, g]).then_inc(mh_ready, 1)
                if step == 1:
                    dve.wait_ge(mh_ready, n + 1)
                    nc.vector.tensor_tensor(cut[:, 1], nm[:, g], cut[:, 0].bitcast(F32), ALU.subtract).then_inc(ml_ready, 1)
                if step == 2:
                    dve.wait_ge(ml_ready, n + 1)
                    if positive(n):
                        dve.wait_ge(m_stored, n * 16)
                    nc.vector.transpose(cutT[:].bitcast(F32), cut[:].rearrange("p h n -> p (h n)").bitcast(F32)).then_inc(mT_ready, 1)

            def body(b):
                for g in range(NG):
                    for j in range(GH):
                        for t in range(T):
                            to, tg = group(b, g + 2)
                            if within(to):
                                largest(to, tg, j, t)
                            to, tg = group(b, g + 1)
                            if within(to) and j == 0:
                                cut_guard(to, tg, t)

            for g in range(2):
                for j in range(GH):
                    for t in range(T):
                        largest(0, g, j, t)
                        if g == 1 and j == 0:
                            cut_guard(0, 0, t)
            batches(dve, body)

        @block.scalar
        def _(act):
            def exponentials(b, g, j):
                for u in range(2):
                    act.wait_ge(st_ready, b * 32 + (g * GH + j) * 2 + u + 1)
                    nc.scalar.activation(probs[g % 2][:, j, u * units[0]:u * units[0] + units[u]],
                                         st_bank[u][:, 0:units[u]], ACT.Exp,
                                         scale=SCALE if causal else 1.0).then_inc(p_ready, 1)

            def keep_out(b, hf):
                act.wait_ge(pv_done, b * NG * T + (2 * hf + 2) * T)
                if not (isinstance(b, int) and b * 2 + hf == 0):
                    act.wait_ge(o_stored, (b * 2 + hf) * 16)
                nc.scalar.activation(oe[:], o_bank[:], ACT.Copy).then_inc(o_ready, 1)

            def body(b):
                for g in range(NG):
                    if not (isinstance(b, int) and b * NG + g < 2):
                        act.wait_ge(pv_done, b * NG * T + g * T - T)
                    for j in range(GH):
                        exponentials(b, g, j)
                    if g % 2 == 0:
                        to, tg = group(b, g - 1)
                        if within(to):
                            keep_out(to, tg // 2)

            batches(act, body)
            keep_out(LAST, 1)

        @block.tensor
        def _(pe):
            if causal:
                pe.wait_ge(masks_ready, 1)

            def score(b, g, j, t):
                n = (g * GH + j) * T + t
                before = b * 64 + (n if n == 0 else n - SR + 1)
                if positive(before):
                    pe.wait_ge(s_used, before)
                keys = P * (t + 1) if causal else S
                out = s_bank[n % SR]
                last = nc.tensor.matmul(out[:, 0:keys], qst[0:KS, g, j, t * P:(t + 1) * P], kst[0:KS, g, j, 0:keys],
                                        start=True, stop=not causal)
                if causal:
                    last = nc.tensor.matmul(out[:, keys - P:keys], identb[:], maskb[:], start=False, stop=True)
                last.then_inc(s_ready, 1)

            def scores_by_key(b, g, j, u):
                if not (isinstance(b, int) and b * NG * GH + g * GH + j == 0):
                    pe.wait_ge(p_ready, b * 32 + (g * GH + j) * 2 + u - 1)
                for c in order[u]:
                    lo = place[c][1]
                    last = nc.tensor.matmul(st_bank[u][:, lo:lo + width[c]], kst[:, g, j, c * P:(c + 1) * P],
                                            qst[:, g, j, S - width[c]:S], start=True, stop=True)
                last.then_inc(st_ready, 1)

            def weigh_values(b, g, c):
                if c == 0:
                    if causal:
                        pe.wait_ge(masked, b * NG * GH + (g + 1) * GH)
                    else:
                        pe.wait_ge(p_ready, b * 32 + (g + 1) * GH * 2)
                    if g % 2 == 0:
                        pe.wait_ge(v_ready, b * 2 + g // 2 + 1)
                        if not (isinstance(b, int) and b * 2 + g // 2 == 0):
                            pe.wait_ge(o_ready, b * 2 + g // 2)
                s = g % 2
                for j in range(GH):
                    last = nc.tensor.matmul(o_bank[32 * j:32 * j + 32, S - width[c]:S], vaug[g // 2][:, s, c, j, :],
                                            probs[s][:, j, at(c):at(c) + width[c]],
                                            start=s == 0 and c == 0, stop=s == 1 and c == T - 1)
                last.then_inc(pv_done, 1)

            def body(b):
                for g in range(NG):
                    for j in range(GH):
                        ahead, behind = group(b, g + 2), group(b, g - 1)
                        if j == 0:
                            pe.wait_ge(m_loaded, (b * NG + g + 1) * 32)
                            if within(ahead[0]):
                                pe.wait_ge(stack[ahead[1]], (ahead[0] + 1) * NL * 16)
                        for u in range(2):
                            if within(ahead[0]):
                                score(*ahead, j, 2 * u)
                            scores_by_key(b, g, j, u)
                            if within(ahead[0]):
                                score(*ahead, j, 2 * u + 1)
                            if within(behind[0]) and (j and u == 0 or j == GH - 1):
                                weigh_values(*behind, j - 1 + u)

            for g in range(2):
                pe.wait_ge(stack[g], NL * 16)
                for j in range(GH):
                    for t in range(T):
                        score(0, g, j, t)
            pe.wait_ge(init, 4)
            batches(pe, body)
            for c in range(T):
                weigh_values(LAST, NG - 1, c)


def attention_out(nc, X, Y, ident, w, outs, rope):
    ctx = ExitStack()
    layer = "rope_" if rope else "ctx_"
    with ctx:
        sb = lambda name, shape, dt=F32: ctx.enter_context(nc.sbuf_tensor(layer + "ao_" + name, shape, dt))
        sems = []

        def sem(name):
            sems.append(ctx.enter_context(nc.semaphore(layer + "ao_" + name)))
            return sems[-1]

        lanes = range(WIDE)
        sb2 = lambda name, shape, dt=F32: [sb(f"{name}{L}", shape, dt) for L in lanes]
        sem2 = lambda name: [sem(f"{name}{L}") for L in lanes]
        banks = [[ctx.enter_context(nc.psum_tensor(f"{layer}ao_bank{L}{i}", [P, 512], F32)) for i in range(2)] for L in lanes]
        wo = sb("wo", [P, D])
        loads = [(wo, w["WoT"])]
        if rope:
            bo, gain, shift = sb("bo", [P, D]), sb("gain", [P, D]), sb("shift", [P, D])
            loads += [(bo, w["out_proj_b"]), (gain, w["ln1_w"]), (shift, w["ln1_b"])]
            yb = sb2("yb", [P, T, D])
        oe, rc = sb2("oe", [P, 2, S]), sb2("rc", [P, 2, 2, T, GH])
        o, oT, r, z = sb2("o", [P, T, D]), sb2("oT", [P, S]), sb2("r", [P, T, D]), sb2("z", [P, T, D])
        stats, mv, rstd = sb2("stats", [P, T, 6]), sb2("mv", [P, T, 2]), sb2("rstd", [P, T])
        half = sb("half", [P, T])
        loaded, half_ready, dve_steps, passed = sem("loaded"), sem("half_ready"), sem("dve_steps"), sem("passed")
        in_ready, turned, o_ready, yb_ready = sem2("in_ready"), sem2("turned"), sem2("o_ready"), sem2("yb_ready")
        oT_ps, oT_ready, wo_ps, x_ready = sem2("oT_ps"), sem2("oT_ready"), sem2("wo_ps"), sem2("x_ready")
        var_ready, rstd_ready = sem2("var_ready"), sem2("rstd_ready")
        PER = WIDE * (4 + 3 + 3 * T + (2 if rope else 0))
        ctx.callback(clear, nc, sems)
        block = ctx.enter_context(nc.Block())

        @block.sync
        def _(sp):
            for L in lanes:
                sp.dma_start(oe[L][:], outs[L].rearrange("k p s -> p k s")).then_inc(in_ready[L], 16)
            for dst, src in loads:
                sp.dma_start(dst[:], src).then_inc(loaded, 16)
            with sp.Fori(1, B // WIDE) as i:
                for L in lanes:
                    sp.wait_ge(turned[L], i * 2)
                    sp.sem_inc(passed, 1)
                    sp.dma_start(oe[L][:], outs[i * WIDE + L].rearrange("k p s -> p k s")).then_inc(in_ready[L], 16)
            for L in lanes:
                sp.wait_ge(x_ready[L], B // WIDE)

        @block.gpsimd
        def _(pool):
            nc.gpsimd.memset(half[:], -0.5).then_inc(half_ready, 1)
            pool.wait_ge(half_ready, 1)
            with pool.Fori(0, B // WIDE) as i:
                if rope:
                    pool.wait_ge(loaded, 16 * len(loads))
                    for L in lanes:
                        nc.gpsimd.tensor_tensor(yb[L][:], Y[:, bass.ds((i * WIDE + L) * T, T), :], bc(bo[:], T),
                                                ALU.add).then_inc(yb_ready[L], 1)
                for L in lanes:
                    pool.wait_ge(var_ready[L], i + 1)
                    nc.gpsimd.tensor_tensor(rstd[L][:], mv[L][:, :, 1], half[:], ALU.pow).then_inc(rstd_ready[L], 1)

        @block.tensor
        def _(pe):
            with pe.Fori(0, B // WIDE) as i:
                for L in lanes:
                    pe.wait_ge(in_ready[L], i * 16 + 16)
                    for hf in range(2):
                        for t in range(T):
                            last = nc.tensor.transpose(banks[L][hf][:, t * P:(t + 1) * P], oe[L][:, hf, t * P:(t + 1) * P], ident[:])
                        last.then_inc(turned[L], 1)
                for L in lanes:
                    pe.wait_ge(o_ready[L], i + 1)
                    for t in range(T):
                        last = nc.tensor.transpose(banks[L][0][:, t * P:(t + 1) * P], o[L][:, t, :], ident[:])
                    last.then_inc(oT_ps[L], 1)
                pe.wait_ge(loaded, 16 * len(loads))
                for L in lanes:
                    pe.wait_ge(oT_ready[L], i + 1)
                    for t in range(T):
                        last = nc.tensor.matmul(banks[L][1][:, t * P:(t + 1) * P], oT[L][:, t * P:(t + 1) * P], wo[:],
                                                start=True, stop=True)
                    last.then_inc(wo_ps[L], 1)
                for L in lanes:
                    pe.wait_ge(x_ready[L], i + 1)

        @block.scalar
        def _(act):
            with act.Fori(0, B // WIDE) as i:
                for L in lanes:
                    act.wait_ge(oT_ps[L], i + 1)
                    nc.scalar.activation(oT[L][:], banks[L][0][:], ACT.Copy).then_inc(oT_ready[L], 1)

        @block.vector
        def _(dve):
            ch = Chain(dve, dve_steps, PER, passed)
            with dve.Fori(0, B // WIDE) as i:
                ch.start(i)
                own = [bass.ds((i * WIDE + L) * T, T) for L in lanes]
                rows = [[bank[:].rearrange("p (t j k) -> p t j k", t=T, k=32) for bank in banks[L]] for L in lanes]
                for L in lanes:
                    for hf in range(2):
                        dve.wait_ge(turned[L], i * 2 + hf + 1)
                        for s in range(2):
                            ch.do(nc.vector.reciprocal(rc[L][:, hf, s], rows[L][hf][:, :, :, 9 * s + DH]))
                ch.sync()
                for L in lanes:
                    for hf in range(2):
                        for s in range(2):
                            h0 = (2 * hf + s) * GH
                            dst = o[L][:, :, h0 * DH:(h0 + GH) * DH].rearrange("p t (j d) -> p t j d", d=DH)
                            last = nc.vector.tensor_tensor(dst, rows[L][hf][:, :, :, 9 * s:9 * s + DH], each(rc[L][:, hf, s], DH),
                                                           ALU.mult)
                            if hf * 2 + s < 3:
                                ch.do(last)
                    last.then_inc(o_ready[L], 1)
                src = [r[L] if rope else banks[L][1][:].rearrange("p (t d) -> p t d", t=T) for L in lanes]
                for L in lanes:
                    dve.wait_ge(wo_ps[L], i + 1)
                    if rope:
                        dve.wait_ge(yb_ready[L], i + 1)
                        ch.do(nc.vector.tensor_tensor(r[L][:], banks[L][1][:].rearrange("p (t d) -> p t d", t=T), yb[L][:], ALU.add))
                if rope:
                    ch.sync()
                for L, last in enumerate(wide_stats(nc, ch, src, stats, mv)):
                    last.then_inc(var_ready[L], 1)
                for L in lanes:
                    dve.wait_ge(rstd_ready[L], i + 1)
                    ln_apply(nc, ch, z[L], src[L], mv[L], rstd[L])
                ch.sync()
                if rope:
                    dve.wait_ge(loaded, 16 * len(loads))
                    for L in lanes:
                        ch.do(nc.vector.tensor_tensor(z[L][:], z[L][:], bc(gain[:], T), ALU.mult))
                    ch.sync()
                for L in lanes:
                    if rope:
                        last = nc.vector.tensor_tensor(Y[:, own[L], :], z[L][:], bc(shift[:], T), ALU.add)
                    else:
                        x = X[:, own[L], :]
                        last = nc.vector.tensor_tensor(x, x, z[L][:], ALU.add)
                    last.then_inc(x_ready[L], 1)
                for L in lanes:
                    dve.wait_ge(x_ready[L], i + 1)
                ch.end()


def attention_layer(nc, X, Y, ident, w, consts, rope):
    name = "rope" if rope else "ctx"
    halves = nc.dram_tensor(name + "_halves", [B, 4, P, S], F32, kind="Internal").ap()
    contexts = None if rope else nc.dram_tensor(name + "_contexts", [B, 4, CE, S], F32, kind="Internal").ap()
    guards = nc.dram_tensor(name + "_guards", [NG, P, 32], F32, kind="Internal").ap()
    outs = nc.dram_tensor(name + "_outs", [B, 2, P, S], F32, kind="Internal").ap()
    with nc.sbuf_tensor(name + "_V", [P, B * T, D], F32) as V:
        project_qkv(nc, X, Y, V, ident, w, consts, halves, contexts, rope)
        attend(nc, V, ident, consts, halves, contexts, guards, outs, rope)
    attention_out(nc, X, Y, ident, w, outs, rope)


def shift_logits(nc, ch, lg, red):
    ch.do(nc.vector.tensor_reduce(red[:, :, 0], lg[:], AXX, ALU.max))
    ch.sync()
    return nc.vector.tensor_tensor(lg[:], lg[:], each(red[:, :, 0], NE), ALU.subtract)


def normalise_gates(nc, ch, lg, red):
    ch.do(nc.vector.tensor_reduce(red[:, :, 1], lg[:], AXX, ALU.add))
    ch.sync()
    ch.do(nc.vector.reciprocal(red[:, :, 0], red[:, :, 1]))
    ch.sync()
    ch.do(nc.vector.tensor_tensor(lg[:], lg[:], each(red[:, :, 0], NE), ALU.mult))
    ch.sync()


def choose(nc, ch, k, probs, order, tmp, red, hot):
    left = probs if k == 0 else tmp
    ch.do(nc.vector.tensor_reduce(red[:, :, 0], left[:], AXX, ALU.max))
    ch.sync()
    ch.do(nc.vector.tensor_tensor(hot[:, k], left[:], each(red[:, :, 0], NE), ALU.is_equal))
    ch.sync()
    ch.do(nc.vector.tensor_tensor(hot[:, k], hot[:, k], bc(order[:], probs.shape[1]), ALU.mult))
    ch.sync()
    ch.do(nc.vector.tensor_reduce(red[:, :, 1], hot[:, k], AXX, ALU.max))
    ch.sync()
    ch.do(nc.vector.tensor_tensor(hot[:, k], hot[:, k], each(red[:, :, 1], NE), ALU.is_equal))
    ch.sync()
    if k == 0:
        ch.do(nc.vector.scalar_tensor_tensor(tmp[:], hot[:, 0], -2.0, probs[:], ALU.mult, ALU.add))
        ch.sync()


def keep_chosen(nc, ch, probs, hot, gates):
    ch.do(nc.vector.tensor_tensor(hot[:, 0], hot[:, 0], hot[:, 1], ALU.add))
    ch.sync()
    return nc.vector.tensor_tensor(gates[:, :, 0:NE], hot[:, 0], probs[:], ALU.mult)


GATING_STEPS = 1 + 3 + 6 + 5 + 1


def gate_tokens(nc, SRC, ident, w, consts, GATES, prefix, experts=None, halves=None, values=None):
    ctx = ExitStack()
    with ctx:
        sb = lambda name, shape, dt=F32: ctx.enter_context(nc.sbuf_tensor(prefix + name, shape, dt))
        sems = []
        lanes = range(WIDE)
        IT = B // WIDE

        def sem(name):
            sems.append(ctx.enter_context(nc.semaphore(prefix + name)))
            return sems[-1]

        sb2 = lambda name, shape, dt=F32: [sb(f"{name}{L}", shape, dt) for L in lanes]
        sem2 = lambda name: [sem(f"{name}{L}") for L in lanes]
        y_bank = [ctx.enter_context(nc.psum_tensor(f"{prefix}y_bank{L}", [P, 512], F32)) for L in lanes]
        small = [ctx.enter_context(nc.psum_tensor(f"{prefix}small{L}", [P, 512], F32)) for L in lanes]
        gw, order = sb("gw", [P, NE]), sb("order", [P, NE])
        loads = [(gw, w["gateT"]), (order, consts["order"])]
        FIRST = 2
        if halves is None:
            gb, eb = sb("gb", [P, NE]), sb("eb", [NE, D])
            loads += [(gb, w["gate_b"]), (eb, w["expert_b"])]
            gl, gT = sb2("gl", [P, T, NE]), sb2("gT", [NE, S])
        else:
            stage = [sb(f"stage{k}", [P, 3, 512]) for k in range(2)]
            high, low = experts
        y, yf = sb2("y", [P, T, D]), sb2("yf", [P, S])
        stats, mv, rstd = sb2("stats", [P, T, 6]), sb2("mv", [P, T, 2]), sb2("rstd", [P, T])
        half = sb("half", [P, T])
        if halves is None:
            lg, tmp = sb("lg", [P, B * T, NE]), sb("tmp", [P, B * T, NE])
            hot, red = sb("hot", [P, 2, B * T, NE]), sb("red", [P, B * T, 2])

        loaded, half_ready, passed, dve_steps = sem("loaded"), sem("half_ready"), sem("passed"), sem("dve_steps")
        staged = [sem(f"staged{k}") for k in range(2)]
        high_ready, low_ready = sem("high_ready"), sem("low_ready")
        var_ready, rstd_ready, y_ready = sem2("var_ready"), sem2("rstd_ready"), sem2("y_ready")
        yT_ps, yf_ready, yT_kept, gate_ps = sem2("yT_ps"), sem2("yf_ready"), sem2("yT_kept"), sem2("gate_ps")
        lg_ready, e_ready, gates_ready = sem("lg_ready"), sem("e_ready"), sem("gates_ready")
        gl_ready, gT_ps, gT_ready, bias_ps, biased = sem2("gl_ready"), sem2("gT_ps"), sem2("gT_ready"), sem2("bias_ps"), sem2("biased")
        PER = (WIDE * (3 * T - 1) + WIDE if halves else 0) + WIDE
        ctx.callback(clear, nc, sems)
        block = ctx.enter_context(nc.Block())

        @block.sync
        def _(sp):
            for dst, src in loads:
                sp.dma_start(dst[:], src).then_inc(loaded, 16)

            def stage_in(e, k):
                sp.dma_start(stage[k][:, 0, :], w["w1"][e]).then_inc(staged[k], 16)
                sp.dma_start(stage[k][:, 1, :], w["w3"][e]).then_inc(staged[k], 16)
                sp.dma_start(stage[k][:, 2, :], w["w2"][e].rearrange("p c d -> p (c d)")).then_inc(staged[k], 16)
            if halves:
                for e in range(FIRST):
                    stage_in(e, e)

        @block.gpsimd
        def _(pool):
            nc.gpsimd.memset(half[:], -0.5).then_inc(half_ready, 1)
            pool.wait_ge(half_ready, 1)
            if halves:
                with pool.Fori(0, IT) as i:
                    for L in lanes:
                        pool.wait_ge(var_ready[L], i + 1)
                        nc.gpsimd.tensor_tensor(rstd[L][:], mv[L][:, :, 1], half[:], ALU.pow).then_inc(rstd_ready[L], 1)

        @block.scalar
        def _(act):
            with act.Fori(0, IT) as i:
                for L in lanes:
                    to = bass.ds((i * WIDE + L) * S, S)
                    act.wait_ge(yT_ps[L], i + 1)
                    nc.scalar.activation(yf[L][:], y_bank[L][:], ACT.Copy).then_inc(yf_ready[L], 1)
                    kept = halves[0][:, to] if halves else values[:, to]
                    nc.scalar.activation(kept, y_bank[L][:], ACT.Copy).then_inc(yT_kept[L], 1)
            if halves:
                for e in range(FIRST):
                    act.wait_ge(staged[e], 48)
                    nc.scalar.activation(high[:, e], stage[e][:], ACT.Copy).then_inc(high_ready, 1)
            else:
                act.wait_ge(lg_ready, 1)
                nc.scalar.activation(lg[:], lg[:], ACT.Exp).then_inc(e_ready, 1)
                with act.Fori(0, IT) as i:
                    for L in lanes:
                        act.wait_ge(gT_ps[L], i + 1)
                        nc.scalar.activation(gT[L][:], small[L][0:NE, :], ACT.Copy).then_inc(gT_ready[L], 1)

        @block.vector
        def _(dve):
            ch = Chain(dve, dve_steps, PER, passed)

            with dve.Fori(0, IT) as i:
                ch.start(i)
                tiles = [bass.ds((i * WIDE + L) * T, T) for L in lanes]
                if halves:
                    for L, last in enumerate(wide_stats(nc, ch, [SRC[:, tiles[L], :] for L in lanes], stats, mv)):
                        last.then_inc(var_ready[L], 1)
                    for L in lanes:
                        x = SRC[:, tiles[L], :]
                        dve.wait_ge(rstd_ready[L], i + 1)
                        for t in range(T):
                            last = nc.vector.tensor_scalar(y[L][:, t, :], x[:, t, :], mv[L][:, t, 0:1], rstd[L][:, t:t + 1],
                                                           ALU.subtract, ALU.mult)
                            if t < T - 1:
                                ch.do(last)
                        last.then_inc(y_ready[L], 1)
                    for L in lanes:
                        to = bass.ds((i * WIDE + L) * S, S)
                        dve.wait_ge(yT_kept[L], i + 1)
                        ch.do(nc.vector.tensor_tensor(halves[1][:, to], yf[L][:], halves[0][:, to].bitcast(F32), ALU.subtract))
                else:
                    for L in lanes:
                        nc.vector.tensor_copy(y[L][:], SRC[:, tiles[L], :]).then_inc(y_ready[L], 1)
                dve.wait_ge(loaded, 16 * len(loads))
                for L in lanes:
                    dve.wait_ge(gate_ps[L], i + 1)
                    logits = small[L][:, 0:T * NE].rearrange("p (t e) -> p t e", e=NE)
                    if halves:
                        ch.do(nc.vector.tensor_copy(GATES[:, tiles[L], 0:NE], logits))
                    else:
                        ch.do(nc.vector.tensor_tensor(lg[:, tiles[L], :], logits, bc(gb[:], T), ALU.add))
                ch.sync()
                ch.end()
            if halves:
                for e in range(FIRST):
                    dve.wait_ge(high_ready, e + 1)
                    nc.vector.tensor_tensor(low[:, e], stage[e][:], high[:, e].bitcast(F32), ALU.subtract).then_inc(low_ready, 1)
            else:
                ch.start(0, IT * PER)
                ch.sync()
                shift_logits(nc, ch, lg, red).then_inc(lg_ready, 1)
                dve.wait_ge(e_ready, 1)
                normalise_gates(nc, ch, lg, red)
                choose(nc, ch, 0, lg, order, tmp, red, hot)
                choose(nc, ch, 1, lg, order, tmp, red, hot)
                keep_chosen(nc, ch, lg, hot, GATES).then_inc(gates_ready, 1)
                dve.wait_ge(gates_ready, 1)
                with dve.Fori(0, IT) as i:
                    for L in lanes:
                        nc.vector.tensor_copy(gl[L][:], GATES[:, bass.ds((i * WIDE + L) * T, T), :]).then_inc(gl_ready[L], 1)
                    for L in lanes:
                        own = SRC[:, bass.ds((i * WIDE + L) * T, T), :]
                        dve.wait_ge(bias_ps[L], i + 1)
                        nc.vector.tensor_tensor(own, y_bank[L][:].rearrange("p (t d) -> p t d", t=T), own, ALU.add).then_inc(biased[L], 1)

        @block.tensor
        def _(pe):
            with pe.Fori(0, IT) as i:
                for L in lanes:
                    pe.wait_ge(y_ready[L], i + 1)
                    for t in range(T):
                        last = nc.tensor.transpose(y_bank[L][:, t * P:(t + 1) * P], y[L][:, t, :], ident[:])
                    last.then_inc(yT_ps[L], 1)
                pe.wait_ge(loaded, 16 * len(loads))
                for L in lanes:
                    pe.wait_ge(yf_ready[L], i + 1)
                    for t in range(T):
                        last = nc.tensor.matmul(small[L][:, t * NE:(t + 1) * NE], yf[L][:, t * P:(t + 1) * P], gw[:],
                                                start=True, stop=True)
                    last.then_inc(gate_ps[L], 1)
                for L in lanes:
                    pe.wait_ge(yT_kept[L], i + 1)
            if not halves:
                pe.wait_ge(lg_ready, 1)
                with pe.Fori(0, IT) as i:
                    for L in lanes:
                        pe.wait_ge(gl_ready[L], i + 1)
                        for t in range(T):
                            last = nc.tensor.transpose(small[L][0:NE, t * P:(t + 1) * P], gl[L][:, t, :], ident[:])
                        last.then_inc(gT_ps[L], 1)
                    for L in lanes:
                        pe.wait_ge(gT_ready[L], i + 1)
                        for t in range(T):
                            last = nc.tensor.matmul(y_bank[L][:, t * P:(t + 1) * P], gT[L][:, t * P:(t + 1) * P], eb[:],
                                                    start=True, stop=True)
                        last.then_inc(bias_ps[L], 1)
                    for L in lanes:
                        pe.wait_ge(biased[L], i + 1)


def mixture_layer(nc, X, Y, ident, w, consts):
    ctx = ExitStack()
    with ctx:
        gates = ctx.enter_context(nc.sbuf_tensor("mo_gates", [P, B * T, NE], F32))
        YT = ctx.enter_context(nc.sbuf_tensor("mo_YT", [P, B * S], F32))
        gate_tokens(nc, Y, ident, w, consts, gates, "mg_", values=YT)
        sems = []

        def sem(name):
            sems.append(ctx.enter_context(nc.semaphore("mo_" + name)))
            return sems[-1]

        lanes = range(LANES)
        sb = lambda name, shape, dt=F32: ctx.enter_context(nc.sbuf_tensor("mo_" + name, shape, dt))
        sb2 = lambda name, shape, dt=F32: [sb(f"{name}{L}", shape, dt) for L in lanes]
        sem2 = lambda name: [sem(f"{name}{L}") for L in lanes]
        pb = [[ctx.enter_context(nc.psum_tensor(f"mo_pb{L}{i}", [P, 1024], F32)) for i in range(2)] for L in lanes]
        we, gain, shift = sb("we", [P, NE * D]), sb("gain", [P, D]), sb("shift", [P, D])
        loads = [(gain, w["ln2_w"]), (shift, w["ln2_b"])]
        yT, g = sb2("yT", [P, S]), sb2("g", [P, T, NE])
        acc, z = sb2("acc", [P, T, D]), sb2("z", [P, T, D])
        stats, mv, rstd = sb2("stats", [P, T, 6]), sb2("mv", [P, T, 2]), sb2("rstd", [P, T])
        half = sb("half", [P, T])
        we_loaded = sem("we_loaded")
        loaded, half_ready, passed = sem("loaded"), sem("half_ready"), sem("passed")
        yT_ready, ex_ps, ex_used, dve_steps = sem2("yT_ready"), sem2("ex_ps"), sem2("ex_used"), sem2("dve_steps")
        var_ready, rstd_ready, z_ready, z_done = sem2("var_ready"), sem2("rstd_ready"), sem2("z_ready"), sem2("z_done")
        scaled = sem2("scaled")
        PER = 1 + T * NE - 2 + 6 * T - 1 + 1
        ctx.callback(clear, nc, sems)
        block = ctx.enter_context(nc.Block())

        @block.sync
        def _(sp):
            for k in range(2):
                cols = slice(k * 512, (k + 1) * 512)
                sp.dma_start(we[:, cols], w["expertT"][:, cols]).then_inc(we_loaded, 16)
            for dst, src in loads:
                sp.dma_start(dst[:], src).then_inc(loaded, 16)

        @block.gpsimd
        def _(pool):
            nc.gpsimd.memset(half[:], -0.5).then_inc(half_ready, 1)
            pool.wait_ge(half_ready, 1)
            with pool.Fori(0, B // LANES) as i:
                def rsqrt(L, k):
                    pool.wait_ge(var_ready[L], i * 2 + k + 1)
                    nc.gpsimd.tensor_tensor(rstd[L][:], mv[L][:, :, 1], half[:], ALU.pow).then_inc(rstd_ready[L], 1)
                for L in lanes:
                    rsqrt(L, 0)
                pool.wait_ge(loaded, 16 * len(loads))
                for L in lanes:
                    pool.wait_ge(z_ready[L], i + 1)
                    nc.gpsimd.tensor_tensor(z[L][:], z[L][:], bc(gain[:], T), ALU.mult).then_inc(scaled[L], 1)
                    pool.wait_ge(scaled[L], i + 1)
                    nc.gpsimd.tensor_tensor(z[L][:], z[L][:], bc(shift[:], T), ALU.add).then_inc(z_done[L], 1)
                for L in lanes:
                    rsqrt(L, 1)

        @block.vector
        def _(dve):
            ch = [Chain(dve, dve_steps[L], PER, passed) for L in lanes]
            with dve.Fori(0, B // LANES) as i:
                tiles = [bass.ds((i * LANES + L) * T, T) for L in lanes]

                def combine(L, pair):
                    dve.wait_ge(ex_ps[L], i * 2 + pair + 1)
                    for e in range(NE):
                        for k in range(2):
                            t = 2 * pair + k
                            ch[L].sync(but=1 if e else 0)
                            before = Y[:, tiles[L], :][:, t, :] if e == 0 else acc[L][:, t, :]
                            last = nc.vector.scalar_tensor_tensor(acc[L][:, t, :], pb[L][k][:, e * D:(e + 1) * D],
                                                                  g[L][:, t, e:e + 1], before, ALU.mult, ALU.add)
                            if k == 0 or e < NE - 1:
                                ch[L].do(last)
                    last.then_inc(ex_used[L], 1)

                for L in lanes:
                    ch[L].start(i)
                    ch[L].do(nc.vector.tensor_copy(g[L][:], gates[:, tiles[L], :]))
                for pair in range(2):
                    for L in lanes:
                        combine(L, pair)

                for L in lanes:
                    dve.wait_ge(ex_used[L], i * 2 + 2)
                    ln_stats(nc, ch[L], acc[L], stats[L], mv[L]).then_inc(var_ready[L], 1)
                for L in lanes:
                    dve.wait_ge(rstd_ready[L], i * 2 + 1)
                    for t in range(T):
                        last = nc.vector.tensor_scalar(z[L][:, t, :], acc[L][:, t, :], mv[L][:, t, 0:1], rstd[L][:, t:t + 1],
                                                       ALU.subtract, ALU.mult)
                        if t < T - 1:
                            ch[L].do(last)
                    last.then_inc(z_ready[L], 1)
                for L in lanes:
                    dve.wait_ge(z_done[L], i + 1)
                    ln_stats(nc, ch[L], z[L], stats[L], mv[L]).then_inc(var_ready[L], 1)
                for L in lanes:
                    dve.wait_ge(rstd_ready[L], i * 2 + 2)
                    ln_apply(nc, ch[L], acc[L], z[L], mv[L], rstd[L])
                for L in lanes:
                    ch[L].sync()
                    x = X[:, tiles[L], :]
                    ch[L].do(nc.vector.tensor_tensor(x, x, acc[L][:], ALU.add))
                for L in lanes:
                    ch[L].sync()
                    ch[L].end()

        @block.scalar
        def _(act):
            with act.Fori(0, B // LANES) as i:
                for L in lanes:
                    nc.scalar.activation(yT[L][:], YT[:, bass.ds((i * LANES + L) * S, S)], ACT.Copy).then_inc(yT_ready[L], 1)
                for L in lanes:
                    act.wait_ge(ex_ps[L], i * 2 + 2)

        @block.tensor
        def _(pe):
            pe.wait_ge(we_loaded, 32)
            with pe.Fori(0, B // LANES) as i:
                for pair in range(2):
                    for L in lanes:
                        if pair == 0:
                            pe.wait_ge(yT_ready[L], i + 1)
                        else:
                            pe.wait_ge(ex_used[L], i * 2 + 1)
                        for k in range(2):
                            t = 2 * pair + k
                            for half_row in range(2):
                                cols = slice(half_row * 512, (half_row + 1) * 512)
                                last = nc.tensor.matmul(pb[L][k][:, cols], yT[L][:, t * P:(t + 1) * P], we[:, cols],
                                                        start=True, stop=True)
                        last.then_inc(ex_ps[L], 1)
                for L in lanes:
                    pe.wait_ge(ex_used[L], i * 2 + 2)


def swiglu_layer(nc, X, ident, w, consts, out):
    N = NE + 1
    RING, LAG = 4, 3
    FINISH = 7
    ER = 3
    ctx = ExitStack()
    with ctx:
        sb = lambda name, shape, dt=F32: ctx.enter_context(nc.sbuf_tensor("sw_" + name, shape, dt))
        high, low = sb("high", [P, N, 3, 512], F32R), sb("low", [P, N, 3, 512], F32R)
        YH, YL = sb("YH", [P, B * S], F32R), sb("YL", [P, B * S], F32R)
        logits = ctx.enter_context(nc.sbuf_tensor("sw_logits", [P, B * T, NE], F32))
        gate_tokens(nc, X, ident, w, consts, logits, "sg_", experts=(high, low), halves=(YH, YL))
        sems = []

        def sem(name):
            sems.append(ctx.enter_context(nc.semaphore("sw_" + name)))
            return sems[-1]

        ps = lambda name: ctx.enter_context(nc.psum_tensor("sw_" + name, [P, 512], F32))
        g_bank, u_bank = [ps(f"g{k}") for k in range(2)], [ps(f"u{k}") for k in range(2)]
        d_bank, turned = [ps(f"d{k}") for k in range(ER)], ps("turned")
        stage = [sb(f"stage{k}", [P, 3, 512]) for k in range(2)]
        FIRST = 2
        GATES, order = sb("GATES", [P, B * T, N]), sb("order", [P, NE])
        tmp, red = sb("tmp", [P, B * T, NE]), sb("red", [P, B * T, 2])
        staged = [sem(f"staged{k}") for k in range(2)]
        x_ready, x_stored = sem("x_ready"), sem("x_stored")
        order_loaded, high_ready, low_ready = sem("order_loaded"), sem("high_ready"), sem("low_ready")
        lg_ready, e_ready, gates_ready = sem("lg_ready"), sem("e_ready"), sem("gates_ready")
        silu = [sb(f"silu{k}", [P, S]) for k in range(2)]
        hf = [sb(f"hf{k}", [P, S]) for k in range(RING)]
        hh = [sb(f"hh{k}", [P, S], F32R) for k in range(RING)]
        hl = [sb(f"hl{k}", [P, S], F32R) for k in range(RING)]
        gates, dT = sb("gates", [P, T, N]), sb("dT", [P, S])
        acc, y = sb("acc", [P, T, D]), sb("y", [P, T, D])
        hot = y[:].rearrange("p t d -> p (t d)").rearrange("p (k t e) -> p k t e", k=2, e=NE)
        stats, mv = sb("stats", [P, T, 6]), sb("mv", [P, T, 2])
        half, rstd = sb("half", [P, T]), sb("rstd", [P, T])

        half_ready, passed = sem("half_ready"), sem("passed")
        g_ps, u_ps, silu_ready, h_ready = sem("g_ps"), sem("u_ps"), sem("silu_ready"), sem("h_ready")
        hh_ready, hl_ready, d_used = sem("hh_ready"), sem("hl_ready"), sem("d_used")
        dT_ready, dt_ps, added = sem("dT_ready"), sem("dt_ps"), sem("added")
        var_ready, rstd_ready, dve_steps = sem("var_ready"), sem("rstd_ready"), sem("dve_steps")
        NC = N * FC
        assert NC % RING == 0 and NC % 2 == 0 and N % ER == 0

        def batches(eng, body):
            body(0)
            with eng.Fori(1, B) as b:
                body(b)

        ctx.callback(clear, nc, sems)
        block = ctx.enter_context(nc.Block())

        @block.sync
        def _(sp):
            sp.dma_start(order[:], consts["order"]).then_inc(order_loaded, 16)
            for e in range(FIRST, N):
                if e >= FIRST + 2:
                    sp.wait_ge(high_ready, e - FIRST - 1)
                    sp.wait_ge(low_ready, e - FIRST - 1)
                sp.dma_start(stage[e % 2][:, 0, :], w["w1"][e]).then_inc(staged[e % 2], 16)
                sp.dma_start(stage[e % 2][:, 1, :], w["w3"][e]).then_inc(staged[e % 2], 16)
                sp.dma_start(stage[e % 2][:, 2, :], w["w2"][e].rearrange("p c d -> p (c d)")).then_inc(staged[e % 2], 16)
            with sp.Fori(0, B) as b:
                sp.wait_ge(x_ready, b + 1)
                sp.sem_inc(passed, 1)
                sp.dma_start(out[b].rearrange("(t p) d -> p t d", p=P), X[:, bass.ds(b * T, T), :]).then_inc(x_stored, 16)
            sp.wait_ge(x_stored, B * 16)

        @block.gpsimd
        def _(pool):
            nc.gpsimd.memset(half[:], -0.5).then_inc(half_ready, 1)
            nc.gpsimd.memset(GATES[:, :, NE:N], 1.0 / NE).then_inc(half_ready, 1)
            pool.wait_ge(half_ready, 2)

            def rsqrt(b):
                pool.wait_ge(var_ready, b + 1)
                nc.gpsimd.tensor_tensor(rstd[:], mv[:, :, 1], half[:], ALU.pow).then_inc(rstd_ready, 1)

            def body(b):
                for n in range(NC):
                    pool.wait_ge(hh_ready, b * NC + n + 1)
                    nc.gpsimd.tensor_tensor(hl[n % RING][:], hf[n % RING][:], hh[n % RING][:].bitcast(F32),
                                            ALU.subtract).then_inc(hl_ready, 1)
                    if n == FINISH and not isinstance(b, int):
                        rsqrt(b - 1)
            batches(pool, body)
            rsqrt(B - 1)

        @block.scalar
        def _(act):
            def high_half(m, k):
                act.wait_ge(h_ready, m + 1)
                if positive(m - RING + 1):
                    act.wait_ge(d_used, m - RING + 1)
                nc.scalar.activation(hh[k][:], hf[k][:], ACT.Copy).then_inc(hh_ready, 1)

            def cut_high(e):
                act.wait_ge(staged[e % 2], 48 * ((e - FIRST) // 2 + 1))
                nc.scalar.activation(high[:, e], stage[e % 2][:], ACT.Copy).then_inc(high_ready, 1)

            def fetch(e, k):
                act.wait_ge(d_used, e * FC + FC)
                if positive(e):
                    act.wait_ge(dt_ps, e)
                nc.scalar.activation(dT[:], d_bank[k][:], ACT.Copy).then_inc(dT_ready, 1)

            def body(b):
                for n in range(NC):
                    m, e = b * NC + n, b * N + n // FC
                    act.wait_ge(g_ps, m + 1)
                    if positive(m - 1):
                        act.wait_ge(h_ready, m - 1)
                    nc.scalar.activation(silu[n % 2][:], g_bank[n % 2][:], ACT.Silu).then_inc(silu_ready, 1)
                    if positive(m):
                        high_half(m - 1, (n - 1) % RING)
                    if n % FC == 3 and positive(e):
                        fetch(e - 1, (n // FC - 1) % ER)
                    if isinstance(b, int):
                        if n % FC == 2 and n // FC + FIRST < N:
                            cut_high(n // FC + FIRST)
                        if n == 0:
                            act.wait_ge(lg_ready, 1)
                            nc.scalar.activation(logits[:], logits[:], ACT.Exp).then_inc(e_ready, 1)
            batches(act, body)
            high_half(B * NC - 1, (NC - 1) % RING)
            fetch(B * N - 1, (N - 1) % ER)

        @block.vector
        def _(dve):
            first = 1 + (N - 2) * (T - 1) + GATING_STEPS
            per = 1 + N * (T - 1) + 3 * T + 1
            ch = Chain(dve, dve_steps, per, passed)
            dve.wait_ge(half_ready, 2)

            def cut_low(e):
                dve.wait_ge(high_ready, e - FIRST + 1)
                nc.vector.tensor_tensor(low[:, e], stage[e % 2][:], high[:, e].bitcast(F32), ALU.subtract).then_inc(low_ready, 1)

            def gate(step):
                if step == 1:
                    dve.wait_ge(e_ready, 1)
                    normalise_gates(nc, ch, logits, red)
                if step == 2:
                    dve.wait_ge(order_loaded, 16)
                    choose(nc, ch, 0, logits, order, tmp, red, hot)
                if step == 4:
                    choose(nc, ch, 1, logits, order, tmp, red, hot)
                if step == 5:
                    keep_chosen(nc, ch, logits, hot, GATES).then_inc(gates_ready, 1)

            def gated(m, n):
                dve.wait_ge(silu_ready, m + 1)
                dve.wait_ge(u_ps, m + 1)
                if positive(m - RING + 1):
                    dve.wait_ge(hl_ready, m - RING + 1)
                nc.vector.tensor_tensor(hf[n % RING][:], silu[n % 2][:], u_bank[n % 2][:], ALU.mult).then_inc(h_ready, 1)

            def add(b, e):
                dve.wait_ge(dt_ps, b * N + e + 1)
                if positive(b * N + e):
                    dve.wait_ge(added, b * N + e)
                if e == 0:
                    dve.wait_ge(gates_ready, 1)
                    ch.do(nc.vector.tensor_copy(gates[:], GATES[:, bass.ds(b * T, T), :]))
                ch.sync()
                for t in range(T):
                    src = turned[:, t * P:(t + 1) * P]
                    if e == 0:
                        last = nc.vector.tensor_scalar(acc[:, t, :], src, gates[:, t, 0:1], None, ALU.mult)
                    else:
                        last = nc.vector.scalar_tensor_tensor(acc[:, t, :], src, gates[:, t, e:e + 1], acc[:, t, :],
                                                              ALU.mult, ALU.add)
                    if t < T - 1:
                        ch.do(last)
                last.then_inc(added, 1)

            def moments(b):
                dve.wait_ge(added, b * N + N)
                ch.do(nc.vector.tensor_scalar_mul(acc[:], acc[:], 0.5))
                ch.sync()
                ln_stats(nc, ch, acc, stats, mv).then_inc(var_ready, 1)

            def normalised(b):
                dve.wait_ge(rstd_ready, b + 1)
                ln_apply(nc, ch, y, acc, mv, rstd)

            def residual(b):
                x = X[:, bass.ds(b * T, T), :]
                ch.sync()
                nc.vector.tensor_tensor(x, x, y[:], ALU.add).then_inc(x_ready, 1)

            def body(b):
                inner = not isinstance(b, int)
                for n in range(NC):
                    gated(b * NC + n, n)
                    if not inner:
                        gate(n)
                        if n % FC == 3 and n // FC + FIRST < N:
                            cut_low(n // FC + FIRST)
                    e = n // FC - 2
                    if n % FC == 2 and (inner or e >= 0):
                        add(b if e >= 0 else b - 1, e % N)
                    if inner and n == FINISH:
                        moments(b - 1)
                    if inner and n == FINISH + 2:
                        normalised(b - 1)
                    if inner and n == FINISH + 4:
                        residual(b - 1)
            ch.start(0)
            shift_logits(nc, ch, logits, red).then_inc(lg_ready, 1)
            body(0)
            assert ch.n == first
            with dve.Fori(1, B) as b:
                ch.start(b, first - per)
                body(b)
                ch.end()
            ch.start(0, first + (B - 1) * per)
            add(B - 1, N - 2)
            add(B - 1, N - 1)
            moments(B - 1)
            normalised(B - 1)
            residual(B - 1)

        @block.tensor
        def _(pe):
            both = lambda e, k, c: [h[:, e, k, c * P:(c + 1) * P] for h in (high, low)]

            def up(b, n):
                m = b * NC + n
                if isinstance(b, int) and n >= FIRST * FC:
                    pe.wait_ge(low_ready, n // FC - FIRST + 1)
                if positive(m - 1):
                    pe.wait_ge(silu_ready, m - 1)
                    pe.wait_ge(h_ready, m - 1)
                tokens = [half[:, bass.ds(b * S, S)] for half in (YH, YL)]
                mm3(nc, g_bank[n % 2][:], both(n // FC, 0, n % FC), tokens).then_inc(g_ps, 1)
                mm3(nc, u_bank[n % 2][:], both(n // FC, 1, n % FC), tokens).then_inc(u_ps, 1)

            def down(b, n):
                e, c = n % NC // FC, n % FC
                pe.wait_ge(hl_ready, b * NC + n + 1)
                if c == 0 and positive(b * N + n // FC - ER + 1):
                    pe.wait_ge(dT_ready, b * N + n // FC - ER + 1)
                mm3(nc, d_bank[e % ER][:], both(e, 2, c), (hh[n % RING][:], hl[n % RING][:]), start=c == 0,
                    stop=c == FC - 1).then_inc(d_used, 1)

            def turn(e):
                pe.wait_ge(dT_ready, e + 1)
                if positive(e):
                    pe.wait_ge(added, e)
                for t in range(T):
                    last = nc.tensor.transpose(turned[:, t * P:(t + 1) * P], dT[:, t * P:(t + 1) * P], ident[:])
                last.then_inc(dt_ps, 1)

            def body(b):
                inner = not isinstance(b, int)
                for n in range(NC):
                    up(b, n)
                    if inner or n >= LAG:
                        down(b, n - LAG)
                    if n % FC == 0 and (inner or n >= 2 * FC):
                        turn(b * N + n // FC - 2)
            batches(pe, body)
            for n in range(NC, NC + LAG):
                down(B - 1, n - LAG)
            turn(B * N - 2)
            turn(B * N - 1)


def build(nc, dram, out):
    ctx = ExitStack()
    with ctx:
        X = ctx.enter_context(nc.sbuf_tensor("X", [P, B * T, D], F32))
        ident = ctx.enter_context(nc.sbuf_tensor("ident", [P, P], F32))
        x_loaded = ctx.enter_context(nc.semaphore("x_loaded"))
        first = slice(0, LANES * T)
        x_dram = dram["video"].rearrange("b (t p) d -> p (b t) d", p=P)
        with nc.Block() as block:
            @block.sync
            def _(sp):
                sp.dma_start(ident[:], dram["ident"]).then_inc(x_loaded, 16)
                sp.dma_start(X[:, first, :], x_dram[:, first, :]).then_inc(x_loaded, 16)
                sp.wait_ge(x_loaded, 32)

        w = lambda prefix: {k[len(prefix):]: v for k, v in dram.items() if k.startswith(prefix)}
        performer_layer(nc, X, ident, w("L0_attn_"), dram)
        with nc.sbuf_tensor("Y", [P, B * T, D], F32) as Y:
            attention_layer(nc, X, Y, ident, w("L0_ffn_"), dram, True)
            mixture_layer(nc, X, Y, ident, w("L0_ffn_"), dram)
        attention_layer(nc, X, None, ident, w("L1_attn_"), dram, False)
        swiglu_layer(nc, X, ident, w("L1_ffn_"), dram, out)


def layouts(i):
    import numpy as np
    i = {k: np.asarray(v) for k, v in i.items()}
    con = np.ascontiguousarray
    rows = lambda a: con(np.broadcast_to(a.reshape(1, -1), (P, a.size)))
    col = lambda a: con(a.reshape(-1, P).T)
    chunks = lambda a: con(a.reshape(-1, P, a.shape[-1]).transpose(1, 0, 2))
    d = {"video": i["L0_attn_video"]}
    p = "L0_attn_"
    for n in ("Wq", "Wk", "Wv", "Wo", "W1"):
        d[p + n + "T"] = con(i[p + n].T)
    d[p + "W2T"] = chunks(i[p + "W2"].T)
    d[p + "projT"] = con(i[p + "proj"].T)
    for n in ("bq", "bk", "b1"):
        d[p + n] = col(i[p + n])
    for n in ("bv", "bo", "b2", "g2", "be2", "g3", "be3"):
        d[p + n] = rows(i[p + n])
    p = "L0_ffn_"
    for n, k in (("q", 0), ("k", 1), ("v", 2)):
        d[p + "W" + n + "T"] = con(i[p + "in_proj_w"][k * D:(k + 1) * D].T)
        d[p + "b" + n] = (rows if n == "v" else col)(i[p + "in_proj_b"][k * D:(k + 1) * D])
    d[p + "WoT"] = con(i[p + "out_proj_w"].T)
    d[p + "gateT"] = con(i[p + "gate_w"].T)
    d[p + "expertT"] = con(i[p + "expert_w"].transpose(2, 0, 1)).reshape(D, NE * D)
    d[p + "expert_b"] = i[p + "expert_b"]
    for n in ("out_proj_b", "gate_b", "ln1_w", "ln1_b", "ln2_w", "ln2_b"):
        d[p + n] = rows(i[p + n])
    p = "L1_attn_"
    for n in ("Wq", "Wk", "Wv", "Wo", "We"):
        d[p + n + "T"] = con(i[p + n].T)
    p = "L1_ffn_"
    d[p + "gateT"] = con(i[p + "gate_W"].T)
    for n in ("w1", "w3"):
        d[p + n] = con(np.concatenate([i[p + n + "_e"], i[p + n + "_s"].transpose(1, 0, 2).reshape(1, D, F)]))
    d[p + "w2"] = con(np.concatenate([i[p + "w2_e"], i[p + "w2_s"].reshape(1, F, D)])
                      .reshape(NE + 1, FC, P, D).transpose(0, 2, 1, 3))
    f = np.float32
    r = np.arange(P)
    d["ident"] = np.eye(P, dtype=f)
    d["hsel"] = (r[:, None] // DH == np.arange(32)[None]).astype(f)
    d["bmask"] = ((r[:, None] % 32) // DH == r[None] // M).astype(f)
    d["causal"] = np.where(r[None] > r[:, None], f(-1e30), f(0))
    d["order"] = np.broadcast_to(np.arange(NE, 0, -1, dtype=f), (P, NE)).copy()
    inv = 1.0 / 10000.0 ** (np.arange(0, DH, 2, dtype=f) / f(DH))
    ang = np.arange(S, dtype=f)[:, None] * inv[None].astype(f)
    cos, sin = np.cos(ang).astype(f), np.sin(ang).astype(f)
    full = lambda a: con(np.tile(a, (1, H)).reshape(T, P, D).transpose(1, 0, 2)).astype(f)
    d["rope_cos"] = full(np.repeat(cos, 2, axis=1))
    d["rope_sin"] = full(np.stack([-sin, sin], axis=-1).reshape(S, DH))
    return d


def kernel(**inputs):
    import numpy as np
    import concourse.bacc as bacc
    from concourse.bass_utils import run_bass_kernel_spmd

    nc = bacc.Bacc("TRN2", target_bir_lowering=False, num_devices=1)
    arrays = layouts(inputs)
    dram = {k: nc.dram_tensor("in_" + k, a.shape, mybir.dt.from_np(a.dtype), kind="ExternalInput").ap()
            for k, a in arrays.items()}
    out = nc.dram_tensor("out", (B, S, D), F32, kind="ExternalOutput").ap()
    build(nc, dram, out)
    r = run_bass_kernel_spmd(nc, [{"in_" + k: a for k, a in arrays.items()}], core_ids=[0])
    return r.results[0]["out"]
```
